# Optimizing a Trainium2 kernel written in Bass

```python
import numpy as np
import jax
import jax.numpy as jnp

def _softmax(x, axis=-1):
    return jax.nn.softmax(x, axis=axis)

def _gelu(x):
    return jax.nn.gelu(x, approximate=True)

def _silu(x):
    return jax.nn.silu(x)

def _sigmoid(x):
    return jax.nn.sigmoid(x)

def _layernorm(x, axis=-1, eps=1e-05):
    m = jnp.mean(x, axis=axis, keepdims=True)
    v = jnp.var(x, axis=axis, keepdims=True)
    return (x - m) / jnp.sqrt(v + eps)

def _scatter_add(tgt, idx, src, axis=0):
    return tgt.at[idx].add(src)

def _segment_sum(src, seg, n):
    return jax.ops.segment_sum(src, seg, n)
kernel_name = 'mk_xattn_seq_d2_seqx_r8_e5b3ff'

def setup_inputs(seed: int=0):
    np.random.seed(seed)
    _w = jnp.asarray

    def _rec_inputs():
        import jax
        import jax.numpy as jnp
        _rk = jax.random.key(seed)
        x = -0.0005207 + 1.001 * jax.random.normal(jax.random.fold_in(_rk, 1), (8, 56, 256), jnp.float32)
        _lenS = 56 - jax.random.randint(jax.random.fold_in(_rk, 7), (8,), 0, max(1, 56 // 4) + 1, jnp.int32)
        _lenS2 = 1500 - jax.random.randint(jax.random.fold_in(_rk, 8), (8,), 0, max(1, 1500 // 4) + 1, jnp.int32)
        _ctx_2048P = jax.random.normal(jax.random.fold_in(_rk, 11), (8, 16, 256), jnp.float32)
        _ctx_2048c = jax.random.dirichlet(jax.random.fold_in(_rk, 511), 0.3 * jnp.ones((16,), jnp.float32), (8, 1500))
        _ctx_2048t = jnp.einsum('bsk,bkd->bsd', _ctx_2048c, _ctx_2048P)
        _ctx_2048t = _ctx_2048t * jax.lax.rsqrt(jnp.mean(jnp.square(_ctx_2048t)) + 1e-12) * 0.953939
        ctx_2048 = 2.81802e-05 + 1.00001 * (_ctx_2048t + 0.3 * jax.random.normal(jax.random.fold_in(_rk, 611), (8, 1500, 256), jnp.float32))
        _validS = jnp.arange(56)[None, :] < _lenS[:, None]
        _validS2 = jnp.arange(1500)[None, :] < _lenS2[:, None]
        _causal = jnp.tril(jnp.ones((56, 56), dtype=bool))
        mask_BxS2_bf1 = jnp.ones((8, 1500), dtype=bool)
        return (x, ctx_2048, mask_BxS2_bf1)
    x, ctx_2048, mask_BxS2_bf1 = _rec_inputs()

    def _L0_xattn_setup():
        import jax, jax.numpy as jnp
        import numpy as np
        B, Q, S1, S2 = (4, 32, 256, 256)
        D, H, K, F = (256, 16, 128, 1024)
        LN_EPS = 1e-05

        def _layer_norm(x, scale, offset):
            mu = jnp.mean(x, axis=-1, keepdims=True)
            var = jnp.var(x, axis=-1, keepdims=True)
            return (x - mu) * jax.lax.rsqrt(var + LN_EPS) * scale + offset

        def _cross_attention(q_in, kv_in, wq, bq, wk, bk, wv, bv, wo, bo, bias_k, bias_v):
            b, q_len, _ = q_in.shape
            t = kv_in.shape[1]
            qh = (q_in @ wq + bq).reshape(b, q_len, H, K)
            kh = (kv_in @ wk + bk).reshape(b, t, H, K)
            vh = (kv_in @ wv + bv).reshape(b, t, H, K)
            kh = jnp.concatenate([kh, jnp.broadcast_to(bias_k, (b, 1, H, K))], axis=1)
            vh = jnp.concatenate([vh, jnp.broadcast_to(bias_v, (b, 1, H, K))], axis=1)
            scale = jnp.sqrt(jnp.asarray(K, q_in.dtype))
            logits = jnp.einsum('bqhk,bthk->bhqt', qh, kh) / scale
            weights = jax.nn.softmax(logits, axis=-1)
            ctx = jnp.einsum('bhqt,bthk->bqhk', weights, vh).reshape(b, q_len, H * K)
            return ctx @ wo + bo

        def _forward(x, xf_1, xf_2, ln1_scale, ln1_offset, wq1, bq1, wk1, bk1, wv1, bv1, wo1, bo1, bias_k1, bias_v1, ln2_scale, ln2_offset, wq2, bq2, wk2, bk2, wv2, bv2, wo2, bo2, bias_k2, bias_v2, ln_mlp_scale, ln_mlp_offset, w_fc1, b_fc1, w_fc2, b_fc2):
            res = x
            h = _layer_norm(x, ln1_scale, ln1_offset)
            x = res + _cross_attention(h, xf_1, wq1, bq1, wk1, bk1, wv1, bv1, wo1, bo1, bias_k1, bias_v1)
            res = x
            h = _layer_norm(x, ln2_scale, ln2_offset)
            x = res + _cross_attention(h, xf_2, wq2, bq2, wk2, bk2, wv2, bv2, wo2, bo2, bias_k2, bias_v2)
            h = _layer_norm(x, ln_mlp_scale, ln_mlp_offset)
            h = jax.nn.gelu(h @ w_fc1 + b_fc1, approximate=False) @ w_fc2 + b_fc2
            return x + h
        key = jax.random.key(seed)
        ks = iter(jax.random.split(key, 64))

        def rn(shape, s=0.02):
            return jax.random.normal(next(ks), shape, jnp.float32) * s
        inp = {'x': rn((B, Q, D), 1.0), 'xf_1': rn((B, S1, D), 1.0), 'xf_2': rn((B, S2, D), 1.0)}
        for i in (1, 2):
            inp[f'ln{i}_scale'] = jnp.ones((D,), jnp.float32)
            inp[f'ln{i}_offset'] = jnp.zeros((D,), jnp.float32)
            inp[f'wq{i}'] = rn((D, H * K))
            inp[f'bq{i}'] = jnp.zeros((H * K,), jnp.float32)
            inp[f'wk{i}'] = rn((D, H * K))
            inp[f'bk{i}'] = jnp.zeros((H * K,), jnp.float32)
            inp[f'wv{i}'] = rn((D, H * K))
            inp[f'bv{i}'] = jnp.zeros((H * K,), jnp.float32)
            inp[f'wo{i}'] = rn((H * K, D))
            inp[f'bo{i}'] = jnp.zeros((D,), jnp.float32)
            inp[f'bias_k{i}'] = rn((1, 1, H, K))
            inp[f'bias_v{i}'] = rn((1, 1, H, K))
        inp['ln_mlp_scale'] = jnp.ones((D,), jnp.float32)
        inp['ln_mlp_offset'] = jnp.zeros((D,), jnp.float32)
        inp['w_fc1'] = rn((D, F))
        inp['b_fc1'] = jnp.zeros((F,), jnp.float32)
        inp['w_fc2'] = rn((F, D))
        inp['b_fc2'] = jnp.zeros((D,), jnp.float32)
        return inp
    _L0_xattn_all = _L0_xattn_setup()
    _L0_xattn_in = {k: v for k, v in _L0_xattn_all.items() if k in ('ln1_scale', 'ln1_offset', 'wq1', 'bq1', 'wk1', 'bk1', 'wv1', 'bv1', 'wo1', 'bo1', 'bias_k1', 'bias_v1', 'ln2_scale', 'ln2_offset', 'wq2', 'bq2', 'wk2', 'bk2', 'wv2', 'bv2', 'wo2', 'bo2', 'bias_k2', 'bias_v2', 'ln_mlp_scale', 'ln_mlp_offset', 'w_fc1', 'b_fc1', 'w_fc2', 'b_fc2')}
    del _L0_xattn_all

    def _L1_xattn_setup():
        import jax, jax.numpy as jnp
        import numpy as np
        HIDDEN = 256
        HEADS = 16
        HEAD_DIM = HIDDEN // HEADS
        LN_EPS = 1e-05
        GATE_INIT = 0.5

        def _layer_norm(x, gamma, beta):
            mu = jnp.mean(x, axis=-1, keepdims=True)
            var = jnp.mean(jnp.square(x - mu), axis=-1, keepdims=True)
            return (x - mu) * jax.lax.rsqrt(var + LN_EPS) * gamma + beta
        key = jax.random.key(seed)
        ks = jax.random.split(key, 8)
        B, T_TEXT, T_AUDIO = (4, 256, 1500)
        s = 0.02
        return {'hidden_states': jax.random.normal(ks[0], (B, T_TEXT, HIDDEN), jnp.float32), 'audio_kv': jax.random.normal(ks[1], (B, T_AUDIO, HIDDEN), jnp.float32), 'audio_attention_mask': jnp.ones((B, T_AUDIO), dtype=bool), 'Wq': jax.random.normal(ks[2], (HIDDEN, HIDDEN), jnp.float32) * s, 'Wk': jax.random.normal(ks[3], (HIDDEN, HIDDEN), jnp.float32) * s, 'Wv': jax.random.normal(ks[4], (HIDDEN, HIDDEN), jnp.float32) * s, 'Wo': jax.random.normal(ks[5], (HIDDEN, HIDDEN), jnp.float32) * s, 'ln_gamma': jnp.ones((HIDDEN,), jnp.float32), 'ln_beta': jnp.zeros((HIDDEN,), jnp.float32), 'gate': jnp.array([GATE_INIT], jnp.float32)}
    _L1_xattn_all = _L1_xattn_setup()
    _L1_xattn_in = {k: v for k, v in _L1_xattn_all.items() if k in ('Wq', 'Wk', 'Wv', 'Wo', 'ln_gamma', 'ln_beta', 'gate')}
    del _L1_xattn_all
    return {'x': x, 'ctx_2048': ctx_2048, 'mask_BxS2_bf1': mask_BxS2_bf1, 'L0_xattn_ln1_scale': _L0_xattn_in['ln1_scale'], 'L0_xattn_ln1_offset': _L0_xattn_in['ln1_offset'], 'L0_xattn_wq1': _L0_xattn_in['wq1'], 'L0_xattn_bq1': _L0_xattn_in['bq1'], 'L0_xattn_wk1': _L0_xattn_in['wk1'], 'L0_xattn_bk1': _L0_xattn_in['bk1'], 'L0_xattn_wv1': _L0_xattn_in['wv1'], 'L0_xattn_bv1': _L0_xattn_in['bv1'], 'L0_xattn_wo1': _L0_xattn_in['wo1'], 'L0_xattn_bo1': _L0_xattn_in['bo1'], 'L0_xattn_bias_k1': _L0_xattn_in['bias_k1'], 'L0_xattn_bias_v1': _L0_xattn_in['bias_v1'], 'L0_xattn_ln2_scale': _L0_xattn_in['ln2_scale'], 'L0_xattn_ln2_offset': _L0_xattn_in['ln2_offset'], 'L0_xattn_wq2': _L0_xattn_in['wq2'], 'L0_xattn_bq2': _L0_xattn_in['bq2'], 'L0_xattn_wk2': _L0_xattn_in['wk2'], 'L0_xattn_bk2': _L0_xattn_in['bk2'], 'L0_xattn_wv2': _L0_xattn_in['wv2'], 'L0_xattn_bv2': _L0_xattn_in['bv2'], 'L0_xattn_wo2': _L0_xattn_in['wo2'], 'L0_xattn_bo2': _L0_xattn_in['bo2'], 'L0_xattn_bias_k2': _L0_xattn_in['bias_k2'], 'L0_xattn_bias_v2': _L0_xattn_in['bias_v2'], 'L0_xattn_ln_mlp_scale': _L0_xattn_in['ln_mlp_scale'], 'L0_xattn_ln_mlp_offset': _L0_xattn_in['ln_mlp_offset'], 'L0_xattn_w_fc1': _L0_xattn_in['w_fc1'], 'L0_xattn_b_fc1': _L0_xattn_in['b_fc1'], 'L0_xattn_w_fc2': _L0_xattn_in['w_fc2'], 'L0_xattn_b_fc2': _L0_xattn_in['b_fc2'], 'L1_xattn_Wq': _L1_xattn_in['Wq'], 'L1_xattn_Wk': _L1_xattn_in['Wk'], 'L1_xattn_Wv': _L1_xattn_in['Wv'], 'L1_xattn_Wo': _L1_xattn_in['Wo'], 'L1_xattn_ln_gamma': _L1_xattn_in['ln_gamma'], 'L1_xattn_ln_beta': _L1_xattn_in['ln_beta'], 'L1_xattn_gate': _L1_xattn_in['gate']}

def reference(x, ctx_2048, mask_BxS2_bf1, L0_xattn_ln1_scale, L0_xattn_ln1_offset, L0_xattn_wq1, L0_xattn_bq1, L0_xattn_wk1, L0_xattn_bk1, L0_xattn_wv1, L0_xattn_bv1, L0_xattn_wo1, L0_xattn_bo1, L0_xattn_bias_k1, L0_xattn_bias_v1, L0_xattn_ln2_scale, L0_xattn_ln2_offset, L0_xattn_wq2, L0_xattn_bq2, L0_xattn_wk2, L0_xattn_bk2, L0_xattn_wv2, L0_xattn_bv2, L0_xattn_wo2, L0_xattn_bo2, L0_xattn_bias_k2, L0_xattn_bias_v2, L0_xattn_ln_mlp_scale, L0_xattn_ln_mlp_offset, L0_xattn_w_fc1, L0_xattn_b_fc1, L0_xattn_w_fc2, L0_xattn_b_fc2, L1_xattn_Wq, L1_xattn_Wk, L1_xattn_Wv, L1_xattn_Wo, L1_xattn_ln_gamma, L1_xattn_ln_beta, L1_xattn_gate):
    import jax
    import jax.numpy as jnp

    def _L0_xattn_ref(x, xf_1, xf_2, ln1_scale, ln1_offset, wq1, bq1, wk1, bk1, wv1, bv1, wo1, bo1, bias_k1, bias_v1, ln2_scale, ln2_offset, wq2, bq2, wk2, bk2, wv2, bv2, wo2, bo2, bias_k2, bias_v2, ln_mlp_scale, ln_mlp_offset, w_fc1, b_fc1, w_fc2, b_fc2):
        import jax, jax.numpy as jnp
        import numpy as np
        B, Q, S1, S2 = (4, 32, 256, 256)
        D, H, K, F = (256, 16, 128, 1024)
        LN_EPS = 1e-05

        def _layer_norm(x, scale, offset):
            mu = jnp.mean(x, axis=-1, keepdims=True)
            var = jnp.var(x, axis=-1, keepdims=True)
            return (x - mu) * jax.lax.rsqrt(var + LN_EPS) * scale + offset

        def _cross_attention(q_in, kv_in, wq, bq, wk, bk, wv, bv, wo, bo, bias_k, bias_v):
            b, q_len, _ = q_in.shape
            t = kv_in.shape[1]
            qh = (q_in @ wq + bq).reshape(b, q_len, H, K)
            kh = (kv_in @ wk + bk).reshape(b, t, H, K)
            vh = (kv_in @ wv + bv).reshape(b, t, H, K)
            kh = jnp.concatenate([kh, jnp.broadcast_to(bias_k, (b, 1, H, K))], axis=1)
            vh = jnp.concatenate([vh, jnp.broadcast_to(bias_v, (b, 1, H, K))], axis=1)
            scale = jnp.sqrt(jnp.asarray(K, q_in.dtype))
            logits = jnp.einsum('bqhk,bthk->bhqt', qh, kh) / scale
            weights = jax.nn.softmax(logits, axis=-1)
            ctx = jnp.einsum('bhqt,bthk->bqhk', weights, vh).reshape(b, q_len, H * K)
            return ctx @ wo + bo

        def _forward(x, xf_1, xf_2, ln1_scale, ln1_offset, wq1, bq1, wk1, bk1, wv1, bv1, wo1, bo1, bias_k1, bias_v1, ln2_scale, ln2_offset, wq2, bq2, wk2, bk2, wv2, bv2, wo2, bo2, bias_k2, bias_v2, ln_mlp_scale, ln_mlp_offset, w_fc1, b_fc1, w_fc2, b_fc2):
            res = x
            h = _layer_norm(x, ln1_scale, ln1_offset)
            x = res + _cross_attention(h, xf_1, wq1, bq1, wk1, bk1, wv1, bv1, wo1, bo1, bias_k1, bias_v1)
            res = x
            h = _layer_norm(x, ln2_scale, ln2_offset)
            x = res + _cross_attention(h, xf_2, wq2, bq2, wk2, bk2, wv2, bv2, wo2, bo2, bias_k2, bias_v2)
            h = _layer_norm(x, ln_mlp_scale, ln_mlp_offset)
            h = jax.nn.gelu(h @ w_fc1 + b_fc1, approximate=False) @ w_fc2 + b_fc2
            return x + h
        return _forward(x, xf_1, xf_2, ln1_scale, ln1_offset, wq1, bq1, wk1, bk1, wv1, bv1, wo1, bo1, bias_k1, bias_v1, ln2_scale, ln2_offset, wq2, bq2, wk2, bk2, wv2, bv2, wo2, bo2, bias_k2, bias_v2, ln_mlp_scale, ln_mlp_offset, w_fc1, b_fc1, w_fc2, b_fc2)

    def _L1_xattn_ref(hidden_states, audio_kv, audio_attention_mask, Wq, Wk, Wv, Wo, ln_gamma, ln_beta, gate):
        import jax, jax.numpy as jnp
        import numpy as np
        HIDDEN = 256
        HEADS = 16
        HEAD_DIM = HIDDEN // HEADS
        LN_EPS = 1e-05
        GATE_INIT = 0.5

        def _layer_norm(x, gamma, beta):
            mu = jnp.mean(x, axis=-1, keepdims=True)
            var = jnp.mean(jnp.square(x - mu), axis=-1, keepdims=True)
            return (x - mu) * jax.lax.rsqrt(var + LN_EPS) * gamma + beta
        B, Tt, D = hidden_states.shape
        Ta = audio_kv.shape[1]
        scale = HEAD_DIM ** (-0.5)
        a = _layer_norm(audio_kv, ln_gamma, ln_beta)
        Q = (hidden_states @ Wq.T).reshape(B, Tt, HEADS, HEAD_DIM).transpose(0, 2, 1, 3)
        K = (a @ Wk.T).reshape(B, Ta, HEADS, HEAD_DIM).transpose(0, 2, 1, 3)
        V = (a @ Wv.T).reshape(B, Ta, HEADS, HEAD_DIM).transpose(0, 2, 1, 3)
        scores = jnp.einsum('bhtd,bhsd->bhts', Q, K) * scale
        mask = audio_attention_mask[:, None, None, :]
        scores = jnp.where(mask, scores, jnp.float32(-jnp.inf))
        attn = jax.nn.softmax(scores, axis=-1)
        out = jnp.einsum('bhts,bhsd->bhtd', attn, V)
        out = out.transpose(0, 2, 1, 3).reshape(B, Tt, D)
        out = out @ Wo.T
        return hidden_states + jnp.tanh(gate) * out
    x = _L0_xattn_ref(x, ctx_2048, ctx_2048, L0_xattn_ln1_scale, L0_xattn_ln1_offset, L0_xattn_wq1, L0_xattn_bq1, L0_xattn_wk1, L0_xattn_bk1, L0_xattn_wv1, L0_xattn_bv1, L0_xattn_wo1, L0_xattn_bo1, L0_xattn_bias_k1, L0_xattn_bias_v1, L0_xattn_ln2_scale, L0_xattn_ln2_offset, L0_xattn_wq2, L0_xattn_bq2, L0_xattn_wk2, L0_xattn_bk2, L0_xattn_wv2, L0_xattn_bv2, L0_xattn_wo2, L0_xattn_bo2, L0_xattn_bias_k2, L0_xattn_bias_v2, L0_xattn_ln_mlp_scale, L0_xattn_ln_mlp_offset, L0_xattn_w_fc1, L0_xattn_b_fc1, L0_xattn_w_fc2, L0_xattn_b_fc2)
    x = _L1_xattn_ref(x, ctx_2048, mask_BxS2_bf1, L1_xattn_Wq, L1_xattn_Wk, L1_xattn_Wv, L1_xattn_Wo, L1_xattn_ln_gamma, L1_xattn_ln_beta, L1_xattn_gate)
    return x

_drawn_inputs = setup_inputs


def setup_inputs(seed=0):
    import zlib

    import numpy as np

    out = dict(_drawn_inputs(seed))
    spreads = {'L0_xattn_ln1_scale': (1.0, 0.6),
     'L0_xattn_ln1_offset': (0.0, 0.8),
     'L0_xattn_bq1': (0.0, 0.8),
     'L0_xattn_bk1': (0.0, 2.0),
     'L0_xattn_bv1': (0.0, 0.1),
     'L0_xattn_bo1': (0.0, 0.1),
     'L0_xattn_ln2_scale': (1.0, 0.6),
     'L0_xattn_ln2_offset': (0.0, 0.8),
     'L0_xattn_bq2': (0.0, 0.8),
     'L0_xattn_bk2': (0.0, 2.0),
     'L0_xattn_bv2': (0.0, 0.1),
     'L0_xattn_bo2': (0.0, 0.1),
     'L0_xattn_ln_mlp_scale': (1.0, 0.6),
     'L0_xattn_ln_mlp_offset': (0.0, 0.694),
     'L0_xattn_b_fc1': (0.0, 0.1),
     'L0_xattn_b_fc2': (0.0, 0.1),
     'L1_xattn_ln_gamma': (1.0, 0.6),
     'L1_xattn_ln_beta': (0.0, 0.8)}
    factors = {'L0_xattn_wq1': 8.0,
     'L0_xattn_wk1': 8.0,
     'L0_xattn_bias_k1': 64.0,
     'L0_xattn_bias_v1': 64.0,
     'L0_xattn_wq2': 8.0,
     'L0_xattn_wk2': 8.0,
     'L0_xattn_bias_k2': 64.0,
     'L0_xattn_bias_v2': 64.0,
     'L1_xattn_Wq': 8.0,
     'L1_xattn_Wk': 8.0}
    for name, (base, spread) in spreads.items():
        noise = np.random.default_rng([zlib.crc32(name.encode()), seed]).standard_normal(out[name].shape)
        drawn = base * np.exp(spread * noise) if base else spread * noise
        out[name] = jnp.asarray(drawn.astype(out[name].dtype))
    for name, factor in factors.items():
        out[name] = (out[name] * factor).astype(out[name].dtype)
    return out
```

```python
from contextlib import ExitStack

import concourse.bass as bass
from concourse import mybir

ALU = mybir.AluOpType
ACT = mybir.ActivationFunctionType
F32 = mybir.dt.float32
F16 = mybir.dt.float16
BF16 = mybir.dt.bfloat16
U8 = mybir.dt.uint8
AX_X = mybir.AxisListType.X

B, Q, D, T, H, F = 8, 56, 256, 1500, 16, 1024
P = 128
DC = D // P
NQ = B * Q
R = H * Q
RT = R // P
TP = 125
NT = T // TP
NB = 3
CW = T // NB
TPB = NT // NB
HPC = 4
WCH = H // HPC
KD = (128, 128, 16)
L = 3
GROUP_A, GROUP_B = 4, 3
PIECES = 4
JP = NT // PIECES
EPS = 1e-5
PROB_SCALE = 4096.0
MASKED = 1e30
FC = F // P

PACK = {}
_at = 0
for _l in (0, 1):
    for _n in ("bq", "bk", "bv", "bias_k"):
        PACK[_n, _l] = _at
        _at += H
for _n, _w in (("ln_scale0", DC), ("ln_offset0", DC), ("ln_scale1", DC), ("ln_offset1", DC), ("ln_scale2", DC),
               ("ln_offset2", DC), ("bo0", DC), ("bo1", DC), ("b_fc2", DC), ("b_fc1", FC)):
    PACK[_n] = _at
    _at += _w
NPACK = _at


def build(nc, x_t, ctx_nat, ctx_t, mask, pack, vrows, a_scale, a_offset, gate, wq, wk, wv, wo, w1, w2, out):
    es = ExitStack()
    with es:
        def sb(name, shape, dt=F32):
            return es.enter_context(nc.sbuf_tensor(name, shape, dt))

        def sem(name):
            return es.enter_context(nc.semaphore(name))

        qc = sb("qc", [P, B, DC * R])
        qs16 = qc[:, :, :].bitcast(F16).rearrange("p b (s c r) -> p b s c r", s=2, c=DC)
        avg = qc[:, :, :].rearrange("p b (c r) -> p b c r", c=DC)
        ctxT = sb("ctxT", [P, 2, 2, DC, T], F16)
        nat = sb("nat", [TP, 2, 2, NT, D], F16)
        stage = sb("stage", [P, PIECES, JP * D])
        stageN = stage[0:TP, :, :].rearrange("p k (j d) -> p k j d", j=JP)
        stageT = stage[:, :, 0:T * DC // PIECES]
        probT_bytes = NT * R * 2 * 2
        arena = sb("arena", [P, probT_bytes // 4])
        probT = arena[0:TP + 1, :].bitcast(F16).rearrange("p (s j r) -> p s j r", s=2, j=NT)
        prob = sb("prob", [P, 2, T + 4])
        WSL = DC * HPC * P
        at = 4 * WSL
        wring = arena[:, 0:at].rearrange("p (k n) -> p k n", k=4)
        hring = arena[:, at:at + 4 * NQ].rearrange("p (k n) -> p k n", k=4)
        hid = arena[:, at:at + FC * NQ].rearrange("p (f n) -> p f n", f=FC)
        bvm = arena[0:H, at + 4 * NQ:at + 4 * NQ + H * P].rearrange("p (h k) -> p h k", h=H)
        at2 = probT_bytes // 4 - DC * NQ
        hT = arena[:, at2:].rearrange("p (c n) -> p c n", c=DC)
        xc = prob[:, 0, 0:DC * NQ].rearrange("p (c n) -> p c n", c=DC)
        sq = prob[:, 1, 0:DC * NQ].rearrange("p (c n) -> p c n", c=DC)
        std = sb("std", [P, NQ])
        xT = sb("xT", [P, DC, NQ])
        pk = sb("pk", [P, NPACK])
        bkd = sb("bkd", [P, 2, H])
        bkm = sb("bkm", [P, 2, H, H])
        vr = sb("vr", [H, 2, 2, P])
        bvd = sb("bvd", [H, 2, P])
        tok16 = sb("tok16", [H, NQ])
        rowbuf = sb("rowbuf", [P, 2 * R])
        tokrow = rowbuf[0:1, :].rearrange("p (i r) -> p i r", i=2)
        maskb = rowbuf[:, 0:T].bitcast(BF16).rearrange("p (i t) -> p i t", i=2)
        ptok = sb("ptok", [1, R])
        ptok16 = sb("ptok16", [H, NQ])
        ident = sb("ident", [P, P])
        dmean = sb("dmean", [P, P])
        selT = sb("selT", [P, 1], F16)
        one = sb("one", [1, 1])
        epsc = sb("epsc", [P, 1])
        mx3 = sb("mx3", [P, 2, 4])
        nmax = sb("nmax", [P, 2, 1])
        sum3 = sb("sum3", [P, 2, 4])
        rsum = sb("rsum", [P, 2, 2])
        stats = sb("stats", [TP, B, NT, 6])
        mu = sb("mu", [TP, B * NT])
        rstd = sb("rstd", [TP, B * NT])
        stt = sb("stt", [TP, 2, B * NT])
        mrb = sb("mrb", [TP, 2, NT])
        a_sc = sb("a_sc", [TP, D])
        a_of = sb("a_of", [TP, D])
        mask8 = sb("mask8", [P, T], U8)
        anym = sb("anym", [P, 4])
        tg = sb("tg", [P, 2])

        S = [es.enter_context(nc.psum_tensor(f"S{i}", [P, 512], F32)) for i in range(NB)]
        TB = [es.enter_context(nc.psum_tensor(f"TB{i}", [P, 512], F32)) for i in range(2)]
        PV = [es.enter_context(nc.psum_tensor(f"PV{i}", [P, 512], F32)) for i in range(2)]
        M = es.enter_context(nc.psum_tensor("M", [P, 512], F32))
        QB = [S[0], S[1], PV[0], PV[1]]

        in_x = sem("in_x")
        in_aud = sem("in_aud")
        in_pack = sem("in_pack")
        passed = sem("passed")
        w_full = [sem(f"w_full{k}") for k in range(4)]
        stage_full = [sem(f"stage_full{k}") for k in range(4)]
        stage_free = sem("stage_free")
        mask_full = sem("mask_full")
        mask_ready = sem("mask_ready")
        const_ready = sem("const_ready")
        bkd_ready = sem("bkd_ready")
        bvd_ready = sem("bvd_ready")
        bvm_ready = sem("bvm_ready")
        mean_ready = sem("mean_ready")
        xc_ready = sem("xc_ready")
        sq_ready = sem("sq_ready")
        var_ready = sem("var_ready")
        std_ready = sem("std_ready")
        rs_ready = sem("rs_ready")
        xn_ready = sem("xn_ready")
        h_ready = sem("h_ready")
        x_ready = sem("x_ready")
        q_mm = sem("q_mm")
        q_evac = sem("q_evac")
        qp_mm = sem("qp_mm")
        qp_hi = sem("qp_hi")
        qp_lo = sem("qp_lo")
        tok_scores = sem("tok_scores")
        tok16_ready = sem("tok16_ready")
        tokrow_full = [sem(f"tokrow_full{k}") for k in range(2)]
        split_hi = sem("split_hi")
        norm_step = sem("norm_step")
        a_ready = sem("a_ready")
        aT_mm = sem("aT_mm")
        aT_hi = sem("aT_hi")
        aT_lo = sem("aT_lo")
        score_ready = sem("score_ready")
        max_part = sem("max_part")
        negmax_ready = sem("negmax_ready")
        exp_done = sem("exp_done")
        sum_ready = sem("sum_ready")
        rsum_ready = sem("rsum_ready")
        probs_ready = sem("probs_ready")
        turned = sem("turned")
        pt_hi = sem("pt_hi")
        pt_lo = sem("pt_lo")
        pv_done = sem("pv_done")
        avg_ready = sem("avg_ready")
        ptok_mm = sem("ptok_mm")
        ptok_evac = sem("ptok_evac")
        ptok_moved = sem("ptok_moved")
        stats_done = sem("stats_done")
        ln_step = sem("ln_step")
        ln_step2 = sem("ln_step2")
        rstd_ready = sem("rstd_ready")
        sd_ready = sem("sd_ready")
        any_step = sem("any_step")
        pool_step = sem("pool_step")
        ah_mm = sem("ah_mm")
        ah_evac = sem("ah_evac")
        wo_mm = sem("wo_mm")
        f1_mm = sem("f1_mm")
        f1_evac = sem("f1_evac")
        f2_mm = sem("f2_mm")
        tg_ready = sem("tg_ready")
        out_done = sem("out_done")

        def slot_uses(l, b, natural):
            return 2 * B * l + 2 * b + (2 if natural else 1) if l < 2 else 4 * B + b + 1

        W_OF = [0, 4 * WCH, 8 * WCH + 4]
        def w_chunk_q(l, n): return W_OF[l] + n
        def w_chunk_o(l, n): return W_OF[l] + 2 * WCH + n
        def w_chunk_m(n): return 8 * WCH + n

        def col(name, c):
            a = PACK[name] + c
            return pk[:, a:a + 1]

        def chunk_used(n):
            for l in reversed(range(L)):
                if n >= W_OF[l]:
                    i = n - W_OF[l]
                    if i < 2 * WCH:
                        return qp_mm, DC * (H * l + HPC * (i // 2 + 1))
                    if i < 4 * WCH:
                        return wo_mm, H * l + HPC * ((i - 2 * WCH) // 2 + 1)
                    i -= 4 * WCH
                    return (f1_mm, 4 * (i + 1)) if i < 2 else (f2_mm, 4 * (i - 1))

        def apart(eng):
            eng.sem_inc(passed, 1)

        def batches(eng, body, tail=None):
            body(0, 0, True, False)
            with eng.Fori(1, B - 2, 2) as b:
                body(b, 1, False, False)
                body(b + 1, 0, False, False)
            body(B - 1, (B - 1) % 2, False, True)

        def pv_part(s):
            if s == 0:
                return (0, 2, 3, 1)
            if s <= 4:
                return (1, s - 1, 4, 1)
            return (0, s - 5, 3, 0)

        PVN = DC * NT * 3

        block = es.enter_context(nc.Block())

        @block.sync
        def _(sp):
            def weights(n, kd, src):
                if n >= 4:
                    sp.wait_ge(*chunk_used(n - 4))
                dst = wring[0:src.shape[0], n % 4, 0:src.shape[1]]
                sp.dma_start(dst, src).then_inc(w_full[n % 4], 16)

            def q_weights(l, lo, hi):
                for n in range(lo, hi):
                    weights(w_chunk_q(l, n), KD[l], (wq if n % 2 == 0 else wk)[l][n // 2])

            def o_weights(l, lo, hi):
                for n in range(lo, hi):
                    weights(w_chunk_o(l, n), KD[l], (wv if n % 2 == 0 else wo)[l][n // 2])

            def piece(l, b, k, natural):
                if l < 2:
                    n = 8 * (B * l + b) + (4 if natural else 0) + k
                    if l > 0 or natural or not isinstance(b, int) or b > 0:
                        sp.wait_ge(stage_free, n - 3)
                        apart(sp)
                    if l == 1 and not natural and (not isinstance(b, int) or b > 0):
                        sp.wait_ge(stats_done, 4 * b - 4 + k + 1)
                        apart(sp)
                else:
                    sp.wait_ge(stage_free, 16 * B + 4 * b + k - 3)
                    apart(sp)
                    if isinstance(b, int) and b == 0:
                        sp.wait_ge(stats_done, 4 * (B - 1) + k + 1)
                        apart(sp)
                    else:
                        sp.wait_ge(aT_mm, 8 * b - 8 + 2 * k + 2)
                        apart(sp)
                bb = bass.ds(b, 1)
                if natural:
                    src = ctx_nat[bb, :, k * JP * D:(k + 1) * JP * D].rearrange("b p n -> (b p) n")
                    dst = stage[0:TP, k, :]
                else:
                    w = T * DC // PIECES
                    src = ctx_t[bb, :, k * w:(k + 1) * w].rearrange("b p n -> (b p) n")
                    dst = stageT[:, k, :]
                sp.dma_start(dst, src).then_inc(stage_full[k], 16)

            def pieces(l, b):
                for natural in ((False, True) if l < 2 else (True,)):
                    for k in range(PIECES):
                        piece(l, b, k, natural)

            def token_row(l, b, par):
                g = B * l + b
                if l > 0 or not isinstance(b, int) or b > 1:
                    sp.wait_ge(score_ready, 3 * RT * (g - 1))
                    apart(sp)
                if isinstance(b, int) and b == 0:
                    sp.wait_ge(tok16_ready, l + 1)
                    apart(sp)
                sp.dma_start(tokrow[0:1, par, :].rearrange("p (h q) -> p h q", h=H),
                             tok16[:, bass.ds(b * Q, Q)]).then_inc(tokrow_full[par], 16)

            def batch_loads(l, b, par):
                pieces(l, b)
                if l < 2:
                    token_row(l, b, par)
                else:
                    mask_load(b)

            def mask_load(b):
                if not isinstance(b, int) or b > 0:
                    sp.wait_ge(mask_ready, b)
                    apart(sp)
                sp.dma_start(mask8[:, :], mask[bass.ds(b, 1), :].broadcast_to([P, T])).then_inc(mask_full, 16)

            sp.dma_start(xT[:, :, :], x_t).then_inc(in_x, 16)
            sp.dma_start(pk[:, :], pack).then_inc(in_pack, 16)
            sp.dma_start(vr[:, :, :, :], vrows).then_inc(in_pack, 16)
            q_weights(0, 0, 4)
            for k in range(PIECES):
                piece(0, 0, k, False)
            sp.dma_start(a_sc[:, :], a_scale.broadcast_to([TP, D])).then_inc(in_aud, 16)
            sp.dma_start(a_of[:, :], a_offset.broadcast_to([TP, D])).then_inc(in_aud, 16)
            sp.dma_start(tg[:, 0:1], gate.broadcast_to([P, 1])).then_inc(in_aud, 16)
            q_weights(0, 4, 8)
            for l in range(L):
                if l == 0:
                    for k in range(PIECES):
                        piece(0, 0, k, True)
                if l < 2:
                    token_row(l, 0, 0)
                else:
                    mask_load(0)
                batch_loads(l, 1, 1)
                with sp.Fori(2, B - 1, 2) as b:
                    batch_loads(l, b, 0)
                    batch_loads(l, b + 1, 1)
                sp.wait_ge(pv_done, 4 * B * (l + 1))
                o_weights(l, 0, 4)
                if l + 1 < L:
                    for k in range(PIECES):
                        piece(l + 1, 0, k, l + 1 == 2)
                    o_weights(l, 4, 8)
                    if l == 1:
                        for n in range(4):
                            weights(w_chunk_m(n), P, (w1 if n < 2 else w2)[n % 2])
                    if l + 1 < 2:
                        for k in range(PIECES):
                            piece(l + 1, 0, k, True)
                    q_weights(l + 1, 0, 8)
                else:
                    o_weights(l, 4, 8)
            for c in range(DC):
                sp.wait_ge(x_ready, 3 * DC + c + 1)
                sp.dma_start(out[:, c, :], xT[:, c, :]).then_inc(out_done, 16)
            sp.wait_ge(out_done, 16 * DC)

        @block.gpsimd
        def _(pool):
            steps = [0]

            def link(ins):
                steps[0] += 1
                ins.then_inc(pool_step, 1)
                pool.wait_ge(pool_step, steps[0])

            nc.gpsimd.memset(one[:, :], 1.0)
            nc.gpsimd.memset(epsc[:, :], EPS)
            nc.gpsimd.memset(dmean[:, :], 1.0 / D)
            nc.gpsimd.memset(selT[:, :], 0.0)
            link(nc.gpsimd.memset(ident[:, :], 0.0))
            nc.gpsimd.affine_select(out=ident[:, :], in_=ident[:, :], compare_op=ALU.not_equal, fill=1.0, base=0,
                                    pattern=[[-1, P]], channel_multiplier=1)
            nc.gpsimd.affine_select(out=selT[:, :], in_=selT[:, :], compare_op=ALU.not_equal, fill=1.0, base=-TP,
                                    pattern=[[0, 1]], channel_multiplier=1).then_inc(const_ready, 1)
            pool.wait_ge(bkd_ready, 1)
            for l in range(2):
                src = bkd[:, l, :].unsqueeze(2).broadcast_to([P, H, H])
                nc.gpsimd.affine_select(out=bkm[:, l, :, :], in_=src, compare_op=ALU.is_equal, fill=0.0, base=0,
                                        pattern=[[1, H], [-1, H]], channel_multiplier=0).then_inc(const_ready, 1)

            def split(l, b, par, natural):
                g = B * l + b
                if l > 0 or not isinstance(b, int) or b >= 2:
                    if natural:
                        pool.wait_ge(pv_done, 4 * g - 4)
                    else:
                        pool.wait_ge(score_ready, 3 * RT * (g - 1))
                for k in range(PIECES):
                    pool.wait_ge(stage_full[k], 16 * slot_uses(l, b, natural))
                    apart(pool)
                    if natural:
                        src = stageN[:, k, :, :]
                        hi, lo = (nat[:, par, i, k * JP:(k + 1) * JP, :] for i in range(2))
                    else:
                        w = T * DC // PIECES
                        src = stageT[:, k, :]
                        hi, lo = (ctxT[:, par, i, k * w // T, (k * w) % T:(k * w) % T + w] for i in range(2))
                    nc.gpsimd.tensor_copy(hi, src).then_inc(split_hi, 1)
                    n = (8 * g + (4 if natural else 0) if l < 2 else 16 * B + 4 * b) + k + 1
                    pool.wait_ge(split_hi, n)
                    ins = nc.gpsimd.tensor_tensor(lo, src, hi, ALU.subtract)
                    ins.then_inc(stage_free, 1)

            def normalise(b):
                if isinstance(b, int) and b == 0:
                    pool.wait_ge(in_aud, 48)
                    pool.wait_ge(rstd_ready, 1)
                base = 9 * b
                for i, src in enumerate((mu, rstd)):
                    ins = nc.gpsimd.tensor_copy(mrb[:, i, :], src[:, bass.ds(b * NT, NT)])
                ins.then_inc(norm_step, 1)
                pool.wait_ge(norm_step, base + 1)
                for k in range(PIECES):
                    pool.wait_ge(stage_full[k], 16 * slot_uses(2, b, True))
                    apart(pool)
                    for j in range(JP):
                        c = k * JP + j
                        ins = nc.gpsimd.tensor_scalar(stageN[:, k, j, :], stageN[:, k, j, :], mrb[:, 0, c:c + 1],
                                                      mrb[:, 1, c:c + 1], ALU.subtract, ALU.mult)
                    ins.then_inc(norm_step, 1)
                    pool.wait_ge(norm_step, base + 2 + 2 * k)
                    bc = [v[:, :].unsqueeze(1).broadcast_to([TP, JP, D]) for v in (a_sc, a_of)]
                    nc.gpsimd.tensor_tensor(stageN[:, k, :, :], stageN[:, k, :, :], bc[0], ALU.mult)\
                        .then_inc(norm_step, 1)
                    pool.wait_ge(norm_step, base + 3 + 2 * k)
                    nc.gpsimd.tensor_tensor(stageN[:, k, :, :], stageN[:, k, :, :], bc[1], ALU.add)\
                        .then_inc(a_ready, 1)

            def prepare(l, b, par):
                if l < 2:
                    split(l, b, par, False)
                else:
                    normalise(b)
                    pool.wait_ge(a_ready, 4 * b + 4)
                split(l, b, par, True)

            for l in range(L):
                first = 0
                if l == 0:
                    prepare(0, 0, 0)
                    prepare(0, 1, 1)
                    first = 2
                if l == 2:
                    prepare(2, 0, 0)
                    prepare(2, 1, 1)
                    first = 2
                with pool.Fori(first, B - 1, 2) as b:
                    prepare(l, b, 0)
                    prepare(l, b + 1, 1)
                if l < 2:
                    pool.wait_ge(pv_done, 4 * B * (l + 1))
                    pool.wait_ge(bvd_ready, 1)
                    src = bvd[:, l, :].unsqueeze(1).broadcast_to([H, H, P])
                    nc.gpsimd.affine_select(out=bvm, in_=src, compare_op=ALU.is_equal, fill=0.0, base=0,
                                            pattern=[[-1, H], [0, P]], channel_multiplier=1).then_inc(bvm_ready, 1)

        @block.tensor
        def _(pe):
            def mm(o, a, c, start, stop, skip=False):
                return nc.tensor.matmul(o, a, c, start=start, stop=stop, skip_group_check=skip)

            def layer_norm(n, x_count):
                if n == 0:
                    pe.wait_ge(const_ready, 3)
                    pe.wait_ge(in_x, 16)
                else:
                    pe.wait_ge(x_ready, x_count)
                for c in range(DC):
                    ins = mm(S[2][:, 0:NQ], dmean[:, :], xT[:, c, :], c == 0, c == DC - 1)
                ins.then_inc(mean_ready, 1)
                pe.wait_ge(sq_ready, n + 1)
                for c in range(DC):
                    ins = mm(M[:, 0:NQ], dmean[:, :], sq[:, c, :], c == 0, c == DC - 1)
                ins.then_inc(var_ready, 1)

            def weights_in(n):
                pe.wait_ge(w_full[n % 4], 16 * (n // 4 + 1))
                return wring[:, n % 4, :]

            def query_projection(l):
                kd = KD[l]
                hid_in = hT if l < 2 else xT
                if l < 2:
                    pe.wait_ge(h_ready, l + 1)
                else:
                    pe.wait_ge(x_ready, 3 * DC)

                def query(h):
                    w = weights_in(w_chunk_q(l, h // HPC * 2)).rearrange("p n -> p n")[:, 0:DC * HPC * kd]\
                        .rearrange("p (c n) -> p c n", c=DC)
                    if l > 0 or h >= 2:
                        pe.wait_ge(q_evac, H * l + h - 1)
                    j = h % HPC
                    for c in range(DC):
                        ins = mm(TB[h % 2][0:kd, 0:NQ], w[:, c, j * kd:(j + 1) * kd], hid_in[:, c, :],
                                 c == 0, c == DC - 1)
                    ins.then_inc(q_mm, 1)

                def through_keys(h):
                    w = weights_in(w_chunk_q(l, h // HPC * 2 + 1)).rearrange("p (j n) -> p j n", j=HPC)
                    pe.wait_ge(q_evac, H * l + h + 1)
                    q = hring[0:kd, h % 4, :]
                    if l < 2:
                        ins = mm(M[0:H, 0:NQ], bkm[:, l, h, :], q, h == 0, h == H - 1)
                        if h == H - 1:
                            ins.then_inc(tok_scores, 1)
                    for c in range(DC):
                        n = DC * (H * l + h) + c
                        if n >= 4:
                            pe.wait_ge(qp_lo, n - 3)
                        ins = mm(QB[n % 4][:, 0:NQ], w[0:kd, h % HPC, c * P:(c + 1) * P], q, True, True)
                        ins.then_inc(qp_mm, 1)

                query(0)
                for h in range(H):
                    if h + 1 < H:
                        query(h + 1)
                    through_keys(h)

            def scores(l, b, s, par, first):
                g = B * l + b
                t = RT * g + s
                if first and s == 0:
                    pe.wait_ge(qp_lo, DC * H * (l + 1))
                if s == 0:
                    if l < 2:
                        pe.wait_ge(stage_free, 8 * g + 4)
                    else:
                        pe.wait_ge(aT_lo, 8 * b + 8)
                bb = bass.ds(b, 1)
                for c in range(NB):
                    if l < 2 and not (first and s == 0):
                        pe.wait_ge(exp_done, 3 * t + c - 2)
                    if l == 2 and not (first and s == 0):
                        pe.wait_ge(max_part, 3 * t + c - 2)
                    o = S[c][:, 0:CW]
                    n = 0
                    for d in range(DC):
                        for qi, ci in ((0, 0), (0, 1), (1, 0)):
                            q = qs16[:, bb, qi, d, s * P:(s + 1) * P].rearrange("p b r -> p (b r)")
                            ins = mm(o, q, ctxT[:, par, ci, d, c * CW:(c + 1) * CW], n == 0, n == 3 * DC - 1)
                            n += 1
                    if l < 2 and c == NB - 1:
                        if s == 0:
                            pe.wait_ge(tokrow_full[par], 64 * l + 8 * (b - par) + 16)
                        ins = mm(S[c][:, CW:CW + 1], tokrow[0:1, par, s * P:(s + 1) * P], one[:, :],
                                 False, True, skip=True)
                    ins.then_inc(score_ready, 1)

            def turn(l, t, tpar, f, W):
                if f == 0:
                    pe.wait_ge(probs_ready, t + 1)
                n = 3 * t + f
                if not (isinstance(t, int) and n < 2):
                    pe.wait_ge(pt_lo, n - 1)
                bank = TB[(3 * tpar + f) % 2]
                for j in range(TPB):
                    c = f * TPB + j
                    ins = nc.tensor.transpose(bank[0:W, j * P:(j + 1) * P],
                                              prob[:, tpar % 2, c * TP:c * TP + W], ident[:, :])
                ins.then_inc(turned, 1)

            def average(l, b, par, grp, lo, hi):
                g = B * l + b
                rows = slice(0, GROUP_A * P) if grp == 0 else slice(GROUP_A * P, R)
                nrow = rows.stop - rows.start
                if lo == 0:
                    pe.wait_ge(pt_lo, 3 * (RT * g + (GROUP_A if grp == 0 else RT)))
                    if grp == 0:
                        pe.wait_ge(stage_free, 8 * g + 8 if l < 2 else 16 * B + 4 * b + 4)
                for m in range(lo, hi):
                    d, r = divmod(m, 3 * NT)
                    j, i = divmod(r, 3)
                    pi, ci = ((0, 0), (1, 0), (0, 1))[i]
                    k = 2 * grp + d
                    if r == 0:
                        if not (isinstance(g, int) and g == 0 and k < 2):
                            pe.wait_ge(avg_ready, 4 * g + k - 1)
                        if l < 2 and d == DC - 1:
                            if not (isinstance(g, int) and g == 0 and grp == 0):
                                pe.wait_ge(ptok_evac, 2 * g + grp)
                            for i2 in range(2):
                                ins = mm(M[0:1, 0:nrow], selT[0:TP + 1, :], probT[:, i2, NT - 1, rows],
                                         i2 == 0, i2 == 1)
                            ins.then_inc(ptok_mm, 1)
                    ins = mm(PV[k % 2][:, 0:nrow], nat[:, par, ci, j, d * P:(d + 1) * P],
                             probT[0:TP, pi, j, rows], r == 0, r == 3 * NT - 1)
                    if r == 3 * NT - 1:
                        ins.then_inc(pv_done, 1)

            def turn_context(b, par, f):
                k, c = divmod(f, DC)
                if c == 0:
                    pe.wait_ge(a_ready, 4 * b + k + 1)
                if not (isinstance(b, int) and b == 0 and f == 0):
                    pe.wait_ge(aT_lo, 8 * b + f)
                for j in range(JP):
                    ins = nc.tensor.transpose(M[:, j * TP:(j + 1) * TP], stageN[:, k, j, c * P:(c + 1) * P],
                                              ident[0:TP, 0:TP])
                ins.then_inc(aT_mm, 1)

            def attention(l):
                W = TP + 1 if l < 2 else TP

                def body(b, par, first, last):
                    t0 = RT * (B * l + b)
                    for s in range(RT):
                        scores(l, b, s, par, first)
                        prev = s > 0 or not first
                        if prev:
                            tp = RT * par + s - 1 if s > 0 else RT * (1 - par) + RT - 1
                            turn(l, t0 + s - 1, tp, 0, W)
                            turn(l, t0 + s - 1, tp, 1, W)
                        extra = l == 2 and not last and 2 <= s < 6
                        if extra:
                            turn_context(b + 1, 1 - par, 2 * (s - 2))
                        grp, part, parts, back = pv_part(s)
                        work = not (first and back)
                        lo, hi = part * PVN // parts, (part + 1) * PVN // parts
                        mid = lo + (hi - lo) * 2 // 3
                        if work:
                            average(l, b - back, (par + back) % 2, grp, lo, mid)
                        if prev:
                            turn(l, t0 + s - 1, tp, 2, W)
                        if work:
                            average(l, b - back, (par + back) % 2, grp, mid, hi)
                        if extra:
                            turn_context(b + 1, 1 - par, 2 * (s - 2) + 1)
                    if last:
                        t = t0 + RT - 1
                        average(l, b, par, 0, 2 * PVN // 3, PVN)
                        for f in range(3):
                            turn(l, t, RT * par + RT - 1, f, W)
                        average(l, b, par, 1, 0, PVN)

                batches(pe, body)

            def output_projection(l):
                kd = KD[l]
                pe.wait_ge(avg_ready, 4 * B * (l + 1))

                def head(h):
                    w = weights_in(w_chunk_o(l, h // HPC * 2))[:, 0:DC * HPC * kd]\
                        .rearrange("p (c n) -> p c n", c=DC)
                    n = H * l + h
                    if n >= 2:
                        pe.wait_ge(ah_evac, n - 1)
                    j = h % HPC
                    o = TB[h % 2][0:kd, 0:NQ]
                    for c in range(DC):
                        ins = mm(o, w[:, c, j * kd:(j + 1) * kd], avg[:, :, c, h * Q:(h + 1) * Q],
                                 c == 0, l == 2 and c == DC - 1)
                    if l < 2:
                        if h == 0:
                            pe.wait_ge(bvm_ready, l + 1)
                            pe.wait_ge(ptok_moved, 16 * B * (l + 1))
                        ins = mm(o, bvm[:, h, :], ptok16[:, :], False, True)
                    ins.then_inc(ah_mm, 1)

                def out(h):
                    w = weights_in(w_chunk_o(l, h // HPC * 2 + 1)).rearrange("p (j n) -> p j n", j=HPC)
                    pe.wait_ge(ah_evac, H * l + h + 1)
                    for c in range(DC):
                        ins = mm(PV[c][:, 0:NQ], w[0:kd, h % HPC, c * P:(c + 1) * P], hring[0:kd, h % 4, :],
                                 h == 0, h == H - 1)
                    ins.then_inc(wo_mm, 1)

                head(0)
                for h in range(H):
                    if h + 1 < H:
                        head(h + 1)
                    out(h)

            def mlp():
                pe.wait_ge(h_ready, 3)
                for f in range(FC):
                    w = weights_in(w_chunk_m(f // 4)).rearrange("p (c n) -> p c n", c=DC)
                    if f >= 2:
                        pe.wait_ge(f1_evac, f - 1)
                    j = f % 4
                    for c in range(DC):
                        ins = mm(TB[f % 2][:, 0:NQ], w[:, c, j * P:(j + 1) * P], hT[:, c, :], c == 0, c == DC - 1)
                    ins.then_inc(f1_mm, 1)
                for f in range(FC):
                    w = weights_in(w_chunk_m(2 + f // 4)).rearrange("p (j n) -> p j n", j=4)
                    pe.wait_ge(f1_evac, f + 1)
                    for c in range(DC):
                        ins = mm(PV[c][:, 0:NQ], w[:, f % 4, c * P:(c + 1) * P], hid[:, f, :], f == 0, f == FC - 1)
                    ins.then_inc(f2_mm, 1)

            layer_norm(0, 0)
            query_projection(0)
            attention(0)
            output_projection(0)
            layer_norm(1, DC)
            query_projection(1)
            attention(1)
            output_projection(1)
            layer_norm(2, 2 * DC)
            mlp()
            query_projection(2)
            for f in range(2 * PIECES):
                turn_context(0, 0, f)
            attention(2)
            output_projection(2)

        @block.scalar
        def _(act):
            def layer_norm(n):
                act.wait_ge(var_ready, n + 1)
                if n == 0:
                    act.wait_ge(const_ready, 3)
                nc.scalar.activation(std[:, :], M[:, 0:NQ], ACT.Sqrt, bias=epsc[:, :]).then_inc(std_ready, 1)
                act.wait_ge(xn_ready, n + 1)
                for c in range(DC):
                    ins = nc.scalar.activation(hT[:, c, :], xc[:, c, :], ACT.Identity,
                                               scale=col(f"ln_scale{n}", c), bias=col(f"ln_offset{n}", c))
                ins.then_inc(h_ready, 1)

            def query_projection(l):
                kd = KD[l]
                for h in range(H + 1):
                    if h < H:
                        act.wait_ge(q_mm, H * l + h + 1)
                        if h >= 4:
                            act.wait_ge(qp_mm, DC * (H * l + h - 3))
                        o = hring[0:kd, h % 4, :]
                        if l < 2:
                            ins = nc.scalar.activation(o, TB[h % 2][0:kd, 0:NQ], ACT.Identity,
                                                       bias=col(("bq", l), h))
                        else:
                            ins = nc.scalar.activation(o, TB[h % 2][0:kd, 0:NQ], ACT.Copy)
                        ins.then_inc(q_evac, 1)
                    if h > 0:
                        for c in range(DC):
                            n = DC * (H * l + h - 1) + c
                            act.wait_ge(qp_mm, n + 1)
                            o = qs16[:, :, 0, c, (h - 1) * Q:h * Q]
                            nc.scalar.activation(o, QB[n % 4][:, 0:NQ].rearrange("p (b q) -> p b q", b=B),
                                                 ACT.Copy, scale=float(kd) ** -0.5).then_inc(qp_hi, 1)
                if l < 2:
                    act.wait_ge(tok_scores, l + 1)
                    nc.scalar.activation(tok16[:, :], M[0:H, 0:NQ], ACT.Copy, scale=float(kd) ** -0.5)\
                        .then_inc(tok16_ready, 1)

            def exponentiate(l, t, tp, c, first):
                i = tp % 2
                w = CW + 1 if l < 2 and c == NB - 1 else CW
                if c == 0:
                    act.wait_ge(negmax_ready, t + 1)
                    if l < 2 and not first:
                        act.wait_ge(turned, 3 * t - 3)
                o = prob[:, i, c * CW:c * CW + w]
                src = S[c][:, 0:w] if l < 2 else o
                nc.scalar.activation(o, src, ACT.Exp, bias=nmax[:, i, :],
                                     accum_out=sum3[:, i, c:c + 1]).then_inc(exp_done, 1)

            def high_half(g, t, tp, s, f, W, fresh):
                act.wait_ge(turned, 3 * t + f + 1)
                if f == 0 and not fresh and s in (0, GROUP_A):
                    act.wait_ge(pv_done, 4 * g - 4 + (2 if s < GROUP_A else 4))
                o = probT[0:W, 0, f * TPB:(f + 1) * TPB, s * P:(s + 1) * P]
                src = TB[(3 * tp + f) % 2][0:W, :].rearrange("p (j r) -> p j r", j=TPB)
                nc.scalar.activation(o, src, ACT.Copy).then_inc(pt_hi, 1)

            def store_average(l, b, k):
                g = B * l + b
                grp, d = divmod(k, 2)
                act.wait_ge(pv_done, 4 * g + k + 1)
                r0, r1 = (0, GROUP_A * P) if grp == 0 else (GROUP_A * P, R)
                o = avg[:, bass.ds(b, 1), d, r0:r1].rearrange("p b r -> p (b r)")
                nc.scalar.activation(o, PV[k % 2][:, 0:r1 - r0], ACT.Copy, scale=1.0 / PROB_SCALE)\
                    .then_inc(avg_ready, 1)

            def store_token(l, b, grp):
                g = B * l + b
                act.wait_ge(ptok_mm, 2 * g + grp + 1)
                if grp == 0 and not (isinstance(g, int) and g == 0):
                    act.wait_ge(ptok_moved, 16 * g)
                r0, r1 = (0, GROUP_A * P) if grp == 0 else (GROUP_A * P, R)
                nc.scalar.activation(ptok[:, r0:r1], M[0:1, 0:r1 - r0], ACT.Copy, scale=1.0 / PROB_SCALE)\
                    .then_inc(ptok_evac, 1)
                if grp == 1:
                    act.wait_ge(ptok_evac, 2 * g + 2)
                    act.dma_start(ptok16[:, bass.ds(b * Q, Q)],
                                  ptok[0:1, :].rearrange("p (h q) -> p h q", h=H)).then_inc(ptok_moved, 16)

            def context_high(b, par, f):
                k, c = divmod(f, DC)
                act.wait_ge(aT_mm, 8 * b + f + 1)
                if f == 0 and not (isinstance(b, int) and b == 0):
                    act.wait_ge(score_ready, 3 * RT * (2 * B + b - 1))
                nc.scalar.activation(ctxT[:, par, 0, c, k * JP * TP:(k + 1) * JP * TP], M[:, 0:JP * TP], ACT.Copy)\
                    .then_inc(aT_hi, 1)

            def attention(l):
                W = TP + 1 if l < 2 else TP

                def body(b, par, first, last):
                    t0 = RT * (B * l + b)
                    for s in range(RT):
                        prev = s > 0 or not first
                        tp = RT * par + s - 1 if s > 0 else RT * (1 - par) + RT - 1
                        ps = (s - 1) % RT
                        extra = l == 2 and not last and 2 <= s < 6
                        start = first and l == 0
                        for f in range(NB):
                            exponentiate(l, t0 + s, RT * par + s, f, start and s < 2)
                            if prev:
                                high_half(B * l + b - (s == 0), t0 + s - 1, tp, ps, f, W, start)
                            if extra and f == 1:
                                context_high(b + 1, 1 - par, 2 * (s - 2))
                        if s == 0 and not first:
                            if l < 2:
                                store_token(l, b - 1, 0)
                            store_average(l, b - 1, 1)
                        if s == 2 and not first:
                            store_average(l, b - 1, 2)
                        if s == 3 and not first and l < 2:
                            store_token(l, b - 1, 1)
                        if s == 4 and not first:
                            store_average(l, b - 1, 3)
                        if s == 6:
                            store_average(l, b, 0)
                        if extra:
                            context_high(b + 1, 1 - par, 2 * (s - 2) + 1)
                    if last:
                        if l < 2:
                            store_token(l, b, 0)
                        store_average(l, b, 1)
                        for f in range(3):
                            high_half(B * l + b, t0 + RT - 1, RT * par + RT - 1, RT - 1, f, W, False)
                        store_average(l, b, 2)
                        if l < 2:
                            store_token(l, b, 1)
                        store_average(l, b, 3)

                batches(act, body)

            def output_projection(l):
                kd = KD[l]
                for h in range(H):
                    act.wait_ge(ah_mm, H * l + h + 1)
                    if h >= 4:
                        act.wait_ge(wo_mm, H * l + h - 3)
                    o = hring[0:kd, h % 4, :]
                    src = TB[h % 2][0:kd, 0:NQ]
                    if l < 2:
                        ins = nc.scalar.activation(o, src, ACT.Identity, bias=col(("bv", l), h))
                    else:
                        ins = nc.scalar.activation(o, src, ACT.Copy)
                    ins.then_inc(ah_evac, 1)

            act.wait_ge(in_pack, 32)
            layer_norm(0)
            query_projection(0)
            attention(0)
            output_projection(0)
            layer_norm(1)
            query_projection(1)
            attention(1)
            act.wait_ge(ln_step, 5)
            nc.scalar.activation(rstd[:, :], stt[:, 0, :], ACT.Sqrt, bias=epsc[0:TP, :]).then_inc(sd_ready, 1)
            output_projection(1)
            layer_norm(2)
            for f in range(FC):
                act.wait_ge(f1_mm, f + 1)
                nc.scalar.activation(hid[:, f, :], TB[f % 2][:, 0:NQ], ACT.Gelu, bias=col("b_fc1", f))\
                    .then_inc(f1_evac, 1)
            act.wait_ge(in_aud, 48)
            nc.scalar.activation(tg[:, 1:2], tg[:, 0:1], ACT.Tanh).then_inc(tg_ready, 1)
            query_projection(2)
            for f in range(2 * PIECES):
                context_high(0, 0, f)
            attention(2)
            output_projection(2)

        @block.vector
        def _(dve):
            def layer_norm(n):
                dve.wait_ge(mean_ready, n + 1)
                for c in range(DC):
                    ins = nc.vector.tensor_tensor(xc[:, c, :], xT[:, c, :], S[2][:, 0:NQ], ALU.subtract)
                ins.then_inc(xc_ready, 1)
                dve.wait_ge(xc_ready, n + 1)
                nc.vector.tensor_tensor(sq, xc, xc, ALU.mult).then_inc(sq_ready, 1)
                dve.wait_ge(std_ready, n + 1)
                nc.vector.reciprocal(std[:, :], std[:, :]).then_inc(rs_ready, 1)
                dve.wait_ge(rs_ready, n + 1)
                for c in range(DC):
                    ins = nc.vector.tensor_tensor(xc[:, c, :], xc[:, c, :], std[:, :], ALU.mult)
                ins.then_inc(xn_ready, 1)

            def query_projection(l):
                for h in range(H):
                    for c in range(DC):
                        n = DC * (H * l + h) + c
                        dve.wait_ge(qp_hi, n + 1)
                        hi, lo = (qs16[:, :, i, c, h * Q:(h + 1) * Q] for i in range(2))
                        nc.vector.scalar_tensor_tensor(
                            lo, QB[n % 4][:, 0:NQ].rearrange("p (b q) -> p b q", b=B), float(KD[l]) ** -0.5, hi,
                            ALU.mult, ALU.subtract).then_inc(qp_lo, 1)

            def maxima(l, t, tp, c, par):
                i = tp % 2
                w = CW + 1 if l < 2 and c == NB - 1 else CW
                dve.wait_ge(score_ready, 3 * t + c + 1)
                if l < 2:
                    nc.vector.tensor_reduce(mx3[:, i, c:c + 1], S[c][:, 0:w], AX_X, ALU.max).then_inc(max_part, 1)
                else:
                    if c == 0:
                        dve.wait_ge(turned, 3 * t - 3)
                    apart(dve)
                    nc.vector.tensor_tensor_reduce(
                        out=prob[:, i, c * CW:(c + 1) * CW], in0=S[c][:, 0:CW],
                        in1=maskb[:, par, c * CW:(c + 1) * CW], scale=1.0, scalar=-3.0e38,
                        op0=ALU.add, op1=ALU.max, accum_out=mx3[:, i, c:c + 1]).then_inc(max_part, 1)

            def row_maximum(l, t, tp):
                i = tp % 2
                dve.wait_ge(max_part, 3 * t + 3)
                nc.vector.tensor_reduce(nmax[:, i, :], mx3[:, i, 0:NB], AX_X, ALU.max, negate=True)\
                    .then_inc(negmax_ready, 1)

            def normalise(l, t, tp):
                i = tp % 2
                w = T + 1 if l < 2 else T
                dve.wait_ge(exp_done, 3 * t + 3)
                nc.vector.tensor_reduce(rsum[:, i, 0:1], sum3[:, i, 0:NB], AX_X, ALU.add).then_inc(sum_ready, 1)
                dve.wait_ge(sum_ready, t + 1)
                nc.vector.reciprocal(rsum[:, i, 1:2], rsum[:, i, 0:1]).then_inc(rsum_ready, 1)
                dve.wait_ge(rsum_ready, t + 1)
                nc.vector.tensor_scalar(prob[:, i, 0:w], prob[:, i, 0:w], rsum[:, i, 1:2], PROB_SCALE,
                                        ALU.mult, ALU.mult).then_inc(probs_ready, 1)

            def low_half(t, tp, s, f, W):
                dve.wait_ge(pt_hi, 3 * t + f + 1)
                hi, lo = (probT[0:W, i, f * TPB:(f + 1) * TPB, s * P:(s + 1) * P] for i in range(2))
                src = TB[(3 * tp + f) % 2][0:W, :].rearrange("p (j r) -> p j r", j=TPB)
                nc.vector.tensor_tensor(lo, src, hi, ALU.subtract).then_inc(pt_lo, 1)

            def context_low(b, par, f):
                k, c = divmod(f, DC)
                dve.wait_ge(aT_hi, 8 * b + f + 1)
                hi, lo = (ctxT[:, par, i, c, k * JP * TP:(k + 1) * JP * TP] for i in range(2))
                nc.vector.tensor_tensor(lo, M[:, 0:JP * TP], hi, ALU.subtract).then_inc(aT_lo, 1)

            def context_stats(b, k):
                dve.wait_ge(stage_full[k], 16 * slot_uses(1, b, True))
                for j in range(JP):
                    o = stats[:, bass.ds(b, 1), k * JP + j, :].rearrange("p b n -> p (b n)")
                    ins = nc.vector.bn_stats(o, stageN[:, k, j, :])
                ins.then_inc(stats_done, 1)

            def mask_row(b, par):
                dve.wait_ge(mask_full, 16 * b + 16)
                base = 4 * b
                nc.vector.tensor_reduce(anym[:, 0:1], mask8[:, :], AX_X, ALU.max).then_inc(any_step, 1)
                dve.wait_ge(any_step, base + 1)
                nc.vector.tensor_scalar(anym[:, 1:2], anym[:, 0:1], 1.0, 3.0e38, ALU.subtract, ALU.mult)\
                    .then_inc(any_step, 1)
                dve.wait_ge(any_step, base + 2)
                nc.vector.tensor_scalar(anym[:, 2:3], anym[:, 1:2], 4.0, 0.0, ALU.mult, ALU.mult).then_inc(any_step, 1)
                dve.wait_ge(any_step, base + 3)
                nc.vector.tensor_scalar(anym[:, 3:4], anym[:, 2:3], -MASKED, None, ALU.add).then_inc(any_step, 1)
                dve.wait_ge(any_step, base + 4)
                nc.vector.tensor_scalar(maskb[:, par, :], mask8[:, :], MASKED, anym[:, 3:4], ALU.mult, ALU.add)\
                    .then_inc(mask_ready, 1)

            def attention(l):
                W = TP + 1 if l < 2 else TP

                def body(b, par, first, last):
                    t0 = RT * (B * l + b)
                    for s in range(RT):
                        prev = s > 0 or not first
                        tp = RT * par + s - 1 if s > 0 else RT * (1 - par) + RT - 1
                        extra = l == 2 and not last and 2 <= s < 6
                        if prev:
                            normalise(l, t0 + s - 1, tp)
                        if l == 2 and s == 0:
                            dve.wait_ge(mask_ready, b + 1)
                        for c in range(NB):
                            maxima(l, t0 + s, RT * par + s, c, par)
                        row_maximum(l, t0 + s, RT * par + s)
                        if prev:
                            low_half(t0 + s - 1, tp, (s - 1) % RT, 0, W)
                            low_half(t0 + s - 1, tp, (s - 1) % RT, 1, W)
                        if extra:
                            context_low(b + 1, 1 - par, 2 * (s - 2))
                        if prev:
                            low_half(t0 + s - 1, tp, (s - 1) % RT, 2, W)
                        if extra:
                            context_low(b + 1, 1 - par, 2 * (s - 2) + 1)
                        if l == 1 and not last and 2 <= s < 6:
                            context_stats(b + 1, s - 2)
                        if l == 2 and not last and s == 6:
                            mask_row(b + 1, 1 - par)
                    if last:
                        normalise(l, t0 + RT - 1, RT * par + RT - 1)
                        for f in range(3):
                            low_half(t0 + RT - 1, RT * par + RT - 1, RT - 1, f, W)

                batches(dve, body)

            def add_output(l):
                dve.wait_ge(wo_mm, H * (l + 1))
                if l == 2:
                    dve.wait_ge(tg_ready, 1)
                for c in range(DC):
                    sc = col(f"bo{l}", c) if l < 2 else tg[:, 1:2]
                    nc.vector.scalar_tensor_tensor(xT[:, c, :], PV[c][:, 0:NQ], sc, xT[:, c, :],
                                                   ALU.add if l < 2 else ALU.mult, ALU.add).then_inc(x_ready, 1)

            dve.wait_ge(in_pack, 32)
            for l in range(2):
                a, c = PACK["bias_k", l], PACK["bk", l]
                ins = nc.vector.tensor_tensor(bkd[:, l, :], pk[:, a:a + H], pk[:, c:c + H], ALU.subtract)
            ins.then_inc(bkd_ready, 1)
            nc.vector.tensor_tensor(bvd[:, :, :], vr[:, :, 0, :], vr[:, :, 1, :], ALU.subtract).then_inc(bvd_ready, 1)
            layer_norm(0)
            query_projection(0)
            attention(0)
            add_output(0)
            layer_norm(1)
            query_projection(1)
            for k in range(PIECES):
                context_stats(0, k)
            attention(1)

            def ln_link(ins, n):
                ins.then_inc(ln_step, 1)
                dve.wait_ge(ln_step, n)
            dve.wait_ge(stats_done, 4 * B)
            st = stats[:, :, :, :].rearrange("p b j n -> p (b j) n")
            ln_link(nc.vector.tensor_tensor(mu[:, :], st[:, :, 1], st[:, :, 4], ALU.add), 1)
            ln_link(nc.vector.tensor_tensor(stt[:, 1, :], st[:, :, 1], st[:, :, 4], ALU.subtract), 2)
            ln_link(nc.vector.tensor_tensor(stt[:, 0, :], st[:, :, 2], st[:, :, 5], ALU.add), 3)
            ln_link(nc.vector.scalar_tensor_tensor(stt[:, 1, :], stt[:, 1, :], D / 4.0, stt[:, 1, :],
                                                   ALU.mult, ALU.mult), 4)
            nc.vector.tensor_scalar(mu[:, :], mu[:, :], 0.5, None, ALU.mult)
            nc.vector.tensor_tensor(stt[:, 0, :], stt[:, 0, :], stt[:, 1, :], ALU.add).then_inc(ln_step2, 1)
            dve.wait_ge(ln_step2, 1)
            ln_link(nc.vector.tensor_scalar(stt[:, 0, :], stt[:, 0, :], 1.0 / D, None, ALU.mult), 5)
            dve.wait_ge(sd_ready, 1)
            nc.vector.reciprocal(rstd[:, :], rstd[:, :]).then_inc(rstd_ready, 1)

            add_output(1)
            layer_norm(2)
            dve.wait_ge(f2_mm, FC)
            for c in range(DC):
                nc.vector.scalar_tensor_tensor(xT[:, c, :], PV[c][:, 0:NQ], col("b_fc2", c), xT[:, c, :],
                                               ALU.add, ALU.add).then_inc(x_ready, 1)
            query_projection(2)
            mask_row(0, 0)
            for f in range(2 * PIECES):
                context_low(0, 0, f)
            attention(2)
            add_output(2)


_L0 = "L0_xattn_"
_L1 = "L1_xattn_"


def kernel(**inputs):
    import numpy as np
    import concourse.bacc as bacc
    from concourse.bass_utils import run_bass_kernel_spmd

    a = {k: np.asarray(v) for k, v in inputs.items()}
    by_partition = lambda v: v.reshape(-1, P).T

    cols = []
    for l in ("1", "2"):
        cols += [by_partition(a[_L0 + n + l].reshape(-1)) for n in ("bq", "bk", "bv", "bias_k")]
    for n in ("ln1_scale", "ln1_offset", "ln2_scale", "ln2_offset", "ln_mlp_scale", "ln_mlp_offset", "bo1", "bo2",
              "b_fc2", "b_fc1"):
        cols.append(by_partition(a[_L0 + n]))

    def by_model_rows(w):
        return w.reshape(DC, P, WCH, -1).transpose(2, 1, 0, 3).reshape(WCH, P, -1)

    def by_head_rows(w):
        return w.reshape(WCH, HPC, -1, D).transpose(0, 2, 1, 3).reshape(WCH, w.shape[0] // H, -1)

    ctx = a["ctx_2048"]
    arrays = {
        "x_t": a["x"].reshape(NQ, DC, P).transpose(2, 1, 0),
        "ctx_nat": ctx.reshape(B, TP, NT * D),
        "ctx_t": ctx.reshape(B, TP, NT, DC, P).transpose(0, 4, 3, 2, 1).reshape(B, P, DC * T),
        "mask": a["mask_BxS2_bf1"].reshape(B, TP, NT).transpose(0, 2, 1).reshape(B, T).view(np.uint8),
        "pack": np.concatenate(cols, axis=1),
        "vrows": np.stack([np.stack([a[_L0 + n + l].reshape(H, P) for n in ("bias_v", "bv")], axis=1)
                           for l in ("1", "2")], axis=1),
        "a_scale": a[_L1 + "ln_gamma"].reshape(1, D),
        "a_offset": a[_L1 + "ln_beta"].reshape(1, D),
        "gate": a[_L1 + "gate"].reshape(1, 1),
        "wq0": by_model_rows(a[_L0 + "wq1"]), "wq1": by_model_rows(a[_L0 + "wq2"]),
        "wq2": by_model_rows(a[_L1 + "Wq"].T),
        "wk0": by_head_rows(a[_L0 + "wk1"].T), "wk1": by_head_rows(a[_L0 + "wk2"].T),
        "wk2": by_head_rows(a[_L1 + "Wk"]),
        "wv0": by_model_rows(a[_L0 + "wv1"]), "wv1": by_model_rows(a[_L0 + "wv2"]),
        "wv2": by_model_rows(a[_L1 + "Wv"].T),
        "wo0": by_head_rows(a[_L0 + "wo1"]), "wo1": by_head_rows(a[_L0 + "wo2"]),
        "wo2": by_head_rows(a[_L1 + "Wo"].T),
        "w1": a[_L0 + "w_fc1"].reshape(DC, P, 2, F // 2).transpose(2, 1, 0, 3).reshape(2, P, -1),
        "w2": a[_L0 + "w_fc2"].reshape(2, FC // 2, P, D).transpose(0, 2, 1, 3).reshape(2, P, -1),
    }
    nc = bacc.Bacc("TRN2", target_bir_lowering=False, num_devices=1)
    args, feed = {}, {}
    for name, v in arrays.items():
        v = np.ascontiguousarray(v)
        feed[f"in_{name}_dram"] = v
        args[name] = nc.dram_tensor(f"in_{name}_dram", v.shape, mybir.dt.from_np(v.dtype), kind="ExternalInput").ap()
    out = nc.dram_tensor("out_0_dram", (P, DC, NQ), F32, kind="ExternalOutput").ap()
    by_layer = {n: [args.pop(f"{n}{l}") for l in range(L)] for n in ("wq", "wk", "wv", "wo")}
    build(nc, **args, **by_layer, out=out)
    r = run_bass_kernel_spmd(nc, [feed], core_ids=[0])
    got = r.results[0]["out_0_dram"]
    return np.ascontiguousarray(got.transpose(2, 1, 0).reshape(B, Q, D))
```

```python
from contextlib import ExitStack

import concourse.bass as bass
from concourse import mybir

ALU = mybir.AluOpType
ACT = mybir.ActivationFunctionType
F32 = mybir.dt.float32
F16 = mybir.dt.float16
BF16 = mybir.dt.bfloat16
U8 = mybir.dt.uint8
AX_X = mybir.AxisListType.X

B, Q, D, T, H, F = 8, 56, 256, 1500, 16, 1024
P = 128
DC = D // P
NQ = B * Q
R = H * Q
RT = R // P
TP = 125
NT = T // TP
NB = 3
CW = T // NB
TPB = NT // NB
HPC = 4
WCH = H // HPC
L = 3
KD = 128
KA = D // H
HA = P // KA
AR = HA * Q
APAD = 4 * P
W_SCALE = 256.0
GROUP_A, GROUP_B = 4, 3
PIECES = 4
JP = NT // PIECES
EPS = 1e-5
PROB_SCALE = 4096.0
MASKED = 1e30
FC = F // P

PACK = {}
_at = 0
for _l in (0, 1):
    for _n in ("bq", "bk", "bv", "bias_k"):
        PACK[_n, _l] = _at
        _at += H
for _n, _w in (("ln_scale0", DC), ("ln_offset0", DC), ("ln_scale1", DC), ("ln_offset1", DC), ("ln_scale2", DC),
               ("ln_offset2", DC), ("bo0", DC), ("bo1", DC), ("b_fc2", DC), ("b_fc1", FC)):
    PACK[_n] = _at
    _at += _w
NPACK = _at


def build(nc, x_t, ctx_nat, ctx_t, mask, pack, vrows, a_scale, a_offset, gate, wq, wk, wv, wo, w1, w2, out):
    es = ExitStack()
    with es:
        def sb(name, shape, dt=F32):
            return es.enter_context(nc.sbuf_tensor(name, shape, dt))

        def sem(name):
            return es.enter_context(nc.semaphore(name))

        qc = sb("qc", [P, B, DC * R])
        qs16 = qc[:, :, :].bitcast(F16).rearrange("p b (s c r) -> p b s c r", s=2, c=DC)
        avg = qc[:, :, :].rearrange("p b (c r) -> p b c r", c=DC)
        ctxT = sb("ctxT", [P, 2, 2, DC, T], F16)
        nat = sb("nat", [TP, 2, 2, NT, D], F16)
        stage = sb("stage", [P, PIECES, JP * D])
        stageN = stage[0:TP, :, :].rearrange("p k (j d) -> p k j d", j=JP)
        stageT = stage[:, :, 0:T * DC // PIECES]
        probT_bytes = NT * R * 2 * 2
        arena = sb("arena", [P, probT_bytes // 4])
        probT = arena[0:TP + 1, :].bitcast(F16).rearrange("p (s j r) -> p s j r", s=2, j=NT)
        prob = sb("prob", [P, 2, T + 4])
        WSL = DC * HPC * P
        at = 4 * WSL
        wring = arena[:, 0:at].rearrange("p (k n) -> p k n", k=4)
        hring = arena[:, at:at + 4 * NQ].rearrange("p (k n) -> p k n", k=4)
        hid = arena[:, at:at + FC * NQ].rearrange("p (f n) -> p f n", f=FC)
        bvm = arena[0:H, at + 4 * NQ:at + 4 * NQ + H * P].rearrange("p (h k) -> p h k", h=H)
        at2 = probT_bytes // 4 - DC * NQ
        hT = arena[:, at2:].rearrange("p (c n) -> p c n", c=DC)
        xc = prob[:, 0, 0:DC * NQ].rearrange("p (c n) -> p c n", c=DC)
        sq = prob[:, 1, 0:DC * NQ].rearrange("p (c n) -> p c n", c=DC)
        std = sb("std", [P, NQ])
        xT = sb("xT", [P, DC, NQ])
        pk = sb("pk", [P, NPACK])
        bkd = sb("bkd", [P, 2, H])
        bkm = sb("bkm", [P, 2, H, H])
        vr = sb("vr", [H, 2, 2, P])
        bvd = sb("bvd", [H, 2, P])
        small = sb("small", [P, 4 * NQ])
        tok16 = small[0:H, 0:NQ]
        rowbuf = sb("rowbuf", [P, 2 * R])
        tokrow = rowbuf[0:1, :].rearrange("p (i r) -> p i r", i=2)
        maskb = rowbuf[:, 0:T].bitcast(BF16).rearrange("p (i t) -> p i t", i=2)
        ptok = small[0:1, 2 * NQ:4 * NQ]
        ptok16 = small[0:H, NQ:2 * NQ]
        ident = sb("ident", [P, P])
        dmean = sb("dmean", [P, P])
        selT = sb("selT", [P, 1], F16)
        one = sb("one", [1, 1])
        epsc = sb("epsc", [P, 1])
        mx3 = sb("mx3", [P, 2, 4])
        nmax = sb("nmax", [P, 2, 1])
        sum3 = sb("sum3", [P, 2, 4])
        rsum = sb("rsum", [P, 2, 2])
        stats = sb("stats", [TP, B, NT, 6])
        mu = sb("mu", [TP, B * NT])
        rstd = sb("rstd", [TP, B * NT])
        stt = sb("stt", [TP, 2, B * NT])
        mrb = sb("mrb", [TP, 2, NT])
        a_sc = sb("a_sc", [TP, D])
        a_of = sb("a_of", [TP, D])
        mask8 = sb("mask8", [P, T], U8)
        anym = sb("anym", [P, 4])
        tg = sb("tg", [P, 2])

        flat = qc[:, :, :].rearrange("p b n -> p (b n)")
        n0 = B * 2 * DC * APAD // 2
        qbd = flat[:, 0:n0].bitcast(F16).rearrange("p (b s c r) -> p b s c r", b=B, s=2, c=DC)
        keyT = flat[:, n0:n0 + 2 * DC * T].bitcast(F16).rearrange("p (i s c t) -> p i s c t", i=2, s=2, c=DC)
        aT = ctxT[:, 0, :, :, :]
        spare = ctxT[:, 1, :, :, :].rearrange("p s c t -> p (s c t)")
        wkv = spare[:, 0:4 * DC * D].rearrange("p (w s c e) -> p w s c e", w=2, s=2, c=DC)
        wqo = spare[:, 4 * DC * D:8 * DC * D].bitcast(F32).rearrange("p (w c e) -> p w c e", w=2, c=DC)
        attnT = small[:, 0:DC * NQ].rearrange("p (c n) -> p c n", c=DC)
        picked = small[:, DC * NQ:DC * NQ + AR].rearrange("p (h q) -> p h q", h=HA)
        qf = small[:, 3 * NQ:4 * NQ]
        qhl = std[:, :].bitcast(F16).rearrange("p (s n) -> p s n", s=2)
        hm = sb("hm", [P, HA])
        hms = sb("hms", [P, HA])

        S = [es.enter_context(nc.psum_tensor(f"S{i}", [P, 512], F32)) for i in range(NB)]
        TB = [es.enter_context(nc.psum_tensor(f"TB{i}", [P, 512], F32)) for i in range(2)]
        PV = [es.enter_context(nc.psum_tensor(f"PV{i}", [P, 512], F32)) for i in range(2)]
        M = es.enter_context(nc.psum_tensor("M", [P, 512], F32))
        QB = [S[0], S[1], PV[0], PV[1]]

        in_x = sem("in_x")
        in_aud = sem("in_aud")
        in_pack = sem("in_pack")
        passed = sem("passed")
        w_full = [sem(f"w_full{k}") for k in range(4)]
        stage_full = [sem(f"stage_full{k}") for k in range(4)]
        stage_free = sem("stage_free")
        mask_full = sem("mask_full")
        mask_ready = sem("mask_ready")
        const_ready = sem("const_ready")
        bkd_ready = sem("bkd_ready")
        bvd_ready = sem("bvd_ready")
        bvm_ready = sem("bvm_ready")
        mean_ready = sem("mean_ready")
        xc_ready = sem("xc_ready")
        sq_ready = sem("sq_ready")
        var_ready = sem("var_ready")
        std_ready = sem("std_ready")
        rs_ready = sem("rs_ready")
        xn_ready = sem("xn_ready")
        h_ready = sem("h_ready")
        x_ready = sem("x_ready")
        q_mm = sem("q_mm")
        q_evac = sem("q_evac")
        qp_mm = sem("qp_mm")
        qp_hi = sem("qp_hi")
        qp_lo = sem("qp_lo")
        tok_scores = sem("tok_scores")
        tok16_ready = sem("tok16_ready")
        tokrow_full = [sem(f"tokrow_full{k}") for k in range(2)]
        split_hi = sem("split_hi")
        norm_step = sem("norm_step")
        a_ready = sem("a_ready")
        m_mm = sem("m_mm")
        m_hi = sem("m_hi")
        m_lo = sem("m_lo")
        w_hi = sem("w_hi")
        w_lo = sem("w_lo")
        in_qo = sem("in_qo")
        aq_mm = sem("aq_mm")
        aq_f = sem("aq_f")
        aq_hi = sem("aq_hi")
        aq_lo = sem("aq_lo")
        qbd_half = sem("qbd_half")
        qbd_ready = sem("qbd_ready")
        picked_ready = sem("picked_ready")
        mask_sum = sem("mask_sum")
        mask_term = sem("mask_term")
        score_ready = sem("score_ready")
        max_part = sem("max_part")
        negmax_ready = sem("negmax_ready")
        exp_done = sem("exp_done")
        sum_ready = sem("sum_ready")
        rsum_ready = sem("rsum_ready")
        probs_ready = sem("probs_ready")
        turned = sem("turned")
        pt_hi = sem("pt_hi")
        pt_lo = sem("pt_lo")
        pv_done = sem("pv_done")
        avg_ready = sem("avg_ready")
        ptok_mm = sem("ptok_mm")
        ptok_evac = sem("ptok_evac")
        ptok_moved = sem("ptok_moved")
        stats_done = sem("stats_done")
        ln_step = sem("ln_step")
        ln_step2 = sem("ln_step2")
        rstd_ready = sem("rstd_ready")
        sd_ready = sem("sd_ready")
        any_step = sem("any_step")
        pool_step = sem("pool_step")
        ah_mm = sem("ah_mm")
        ah_evac = sem("ah_evac")
        wo_mm = sem("wo_mm")
        f1_mm = sem("f1_mm")
        f1_evac = sem("f1_evac")
        f2_mm = sem("f2_mm")
        tg_ready = sem("tg_ready")
        out_done = sem("out_done")

        def slot_uses(l, b, natural):
            return 2 * B * l + 2 * b + (2 if natural else 1) if l < 2 else 4 * B + b + 1

        chunks = []
        W_Q, W_O = [], []
        for l in range(2):
            W_Q.append(len(chunks))
            for n in range(2 * WCH):
                chunks.append(((wq, wk)[n % 2][l][n // 2], (qp_mm, DC * (H * l + HPC * (n // 2 + 1)))))
            W_O.append(len(chunks))
            for n in range(2 * WCH):
                chunks.append(((wv, wo)[n % 2][l][n // 2], (wo_mm, H * l + HPC * (n // 2 + 1))))
        W_KV = len(chunks)
        chunks += [(wk[2], (w_lo, 1)), (wv[2], (w_lo, 2))]
        W_M = len(chunks)
        chunks += [(w1[0], (f1_mm, 4)), (w1[1], (f1_mm, 8)), (w2[0], (f2_mm, 4)), (w2[1], (f2_mm, 8))]

        UB = [M, PV[1]]
        NFILL = PIECES * DC
        NKU = DC * NB
        NVU = NT // 2
        MU = NFILL + NKU + NVU
        UNITS = [[0, 1, 2], [3, 4, 5], [6, 7], [8, 9, 10], [11, 12, 13], [14, 15, 16], [17, 18, 19]]

        def unit_out(par, u, half):
            bank = UB[u % 2]
            if u < NFILL + NKU:
                n, m = divmod(u - NFILL, DC)
                return keyT[:, par, half, m, n * CW:(n + 1) * CW], bank[:, 0:CW]
            c = 2 * (u - NFILL - NKU)
            return nat[:, par, half, c:c + 2, :].rearrange("p j d -> p (j d)"), bank[0:TP, :]

        def col(name, c):
            a = PACK[name] + c
            return pk[:, a:a + 1]

        def apart(eng):
            eng.sem_inc(passed, 1)

        def batches(eng, body, tail=None):
            body(0, 0, True, False)
            with eng.Fori(1, B - 2, 2) as b:
                body(b, 1, False, False)
                body(b + 1, 0, False, False)
            body(B - 1, (B - 1) % 2, False, True)

        def pv_part(l, s):
            if s == 0:
                return (0, 2, 3, 1)
            if s <= 3 or (s == 4 and l < 2):
                return (1, s - 1, 4 if l < 2 else 3, 1)
            return (0, s - 5, 3, 0) if s > 4 else None

        def group(l, grp):
            if l < 2:
                return (slice(0, GROUP_A * P) if grp == 0 else slice(GROUP_A * P, R)), DC * NT * 3
            return slice(grp * AR, (grp + 1) * AR), NT * 3

        def pv_before(l, b):
            return 4 * (B * l + b) if l < 2 else 8 * B + 2 * b

        block = es.enter_context(nc.Block())

        @block.sync
        def _(sp):
            def weights(lo, hi):
                for n in range(lo, hi):
                    if n >= 4:
                        sp.wait_ge(*chunks[n - 4][1])
                    src = chunks[n][0]
                    sp.dma_start(wring[:, n % 4, 0:src.shape[1]], src).then_inc(w_full[n % 4], 16)

            def piece(l, b, k, natural):
                if l < 2:
                    n = 8 * (B * l + b) + (4 if natural else 0) + k
                    if l > 0 or natural or not isinstance(b, int) or b > 0:
                        sp.wait_ge(stage_free, n - 3)
                        apart(sp)
                    if l == 1 and not natural and (not isinstance(b, int) or b > 0):
                        sp.wait_ge(stats_done, 4 * b - 4 + k + 1)
                        apart(sp)
                else:
                    if isinstance(b, int) and b == 0:
                        sp.wait_ge(stage_free, 16 * B + k - 3)
                        sp.wait_ge(stats_done, 4 * (B - 1) + k + 1)
                    else:
                        sp.wait_ge(m_mm, MU * (b - 1) + DC * (k + 1))
                        apart(sp)
                bb = bass.ds(b, 1)
                if natural:
                    src = ctx_nat[bb, :, k * JP * D:(k + 1) * JP * D].rearrange("b p n -> (b p) n")
                    dst = stage[0:TP, k, :]
                else:
                    w = T * DC // PIECES
                    src = ctx_t[bb, :, k * w:(k + 1) * w].rearrange("b p n -> (b p) n")
                    dst = stageT[:, k, :]
                sp.dma_start(dst, src).then_inc(stage_full[k], 16)

            def pieces(l, b):
                for natural in ((False, True) if l < 2 else (True,)):
                    for k in range(PIECES):
                        piece(l, b, k, natural)

            def token_row(l, b, par):
                g = B * l + b
                if l > 0 or not isinstance(b, int) or b > 1:
                    sp.wait_ge(score_ready, 3 * RT * (g - 1))
                    apart(sp)
                if isinstance(b, int) and b == 0:
                    sp.wait_ge(tok16_ready, l + 1)
                    apart(sp)
                sp.dma_start(tokrow[0:1, par, :].rearrange("p (h q) -> p h q", h=H),
                             tok16[:, bass.ds(b * Q, Q)]).then_inc(tokrow_full[par], 16)

            def batch_loads(l, b, par):
                pieces(l, b)
                if l < 2:
                    token_row(l, b, par)
                else:
                    mask_load(b)

            def mask_load(b):
                if not isinstance(b, int) or b > 0:
                    sp.wait_ge(mask_ready, b)
                    apart(sp)
                sp.dma_start(mask8[:, :], mask[bass.ds(b, 1), :].broadcast_to([P, T])).then_inc(mask_full, 16)

            sp.dma_start(xT[:, :, :], x_t).then_inc(in_x, 16)
            sp.dma_start(pk[:, :], pack).then_inc(in_pack, 16)
            sp.dma_start(vr[:, :, :, :], vrows).then_inc(in_pack, 16)
            weights(0, 4)
            for k in range(PIECES):
                piece(0, 0, k, False)
            sp.dma_start(a_sc[:, :], a_scale.broadcast_to([TP, D])).then_inc(in_aud, 16)
            sp.dma_start(a_of[:, :], a_offset.broadcast_to([TP, D])).then_inc(in_aud, 16)
            sp.dma_start(tg[:, 0:1], gate.broadcast_to([P, 1])).then_inc(in_aud, 16)
            weights(4, 8)
            for k in range(PIECES):
                piece(0, 0, k, True)
            for l in range(L):
                if l < 2:
                    token_row(l, 0, 0)
                batch_loads(l, 1, 1)
                with sp.Fori(2, B - 1, 2) as b:
                    batch_loads(l, b, 0)
                    batch_loads(l, b + 1, 1)
                if l == 2:
                    break
                sp.wait_ge(pv_done, 4 * B * (l + 1))
                weights(W_O[l], W_O[l] + 4)
                for k in range(PIECES):
                    piece(l + 1, 0, k, l + 1 == 2)
                if l == 0:
                    weights(W_O[0] + 4, W_O[0] + 8)
                    for k in range(PIECES):
                        piece(1, 0, k, True)
                    weights(W_Q[1], W_Q[1] + 8)
                else:
                    mask_load(0)
                    for w in range(2):
                        sp.dma_start(wqo[:, w, :, :], (wq, wo)[w][2].rearrange("p (c e) -> p c e", c=DC))\
                            .then_inc(in_qo, 16)
                    weights(W_O[1] + 4, len(chunks))
            for c in range(DC):
                sp.wait_ge(x_ready, 3 * DC + c + 1)
                sp.dma_start(out[:, c, :], xT[:, c, :]).then_inc(out_done, 16)
            sp.wait_ge(out_done, 16 * DC)

        @block.gpsimd
        def _(pool):
            steps = [0]

            def link(ins):
                steps[0] += 1
                ins.then_inc(pool_step, 1)
                pool.wait_ge(pool_step, steps[0])

            nc.gpsimd.memset(one[:, :], 1.0)
            nc.gpsimd.memset(epsc[:, :], EPS)
            nc.gpsimd.memset(dmean[:, :], 1.0 / D)
            nc.gpsimd.memset(selT[:, :], 0.0)
            link(nc.gpsimd.memset(ident[:, :], 0.0))
            nc.gpsimd.affine_select(out=ident[:, :], in_=ident[:, :], compare_op=ALU.not_equal, fill=1.0, base=0,
                                    pattern=[[-1, P]], channel_multiplier=1)
            nc.gpsimd.affine_select(out=selT[:, :], in_=selT[:, :], compare_op=ALU.not_equal, fill=1.0, base=-TP,
                                    pattern=[[0, 1]], channel_multiplier=1).then_inc(const_ready, 1)
            pool.wait_ge(bkd_ready, 1)
            for l in range(2):
                src = bkd[:, l, :].unsqueeze(2).broadcast_to([P, H, H])
                nc.gpsimd.affine_select(out=bkm[:, l, :, :], in_=src, compare_op=ALU.is_equal, fill=0.0, base=0,
                                        pattern=[[1, H], [-1, H]], channel_multiplier=0).then_inc(const_ready, 1)

            def split(l, b, par, natural):
                g = B * l + b
                if l > 0 or not isinstance(b, int) or b >= 2:
                    if natural:
                        pool.wait_ge(pv_done, 4 * g - 4)
                    else:
                        pool.wait_ge(score_ready, 3 * RT * (g - 1))
                for k in range(PIECES):
                    pool.wait_ge(stage_full[k], 16 * slot_uses(l, b, natural))
                    apart(pool)
                    if natural:
                        src = stageN[:, k, :, :]
                        hi, lo = (nat[:, par, i, k * JP:(k + 1) * JP, :] for i in range(2))
                    else:
                        w = T * DC // PIECES
                        src = stageT[:, k, :]
                        hi, lo = (ctxT[:, par, i, k * w // T, (k * w) % T:(k * w) % T + w] for i in range(2))
                    nc.gpsimd.tensor_copy(hi, src).then_inc(split_hi, 1)
                    n = (8 * g + (4 if natural else 0) if l < 2 else 16 * B + 4 * b) + k + 1
                    pool.wait_ge(split_hi, n)
                    ins = nc.gpsimd.tensor_tensor(lo, src, hi, ALU.subtract)
                    ins.then_inc(stage_free, 1)

            link(nc.gpsimd.memset(hm[:, :], 1.0))
            link(nc.gpsimd.affine_select(out=hm[:, :], in_=hm[:, :], compare_op=ALU.is_ge, fill=0.0, base=0,
                                         pattern=[[-KA, HA]], channel_multiplier=1))
            link(nc.gpsimd.affine_select(out=hm[:, :], in_=hm[:, :], compare_op=ALU.is_ge, fill=0.0, base=KA - 1,
                                         pattern=[[KA, HA]], channel_multiplier=-1))
            nc.gpsimd.tensor_scalar(hms[:, :], hm[:, :], 1.0 / PROB_SCALE, None, ALU.mult).then_inc(const_ready, 1)

            def normalise(b):
                if isinstance(b, int) and b == 0:
                    pool.wait_ge(in_aud, 48)
                    pool.wait_ge(rstd_ready, 1)
                base = 9 * b
                for i, src in enumerate((mu, rstd)):
                    ins = nc.gpsimd.tensor_copy(mrb[:, i, :], src[:, bass.ds(b * NT, NT)])
                ins.then_inc(norm_step, 1)
                pool.wait_ge(norm_step, base + 1)
                for k in range(PIECES):
                    pool.wait_ge(stage_full[k], 16 * slot_uses(2, b, True))
                    apart(pool)
                    for j in range(JP):
                        c = k * JP + j
                        ins = nc.gpsimd.tensor_scalar(stageN[:, k, j, :], stageN[:, k, j, :], mrb[:, 0, c:c + 1],
                                                      mrb[:, 1, c:c + 1], ALU.subtract, ALU.mult)
                    ins.then_inc(norm_step, 1)
                    pool.wait_ge(norm_step, base + 2 + 2 * k)
                    bc = [v[:, :].unsqueeze(1).broadcast_to([TP, JP, D]) for v in (a_sc, a_of)]
                    nc.gpsimd.tensor_tensor(stageN[:, k, :, :], stageN[:, k, :, :], bc[0], ALU.mult)\
                        .then_inc(norm_step, 1)
                    pool.wait_ge(norm_step, base + 3 + 2 * k)
                    nc.gpsimd.tensor_tensor(stageN[:, k, :, :], stageN[:, k, :, :], bc[1], ALU.add)\
                        .then_inc(a_ready, 1)

            def prepare(l, b, par):
                if l < 2:
                    split(l, b, par, False)
                else:
                    normalise(b)
                    return
                split(l, b, par, True)

            for l in range(L):
                first = 0
                if l == 0:
                    prepare(0, 0, 0)
                    prepare(0, 1, 1)
                    first = 2
                if l == 2:
                    prepare(2, 0, 0)
                    prepare(2, 1, 1)
                    first = 2
                with pool.Fori(first, B - 1, 2) as b:
                    prepare(l, b, 0)
                    prepare(l, b + 1, 1)
                if l < 2:
                    pool.wait_ge(pv_done, 4 * B * (l + 1))
                    pool.wait_ge(bvd_ready, 1)
                    src = bvd[:, l, :].unsqueeze(1).broadcast_to([H, H, P])
                    nc.gpsimd.affine_select(out=bvm, in_=src, compare_op=ALU.is_equal, fill=0.0, base=0,
                                            pattern=[[-1, H], [0, P]], channel_multiplier=1).then_inc(bvm_ready, 1)

        @block.tensor
        def _(pe):
            def mm(o, a, c, start, stop, skip=False):
                return nc.tensor.matmul(o, a, c, start=start, stop=stop, skip_group_check=skip)

            def layer_norm(n, x_count):
                if n == 0:
                    pe.wait_ge(const_ready, 4)
                    pe.wait_ge(in_x, 16)
                else:
                    pe.wait_ge(x_ready, x_count)
                for c in range(DC):
                    ins = mm(S[2][:, 0:NQ], dmean[:, :], xT[:, c, :], c == 0, c == DC - 1)
                ins.then_inc(mean_ready, 1)
                pe.wait_ge(sq_ready, n + 1)
                for c in range(DC):
                    ins = mm(S[0][:, 0:NQ], dmean[:, :], sq[:, c, :], c == 0, c == DC - 1)
                ins.then_inc(var_ready, 1)

            def weights_in(n):
                pe.wait_ge(w_full[n % 4], 16 * (n // 4 + 1))
                return wring[:, n % 4, :]

            def query_projection(l):
                pe.wait_ge(h_ready, l + 1)

                def query(h):
                    w = weights_in(W_Q[l] + h // HPC * 2).rearrange("p (c n) -> p c n", c=DC)
                    if l > 0 or h >= 2:
                        pe.wait_ge(q_evac, H * l + h - 1)
                    j = h % HPC
                    for c in range(DC):
                        ins = mm(TB[h % 2][:, 0:NQ], w[:, c, j * KD:(j + 1) * KD], hT[:, c, :],
                                 c == 0, c == DC - 1)
                    ins.then_inc(q_mm, 1)

                def through_keys(h):
                    w = weights_in(W_Q[l] + h // HPC * 2 + 1).rearrange("p (j n) -> p j n", j=HPC)
                    pe.wait_ge(q_evac, H * l + h + 1)
                    q = hring[:, h % 4, :]
                    ins = mm(M[0:H, 0:NQ], bkm[:, l, h, :], q, h == 0, h == H - 1)
                    if h == H - 1:
                        ins.then_inc(tok_scores, 1)
                    for c in range(DC):
                        n = DC * (H * l + h) + c
                        if n >= 4:
                            pe.wait_ge(qp_lo, n - 3)
                        ins = mm(QB[n % 4][:, 0:NQ], w[:, h % HPC, c * P:(c + 1) * P], q, True, True)
                        ins.then_inc(qp_mm, 1)

                query(0)
                for h in range(H):
                    if h + 1 < H:
                        query(h + 1)
                    through_keys(h)

            def scores(l, b, s, par, first):
                g = B * l + b
                t = RT * g + s
                if first and s == 0:
                    if l < 2:
                        pe.wait_ge(qp_lo, DC * H * (l + 1))
                    else:
                        pe.wait_ge(qbd_ready, 1)
                if s == 0:
                    if l < 2:
                        pe.wait_ge(stage_free, 8 * g + 4)
                    else:
                        pe.wait_ge(m_lo, MU * b + NFILL + NKU)
                bb = bass.ds(b, 1)
                for c in range(NB):
                    if l < 2 and not (first and s == 0):
                        pe.wait_ge(exp_done, 3 * t + c - 2)
                    if l == 2 and not (first and s == 0):
                        pe.wait_ge(max_part, 3 * t + c - 2)
                    o = S[c][:, 0:CW]
                    ds = range(DC) if l < 2 or s == RT // 2 else (int(s > RT // 2),)
                    n = 0
                    for d in ds:
                        for qi, ci in ((0, 0), (0, 1), (1, 0)):
                            if l < 2:
                                q = qs16[:, bb, qi, d, s * P:(s + 1) * P]
                                k = ctxT[:, par, ci, d, c * CW:(c + 1) * CW]
                            else:
                                r0 = s * P - d * (R - APAD)
                                q = qbd[:, bb, qi, d, r0:r0 + P]
                                k = keyT[:, par, ci, d, c * CW:(c + 1) * CW]
                            ins = mm(o, q.rearrange("p b r -> p (b r)"), k, n == 0, n == 3 * len(ds) - 1)
                            n += 1
                    if l < 2 and c == NB - 1:
                        if s == 0:
                            pe.wait_ge(tokrow_full[par], 64 * l + 8 * (b - par) + 16)
                        ins = mm(S[c][:, CW:CW + 1], tokrow[0:1, par, s * P:(s + 1) * P], one[:, :],
                                 False, True, skip=True)
                    ins.then_inc(score_ready, 1)

            def turn(l, t, tpar, f, W):
                if f == 0:
                    pe.wait_ge(probs_ready, t + 1)
                n = 3 * t + f
                if not (isinstance(t, int) and n < 2):
                    pe.wait_ge(pt_lo, n - 1)
                bank = TB[(3 * tpar + f) % 2]
                for j in range(TPB):
                    c = f * TPB + j
                    ins = nc.tensor.transpose(bank[0:W, j * P:(j + 1) * P],
                                              prob[:, tpar % 2, c * TP:c * TP + W], ident[:, :])
                ins.then_inc(turned, 1)

            def average(l, b, par, grp, lo, hi):
                g = B * l + b
                rows, _ = group(l, grp)
                nrow = rows.stop - rows.start
                if lo == 0:
                    pe.wait_ge(pt_lo, 3 * (RT * g + (GROUP_A if grp == 0 else RT)))
                    if grp == 0:
                        if l < 2:
                            pe.wait_ge(stage_free, 8 * g + 8)
                        else:
                            pe.wait_ge(m_lo, MU * b + MU)
                for m in range(lo, hi):
                    d, r = divmod(m, 3 * NT)
                    j, i = divmod(r, 3)
                    pi, ci = ((0, 0), (1, 0), (0, 1))[i]
                    k = 2 * grp + d if l < 2 else grp
                    if r == 0:
                        if l == 2:
                            pe.wait_ge(avg_ready, pv_before(l, b) + k)
                        elif not (isinstance(g, int) and g == 0 and k < 2):
                            pe.wait_ge(avg_ready, pv_before(l, b) + k - 1)
                        if l < 2 and d == DC - 1:
                            if not (isinstance(g, int) and g == 0 and grp == 0):
                                pe.wait_ge(ptok_evac, 2 * g + grp)
                            for i2 in range(2):
                                ins = mm(M[0:1, 0:nrow], selT[0:TP + 1, :], probT[:, i2, NT - 1, rows],
                                         i2 == 0, i2 == 1)
                            ins.then_inc(ptok_mm, 1)
                    e = d if l < 2 else grp
                    ins = mm(PV[k % 2 if l < 2 else 0][:, 0:nrow], nat[:, par, ci, j, e * P:(e + 1) * P],
                             probT[0:TP, pi, j, rows], r == 0, r == 3 * NT - 1)
                    if r == 3 * NT - 1:
                        ins.then_inc(pv_done, 1)

            def unit(b, par, u):
                if not (isinstance(b, int) and b == 0 and u < 2):
                    pe.wait_ge(m_lo, MU * b + u - 1)
                o = UB[u % 2]
                if u < NFILL:
                    k, c = divmod(u, DC)
                    if c == 0:
                        pe.wait_ge(a_ready, 4 * b + k + 1)
                    for j in range(JP):
                        ins = nc.tensor.transpose(o[:, j * TP:(j + 1) * TP], stageN[:, k, j, c * P:(c + 1) * P],
                                                  ident[0:TP, 0:TP])
                elif u < NFILL + NKU:
                    n, m = divmod(u - NFILL, DC)
                    i = 0
                    for d in range(DC):
                        for wi, ai in ((0, 0), (0, 1), (1, 0)):
                            ins = mm(o[:, 0:CW], wkv[:, 0, wi, d, m * P:(m + 1) * P],
                                     aT[:, ai, d, n * CW:(n + 1) * CW], i == 0, i == 3 * DC - 1)
                            i += 1
                else:
                    for j in range(2):
                        c = 2 * (u - NFILL - NKU) + j
                        i = 0
                        for d in range(DC):
                            for wi, ai in ((0, 0), (1, 0), (0, 1)):
                                ins = mm(o[0:TP, j * D:(j + 1) * D], aT[:, ai, d, c * TP:(c + 1) * TP],
                                         wkv[:, 1, wi, d, :], i == 0, i == 3 * DC - 1)
                                i += 1
                ins.then_inc(m_mm, 1)

            def attention(l):
                W = TP + 1 if l < 2 else TP

                def body(b, par, first, last):
                    t0 = RT * (B * l + b)
                    for s in range(RT):
                        scores(l, b, s, par, first)
                        prev = s > 0 or not first
                        if prev:
                            tp = RT * par + s - 1 if s > 0 else RT * (1 - par) + RT - 1
                            turn(l, t0 + s - 1, tp, 0, W)
                            turn(l, t0 + s - 1, tp, 1, W)
                        units = UNITS[s] if l == 2 and not last else []
                        for u in units[0:2]:
                            unit(b + 1, 1 - par, u)
                        work = pv_part(l, s)
                        if work is not None:
                            grp, part, parts, back = work
                            n = group(l, grp)[1]
                            lo, hi = part * n // parts, (part + 1) * n // parts
                            mid = lo + (hi - lo) * 2 // 3
                        if work is None or (first and back):
                            lo = mid = hi = 0
                        if hi:
                            average(l, b - back, (par + back) % 2, grp, lo, mid)
                        if prev:
                            turn(l, t0 + s - 1, tp, 2, W)
                        if hi:
                            average(l, b - back, (par + back) % 2, grp, mid, hi)
                        for u in units[2:3]:
                            unit(b + 1, 1 - par, u)
                    if last:
                        t = t0 + RT - 1
                        n = group(l, 0)[1]
                        average(l, b, par, 0, 2 * n // 3, n)
                        for f in range(3):
                            turn(l, t, RT * par + RT - 1, f, W)
                        average(l, b, par, 1, 0, group(l, 1)[1])

                batches(pe, body)

            def output_projection(l):
                pe.wait_ge(avg_ready, 4 * B * (l + 1))

                def head(h):
                    w = weights_in(W_O[l] + h // HPC * 2).rearrange("p (c n) -> p c n", c=DC)
                    n = H * l + h
                    if n >= 2:
                        pe.wait_ge(ah_evac, n - 1)
                    j = h % HPC
                    o = TB[h % 2][:, 0:NQ]
                    for c in range(DC):
                        mm(o, w[:, c, j * KD:(j + 1) * KD], avg[:, :, c, h * Q:(h + 1) * Q], c == 0, False)
                    if h == 0:
                        pe.wait_ge(bvm_ready, l + 1)
                        pe.wait_ge(ptok_moved, 16 * B * (l + 1))
                    mm(o, bvm[:, h, :], ptok16, False, True).then_inc(ah_mm, 1)

                def out(h):
                    w = weights_in(W_O[l] + h // HPC * 2 + 1).rearrange("p (j n) -> p j n", j=HPC)
                    pe.wait_ge(ah_evac, H * l + h + 1)
                    for c in range(DC):
                        ins = mm(PV[c][:, 0:NQ], w[:, h % HPC, c * P:(c + 1) * P], hring[:, h % 4, :],
                                 h == 0, h == H - 1)
                    ins.then_inc(wo_mm, 1)

                head(0)
                for h in range(H):
                    if h + 1 < H:
                        head(h + 1)
                    out(h)

            def mlp():
                pe.wait_ge(h_ready, 3)
                pe.wait_ge(m_lo, MU)
                for f in range(FC):
                    w = weights_in(W_M + f // 4).rearrange("p (c n) -> p c n", c=DC)
                    if f >= 2:
                        pe.wait_ge(f1_evac, f - 1)
                    j = f % 4
                    for c in range(DC):
                        ins = mm(TB[f % 2][:, 0:NQ], w[:, c, j * P:(j + 1) * P], hT[:, c, :], c == 0, c == DC - 1)
                    ins.then_inc(f1_mm, 1)
                for f in range(FC):
                    w = weights_in(W_M + 2 + f // 4).rearrange("p (j n) -> p j n", j=4)
                    pe.wait_ge(f1_evac, f + 1)
                    for c in range(DC):
                        ins = mm(PV[c][:, 0:NQ], w[:, f % 4, c * P:(c + 1) * P], hid[:, f, :], f == 0, f == FC - 1)
                    ins.then_inc(f2_mm, 1)

            layer_norm(0, 0)
            query_projection(0)
            attention(0)
            output_projection(0)
            layer_norm(1, DC)
            query_projection(1)
            attention(1)
            output_projection(1)
            pe.wait_ge(w_lo, 2)
            pe.wait_ge(x_ready, 2 * DC)
            for u in range(MU // 2):
                unit(0, 0, u)
            layer_norm(2, 2 * DC)
            for u in range(MU // 2, MU):
                unit(0, 0, u)
            mlp()
            pe.wait_ge(x_ready, 3 * DC)
            pe.wait_ge(in_qo, 32)
            for m in range(DC):
                for c in range(DC):
                    ins = mm(TB[m][:, 0:NQ], wqo[:, 0, c, m * P:(m + 1) * P], xT[:, c, :], c == 0, c == DC - 1)
                ins.then_inc(aq_mm, 1)
            attention(2)
            pe.wait_ge(avg_ready, 8 * B + 2 * B)
            for m in range(DC):
                for c in range(DC):
                    ins = mm(PV[m][:, 0:NQ], wqo[:, 1, c, m * P:(m + 1) * P], attnT[:, c, :], c == 0, c == DC - 1)
                ins.then_inc(wo_mm, 1)

        @block.scalar
        def _(act):
            def layer_norm(n):
                act.wait_ge(var_ready, n + 1)
                if n == 0:
                    act.wait_ge(const_ready, 4)
                nc.scalar.activation(std[:, :], S[0][:, 0:NQ], ACT.Sqrt, bias=epsc[:, :]).then_inc(std_ready, 1)
                act.wait_ge(xn_ready, n + 1)
                for c in range(DC):
                    ins = nc.scalar.activation(hT[:, c, :], xc[:, c, :], ACT.Identity,
                                               scale=col(f"ln_scale{n}", c), bias=col(f"ln_offset{n}", c))
                ins.then_inc(h_ready, 1)

            def query_projection(l):
                for h in range(H + 1):
                    if h < H:
                        act.wait_ge(q_mm, H * l + h + 1)
                        if h >= 4:
                            act.wait_ge(qp_mm, DC * (H * l + h - 3))
                        nc.scalar.activation(hring[:, h % 4, :], TB[h % 2][:, 0:NQ], ACT.Identity,
                                             bias=col(("bq", l), h)).then_inc(q_evac, 1)
                    if h > 0:
                        for c in range(DC):
                            n = DC * (H * l + h - 1) + c
                            act.wait_ge(qp_mm, n + 1)
                            o = qs16[:, :, 0, c, (h - 1) * Q:h * Q]
                            nc.scalar.activation(o, QB[n % 4][:, 0:NQ].rearrange("p (b q) -> p b q", b=B),
                                                 ACT.Copy, scale=KD ** -0.5).then_inc(qp_hi, 1)
                act.wait_ge(tok_scores, l + 1)
                nc.scalar.activation(tok16, M[0:H, 0:NQ], ACT.Copy, scale=KD ** -0.5).then_inc(tok16_ready, 1)

            def exponentiate(l, t, tp, c, first):
                i = tp % 2
                w = CW + 1 if l < 2 and c == NB - 1 else CW
                if c == 0:
                    act.wait_ge(negmax_ready, t + 1)
                    if l < 2 and not first:
                        act.wait_ge(turned, 3 * t - 3)
                o = prob[:, i, c * CW:c * CW + w]
                src = S[c][:, 0:w] if l < 2 else o
                nc.scalar.activation(o, src, ACT.Exp, bias=nmax[:, i, :],
                                     accum_out=sum3[:, i, c:c + 1]).then_inc(exp_done, 1)

            def high_half(l, g, t, tp, s, f, W, fresh):
                act.wait_ge(turned, 3 * t + f + 1)
                if l < 2 and f == 0 and not fresh and s in (0, GROUP_A):
                    act.wait_ge(pv_done, 4 * g - 4 + (2 if s < GROUP_A else 4))
                if l == 2 and f == 0 and not fresh and s in (0, RT // 2):
                    act.wait_ge(pv_done, 2 * g + 4 * B - 2 + (1 if s == 0 else 2))
                o = probT[0:W, 0, f * TPB:(f + 1) * TPB, s * P:(s + 1) * P]
                src = TB[(3 * tp + f) % 2][0:W, :].rearrange("p (j r) -> p j r", j=TPB)
                nc.scalar.activation(o, src, ACT.Copy).then_inc(pt_hi, 1)

            def store_average(l, b, k):
                g = B * l + b
                grp, d = divmod(k, 2)
                act.wait_ge(pv_done, 4 * g + k + 1)
                r0, r1 = (0, GROUP_A * P) if grp == 0 else (GROUP_A * P, R)
                o = avg[:, bass.ds(b, 1), d, r0:r1].rearrange("p b r -> p (b r)")
                nc.scalar.activation(o, PV[k % 2][:, 0:r1 - r0], ACT.Copy, scale=1.0 / PROB_SCALE)\
                    .then_inc(avg_ready, 1)

            def store_token(l, b, grp):
                g = B * l + b
                act.wait_ge(ptok_mm, 2 * g + grp + 1)
                if grp == 0 and not (isinstance(g, int) and g == 0):
                    act.wait_ge(ptok_moved, 16 * g)
                r0, r1 = (0, GROUP_A * P) if grp == 0 else (GROUP_A * P, R)
                nc.scalar.activation(ptok[:, r0:r1], M[0:1, 0:r1 - r0], ACT.Copy, scale=1.0 / PROB_SCALE)\
                    .then_inc(ptok_evac, 1)
                if grp == 1:
                    act.wait_ge(ptok_evac, 2 * g + 2)
                    act.dma_start(ptok16[:, bass.ds(b * Q, Q)],
                                  ptok[0:1, :].rearrange("p (h q) -> p h q", h=H)).then_inc(ptok_moved, 16)

            def unit_high(b, par, u):
                act.wait_ge(m_mm, MU * b + u + 1)
                if u < NFILL:
                    k, c = divmod(u, DC)
                    o, src, scale = aT[:, 0, c, k * JP * TP:(k + 1) * JP * TP], UB[u % 2][:, 0:JP * TP], 1.0
                else:
                    o, src = unit_out(par, u, 0)
                    scale = 1.0 / W_SCALE
                nc.scalar.activation(o, src, ACT.Copy, scale=scale).then_inc(m_hi, 1)

            def mask_row(b, par):
                act.wait_ge(mask_full, 16 * b + 16)
                nc.scalar.activation(maskb[:, par, :], mask8[:, :], ACT.Copy, accum_out=anym[:, 0:1])\
                    .then_inc(mask_sum, 1)
                act.wait_ge(mask_term, 4 * b + 4)
                nc.scalar.activation(maskb[:, par, :], mask8[:, :], ACT.Identity, scale=MASKED,
                                     bias=anym[:, 3:4]).then_inc(mask_ready, 1)

            def attention(l):
                W = TP + 1 if l < 2 else TP

                def body(b, par, first, last):
                    t0 = RT * (B * l + b)
                    for s in range(RT):
                        prev = s > 0 or not first
                        tp = RT * par + s - 1 if s > 0 else RT * (1 - par) + RT - 1
                        ps = (s - 1) % RT
                        units = UNITS[s] if l == 2 and not last else []
                        start = first and l == 0
                        for f in range(NB):
                            if prev and f < 2:
                                high_half(l, B * l + b - (s == 0), t0 + s - 1, tp, ps, f, W, start or
                                          (l == 2 and first))
                            for u in units[f - 1:f] if f else []:
                                unit_high(b + 1, 1 - par, u)
                            exponentiate(l, t0 + s, RT * par + s, f, start and s < 2)
                        if prev:
                            high_half(l, B * l + b - (s == 0), t0 + s - 1, tp, ps, 2, W, start or
                                      (l == 2 and first))
                        if l == 2:
                            if s == 5 and not last:
                                mask_row(b + 1, 1 - par)
                            for u in units[2:3]:
                                unit_high(b + 1, 1 - par, u)
                            continue
                        if s == 0 and not first:
                            if l < 2:
                                store_token(l, b - 1, 0)
                            store_average(l, b - 1, 1)
                        if s == 2 and not first:
                            store_average(l, b - 1, 2)
                        if s == 3 and not first and l < 2:
                            store_token(l, b - 1, 1)
                        if s == 4 and not first:
                            store_average(l, b - 1, 3)
                        if s == 6:
                            store_average(l, b, 0)
                    if last:
                        if l < 2:
                            store_token(l, b, 0)
                            store_average(l, b, 1)
                        for f in range(3):
                            high_half(l, B * l + b, t0 + RT - 1, RT * par + RT - 1, RT - 1, f, W, False)
                        if l < 2:
                            store_average(l, b, 2)
                            store_token(l, b, 1)
                            store_average(l, b, 3)

                batches(act, body)

            def output_projection(l):
                for h in range(H):
                    act.wait_ge(ah_mm, H * l + h + 1)
                    if h >= 4:
                        act.wait_ge(wo_mm, H * l + h - 3)
                    nc.scalar.activation(hring[:, h % 4, :], TB[h % 2][:, 0:NQ], ACT.Identity,
                                         bias=col(("bv", l), h)).then_inc(ah_evac, 1)

            act.wait_ge(in_pack, 32)
            layer_norm(0)
            query_projection(0)
            attention(0)
            output_projection(0)
            layer_norm(1)
            query_projection(1)
            attention(1)
            act.wait_ge(ln_step, 5)
            nc.scalar.activation(rstd[:, :], stt[:, 0, :], ACT.Sqrt, bias=epsc[0:TP, :]).then_inc(sd_ready, 1)
            output_projection(1)
            for w in range(2):
                n = W_KV + w
                act.wait_ge(w_full[n % 4], 16 * (n // 4 + 1))
                nc.scalar.activation(wkv[:, w, 0, :, :], wring[:, n % 4, 0:DC * D].rearrange("p (c e) -> p c e", c=DC),
                                     ACT.Copy, scale=W_SCALE).then_inc(w_hi, 1)
            for u in range(MU // 2):
                unit_high(0, 0, u)
            layer_norm(2)
            for u in range(MU // 2, MU):
                unit_high(0, 0, u)
            mask_row(0, 0)
            for f in range(FC):
                act.wait_ge(f1_mm, f + 1)
                nc.scalar.activation(hid[:, f, :], TB[f % 2][:, 0:NQ], ACT.Gelu, bias=col("b_fc1", f))\
                    .then_inc(f1_evac, 1)
            act.wait_ge(in_aud, 48)
            nc.scalar.activation(tg[:, 1:2], tg[:, 0:1], ACT.Tanh).then_inc(tg_ready, 1)
            for m in range(DC):
                act.wait_ge(aq_mm, m + 1)
                if m > 0:
                    act.wait_ge(qbd_half, 1)
                nc.scalar.activation(qf, TB[m][:, 0:NQ], ACT.Copy, scale=KA ** -0.5).then_inc(aq_f, 1)
                act.wait_ge(aq_f, m + 1)
                nc.scalar.activation(qhl[:, 0, :], qf, ACT.Copy).then_inc(aq_hi, 1)
            attention(2)

        @block.vector
        def _(dve):
            def layer_norm(n):
                dve.wait_ge(mean_ready, n + 1)
                for c in range(DC):
                    ins = nc.vector.tensor_tensor(xc[:, c, :], xT[:, c, :], S[2][:, 0:NQ], ALU.subtract)
                ins.then_inc(xc_ready, 1)
                dve.wait_ge(xc_ready, n + 1)
                nc.vector.tensor_tensor(sq, xc, xc, ALU.mult).then_inc(sq_ready, 1)
                dve.wait_ge(std_ready, n + 1)
                nc.vector.reciprocal(std[:, :], std[:, :]).then_inc(rs_ready, 1)
                dve.wait_ge(rs_ready, n + 1)
                for c in range(DC):
                    ins = nc.vector.tensor_tensor(xc[:, c, :], xc[:, c, :], std[:, :], ALU.mult)
                ins.then_inc(xn_ready, 1)

            def query_projection(l):
                for h in range(H):
                    for c in range(DC):
                        n = DC * (H * l + h) + c
                        dve.wait_ge(qp_hi, n + 1)
                        hi, lo = (qs16[:, :, i, c, h * Q:(h + 1) * Q] for i in range(2))
                        nc.vector.scalar_tensor_tensor(
                            lo, QB[n % 4][:, 0:NQ].rearrange("p (b q) -> p b q", b=B), KD ** -0.5, hi,
                            ALU.mult, ALU.subtract).then_inc(qp_lo, 1)

            def maxima(l, t, tp, c, par):
                i = tp % 2
                w = CW + 1 if l < 2 and c == NB - 1 else CW
                dve.wait_ge(score_ready, 3 * t + c + 1)
                if l < 2:
                    nc.vector.tensor_reduce(mx3[:, i, c:c + 1], S[c][:, 0:w], AX_X, ALU.max).then_inc(max_part, 1)
                else:
                    if c == 0:
                        dve.wait_ge(turned, 3 * t - 3)
                    apart(dve)
                    nc.vector.tensor_tensor_reduce(
                        out=prob[:, i, c * CW:(c + 1) * CW], in0=S[c][:, 0:CW],
                        in1=maskb[:, par, c * CW:(c + 1) * CW], scale=1.0, scalar=-3.0e38,
                        op0=ALU.add, op1=ALU.max, accum_out=mx3[:, i, c:c + 1]).then_inc(max_part, 1)

            def row_maximum(l, t, tp):
                i = tp % 2
                dve.wait_ge(max_part, 3 * t + 3)
                nc.vector.tensor_reduce(nmax[:, i, :], mx3[:, i, 0:NB], AX_X, ALU.max, negate=True)\
                    .then_inc(negmax_ready, 1)

            def normalise(l, t, tp):
                i = tp % 2
                w = T + 1 if l < 2 else T
                dve.wait_ge(exp_done, 3 * t + 3)
                nc.vector.tensor_reduce(rsum[:, i, 0:1], sum3[:, i, 0:NB], AX_X, ALU.add).then_inc(sum_ready, 1)
                dve.wait_ge(sum_ready, t + 1)
                nc.vector.reciprocal(rsum[:, i, 1:2], rsum[:, i, 0:1]).then_inc(rsum_ready, 1)
                dve.wait_ge(rsum_ready, t + 1)
                nc.vector.tensor_scalar(prob[:, i, 0:w], prob[:, i, 0:w], rsum[:, i, 1:2], PROB_SCALE,
                                        ALU.mult, ALU.mult).then_inc(probs_ready, 1)

            def low_half(t, tp, s, f, W):
                dve.wait_ge(pt_hi, 3 * t + f + 1)
                hi, lo = (probT[0:W, i, f * TPB:(f + 1) * TPB, s * P:(s + 1) * P] for i in range(2))
                src = TB[(3 * tp + f) % 2][0:W, :].rearrange("p (j r) -> p j r", j=TPB)
                nc.vector.tensor_tensor(lo, src, hi, ALU.subtract).then_inc(pt_lo, 1)

            def unit_low(b, par, u):
                dve.wait_ge(m_hi, MU * b + u + 1)
                if u < NFILL:
                    k, c = divmod(u, DC)
                    hi, lo = (aT[:, i, c, k * JP * TP:(k + 1) * JP * TP] for i in range(2))
                    nc.vector.tensor_tensor(lo, UB[u % 2][:, 0:JP * TP], hi, ALU.subtract).then_inc(m_lo, 1)
                else:
                    hi, src = unit_out(par, u, 0)
                    lo, _ = unit_out(par, u, 1)
                    nc.vector.scalar_tensor_tensor(lo, src, 1.0 / W_SCALE, hi, ALU.mult, ALU.subtract)\
                        .then_inc(m_lo, 1)

            def pick_average(b, grp):
                n = 2 * b + grp + 1
                dve.wait_ge(pv_done, 8 * B + n)
                if not isinstance(b, int) or n > 1:
                    dve.wait_ge(avg_ready, 8 * B + n - 1)
                nc.vector.tensor_tensor(picked, PV[0][:, 0:AR].rearrange("p (h q) -> p h q", h=HA),
                                        hms[:, :].unsqueeze(2).broadcast_to([P, HA, Q]), ALU.mult)\
                    .then_inc(picked_ready, 1)
                dve.wait_ge(picked_ready, n)
                nc.vector.tensor_reduce(attnT[:, grp, bass.ds(b * Q, Q)], picked.rearrange("p h q -> p q h"),
                                        AX_X, ALU.add).then_inc(avg_ready, 1)

            def context_stats(b, k):
                dve.wait_ge(stage_full[k], 16 * slot_uses(1, b, True))
                for j in range(JP):
                    o = stats[:, bass.ds(b, 1), k * JP + j, :].rearrange("p b n -> p (b n)")
                    ins = nc.vector.bn_stats(o, stageN[:, k, j, :])
                ins.then_inc(stats_done, 1)

            def mask_term_of(b):
                dve.wait_ge(mask_sum, b + 1)
                base = 4 * b
                nc.vector.tensor_scalar(anym[:, 1:2], anym[:, 0:1], 1.0, 1.0, ALU.min, ALU.subtract)\
                    .then_inc(mask_term, 1)
                dve.wait_ge(mask_term, base + 1)
                nc.vector.tensor_scalar(anym[:, 2:3], anym[:, 1:2], 3.0e38, 4.0, ALU.mult, ALU.mult)\
                    .then_inc(mask_term, 1)
                dve.wait_ge(mask_term, base + 2)
                nc.vector.tensor_scalar(anym[:, 1:2], anym[:, 2:3], 0.0, -MASKED, ALU.mult, ALU.add)\
                    .then_inc(mask_term, 1)
                dve.wait_ge(mask_term, base + 3)
                nc.vector.tensor_copy(anym[:, 3:4], anym[:, 1:2]).then_inc(mask_term, 1)

            def attention(l):
                W = TP + 1 if l < 2 else TP

                def body(b, par, first, last):
                    t0 = RT * (B * l + b)
                    for s in range(RT):
                        prev = s > 0 or not first
                        tp = RT * par + s - 1 if s > 0 else RT * (1 - par) + RT - 1
                        units = UNITS[s] if l == 2 and not last else []
                        if l == 2 and s == 0:
                            dve.wait_ge(mask_ready, b + 1)
                        for c in range(NB):
                            maxima(l, t0 + s, RT * par + s, c, par)
                        row_maximum(l, t0 + s, RT * par + s)
                        if prev:
                            low_half(t0 + s - 1, tp, (s - 1) % RT, 0, W)
                            low_half(t0 + s - 1, tp, (s - 1) % RT, 1, W)
                        for u in units[0:2]:
                            unit_low(b + 1, 1 - par, u)
                        normalise(l, t0 + s, RT * par + s)
                        if prev:
                            low_half(t0 + s - 1, tp, (s - 1) % RT, 2, W)
                        if l == 2 and not last and s == 5:
                            mask_term_of(b + 1)
                        for u in units[2:3]:
                            unit_low(b + 1, 1 - par, u)
                        if l == 2 and not first and s == 0:
                            pick_average(b - 1, 0)
                        if l == 2 and not first and s == 3:
                            pick_average(b - 1, 1)
                        if l == 1 and not last and 2 <= s < 6:
                            context_stats(b + 1, s - 2)
                    if last:
                        for f in range(3):
                            low_half(t0 + RT - 1, RT * par + RT - 1, RT - 1, f, W)
                        if l == 2:
                            pick_average(b, 0)
                            pick_average(b, 1)

                batches(dve, body)

            def add_output(l):
                if l < 2:
                    dve.wait_ge(wo_mm, H * (l + 1))
                else:
                    dve.wait_ge(tg_ready, 1)
                for c in range(DC):
                    sc = col(f"bo{l}", c) if l < 2 else tg[:, 1:2]
                    if l == 2:
                        dve.wait_ge(wo_mm, 2 * H + c + 1)
                    nc.vector.scalar_tensor_tensor(xT[:, c, :], PV[c][:, 0:NQ], sc, xT[:, c, :],
                                                   ALU.add if l < 2 else ALU.mult, ALU.add).then_inc(x_ready, 1)

            dve.wait_ge(in_pack, 32)
            for l in range(2):
                a, c = PACK["bias_k", l], PACK["bk", l]
                ins = nc.vector.tensor_tensor(bkd[:, l, :], pk[:, a:a + H], pk[:, c:c + H], ALU.subtract)
            ins.then_inc(bkd_ready, 1)
            nc.vector.tensor_tensor(bvd[:, :, :], vr[:, :, 0, :], vr[:, :, 1, :], ALU.subtract).then_inc(bvd_ready, 1)
            layer_norm(0)
            query_projection(0)
            attention(0)
            add_output(0)
            layer_norm(1)
            query_projection(1)
            for k in range(PIECES):
                context_stats(0, k)
            attention(1)

            def ln_link(ins, n):
                ins.then_inc(ln_step, 1)
                dve.wait_ge(ln_step, n)
            dve.wait_ge(stats_done, 4 * B)
            st = stats[:, :, :, :].rearrange("p b j n -> p (b j) n")
            ln_link(nc.vector.tensor_tensor(mu[:, :], st[:, :, 1], st[:, :, 4], ALU.add), 1)
            ln_link(nc.vector.tensor_tensor(stt[:, 1, :], st[:, :, 1], st[:, :, 4], ALU.subtract), 2)
            ln_link(nc.vector.tensor_tensor(stt[:, 0, :], st[:, :, 2], st[:, :, 5], ALU.add), 3)
            ln_link(nc.vector.scalar_tensor_tensor(stt[:, 1, :], stt[:, 1, :], D / 4.0, stt[:, 1, :],
                                                   ALU.mult, ALU.mult), 4)
            nc.vector.tensor_scalar(mu[:, :], mu[:, :], 0.5, None, ALU.mult)
            nc.vector.tensor_tensor(stt[:, 0, :], stt[:, 0, :], stt[:, 1, :], ALU.add).then_inc(ln_step2, 1)
            dve.wait_ge(ln_step2, 1)
            ln_link(nc.vector.tensor_scalar(stt[:, 0, :], stt[:, 0, :], 1.0 / D, None, ALU.mult), 5)
            dve.wait_ge(sd_ready, 1)
            nc.vector.reciprocal(rstd[:, :], rstd[:, :]).then_inc(rstd_ready, 1)

            add_output(1)
            for w in range(2):
                n = W_KV + w
                dve.wait_ge(w_hi, w + 1)
                nc.vector.scalar_tensor_tensor(wkv[:, w, 1, :, :].rearrange("p c e -> p (c e)"),
                                               wring[:, n % 4, 0:DC * D], W_SCALE,
                                               wkv[:, w, 0, :, :].rearrange("p c e -> p (c e)"),
                                               ALU.mult, ALU.subtract).then_inc(w_lo, 1)
            for u in range(MU // 2):
                unit_low(0, 0, u)
            layer_norm(2)
            for u in range(MU // 2, MU):
                unit_low(0, 0, u)
            mask_term_of(0)
            nc.vector.memset(qbd[:, :, :, 0, AR:APAD], 0.0)
            nc.vector.memset(qbd[:, :, :, 1, 0:APAD - AR], 0.0)
            dve.wait_ge(f2_mm, FC)
            for c in range(DC):
                nc.vector.scalar_tensor_tensor(xT[:, c, :], PV[c][:, 0:NQ], col("b_fc2", c), xT[:, c, :],
                                               ALU.add, ALU.add).then_inc(x_ready, 1)
            for m in range(DC):
                dve.wait_ge(aq_hi, m + 1)
                nc.vector.tensor_tensor(qhl[:, 1, :], qf, qhl[:, 0, :], ALU.subtract).then_inc(aq_lo, 1)
                dve.wait_ge(aq_lo, m + 1)
                for i in range(2):
                    for j in range(HA):
                        r0 = j * Q + m * (APAD - AR)
                        ins = nc.vector.tensor_scalar(qbd[:, :, i, m, r0:r0 + Q],
                                                      qhl[:, i, :].rearrange("p (b q) -> p b q", b=B),
                                                      hm[:, j:j + 1], None, ALU.mult)
                ins.then_inc((qbd_half, qbd_ready)[m], 1)
            attention(2)
            add_output(2)


_L0 = "L0_xattn_"
_L1 = "L1_xattn_"


def kernel(**inputs):
    import numpy as np
    import concourse.bacc as bacc
    from concourse.bass_utils import run_bass_kernel_spmd

    a = {k: np.asarray(v) for k, v in inputs.items()}
    by_partition = lambda v: v.reshape(-1, P).T

    cols = []
    for l in ("1", "2"):
        cols += [by_partition(a[_L0 + n + l].reshape(-1)) for n in ("bq", "bk", "bv", "bias_k")]
    for n in ("ln1_scale", "ln1_offset", "ln2_scale", "ln2_offset", "ln_mlp_scale", "ln_mlp_offset", "bo1", "bo2",
              "b_fc2", "b_fc1"):
        cols.append(by_partition(a[_L0 + n]))

    def by_model_rows(w):
        return w.reshape(DC, P, WCH, -1).transpose(2, 1, 0, 3).reshape(WCH, P, -1)

    def by_head_rows(w):
        return w.reshape(WCH, HPC, -1, D).transpose(0, 2, 1, 3).reshape(WCH, w.shape[0] // H, -1)

    def audio(w):
        return w.T.reshape(DC, P, D).transpose(1, 0, 2).reshape(P, DC * D)

    ctx = a["ctx_2048"]
    arrays = {
        "x_t": a["x"].reshape(NQ, DC, P).transpose(2, 1, 0),
        "ctx_nat": ctx.reshape(B, TP, NT * D),
        "ctx_t": ctx.reshape(B, TP, NT, DC, P).transpose(0, 4, 3, 2, 1).reshape(B, P, DC * T),
        "mask": a["mask_BxS2_bf1"].reshape(B, TP, NT).transpose(0, 2, 1).reshape(B, T).view(np.uint8),
        "pack": np.concatenate(cols, axis=1),
        "vrows": np.stack([np.stack([a[_L0 + n + l].reshape(H, P) for n in ("bias_v", "bv")], axis=1)
                           for l in ("1", "2")], axis=1),
        "a_scale": a[_L1 + "ln_gamma"].reshape(1, D),
        "a_offset": a[_L1 + "ln_beta"].reshape(1, D),
        "gate": a[_L1 + "gate"].reshape(1, 1),
        "wq0": by_model_rows(a[_L0 + "wq1"]), "wq1": by_model_rows(a[_L0 + "wq2"]),
        "wq2": audio(a[_L1 + "Wq"]), "wk2": audio(a[_L1 + "Wk"]), "wv2": audio(a[_L1 + "Wv"]),
        "wo2": audio(a[_L1 + "Wo"]),
        "wk0": by_head_rows(a[_L0 + "wk1"].T), "wk1": by_head_rows(a[_L0 + "wk2"].T),
        "wv0": by_model_rows(a[_L0 + "wv1"]), "wv1": by_model_rows(a[_L0 + "wv2"]),
        "wo0": by_head_rows(a[_L0 + "wo1"]), "wo1": by_head_rows(a[_L0 + "wo2"]),
        "w1": a[_L0 + "w_fc1"].reshape(DC, P, 2, F // 2).transpose(2, 1, 0, 3).reshape(2, P, -1),
        "w2": a[_L0 + "w_fc2"].reshape(2, FC // 2, P, D).transpose(0, 2, 1, 3).reshape(2, P, -1),
    }
    nc = bacc.Bacc("TRN2", target_bir_lowering=False, num_devices=1)
    args, feed = {}, {}
    for name, v in arrays.items():
        v = np.ascontiguousarray(v)
        feed[f"in_{name}_dram"] = v
        args[name] = nc.dram_tensor(f"in_{name}_dram", v.shape, mybir.dt.from_np(v.dtype), kind="ExternalInput").ap()
    out = nc.dram_tensor("out_0_dram", (P, DC, NQ), F32, kind="ExternalOutput").ap()
    by_layer = {n: [args.pop(f"{n}{l}") for l in range(L)] for n in ("wq", "wk", "wv", "wo")}
    build(nc, **args, **by_layer, out=out)
    r = run_bass_kernel_spmd(nc, [feed], core_ids=[0])
    got = r.results[0]["out_0_dram"]
    return np.ascontiguousarray(got.transpose(2, 1, 0).reshape(B, Q, D))
```

```python
from contextlib import ExitStack

import concourse.bass as bass
from concourse import mybir

ALU = mybir.AluOpType
ACT = mybir.ActivationFunctionType
F32 = mybir.dt.float32
F16 = mybir.dt.float16
BF16 = mybir.dt.bfloat16
U8 = mybir.dt.uint8
AX_X = mybir.AxisListType.X

B, Q, D, T, H, F = 8, 56, 256, 1500, 16, 1024
P = 128
DC = D // P
NQ = B * Q
R = H * Q
RT = R // P
TP = 125
NT = T // TP
QP = NQ // 4
NB = 3
CW = T // NB
TPB = NT // NB
HPC = 4
WCH = H // HPC
L = 3
KD = 128
KA = D // H
HA = P // KA
HA_ACT = 5
AR = HA * Q
APAD = 4 * P
W_SCALE = 64.0
TOK_SCALE = 16.0
GROUP_A = 4
HEADS_A = GROUP_A * P // Q
PIECES = 4
JP = NT // PIECES
EPS = 1e-5
QK_SCALE = KD ** -0.5 / W_SCALE ** 2
PROB_SCALE = 4096.0
MASKED = 1e30
FC = F // P

PACK = {}
_at = 0
for _l in (0, 1):
    for _n in ("bq", "bk", "bv", "bias_k"):
        PACK[_n, _l] = _at
        _at += H
for _n, _w in (("ln_scale0", DC), ("ln_offset0", DC), ("ln_scale1", DC), ("ln_offset1", DC), ("ln_scale2", DC),
               ("ln_offset2", DC), ("bo0", DC), ("bo1", DC), ("b_fc2", DC), ("b_fc1", FC)):
    PACK[_n] = _at
    _at += _w
NPACK = _at


def build(nc, x_t, ctx_nat, ctx_t, mask, pack, vrows, a_scale, a_offset, gate, wq, wk, wv, wo, w1, w2, out):
    es = ExitStack()
    with es:
        def sb(name, shape, dt=F32):
            return es.enter_context(nc.sbuf_tensor(name, shape, dt))

        def sem(name):
            return es.enter_context(nc.semaphore(name))

        qc = sb("qc", [P, B, DC * R])
        qs16 = qc[:, :, :].bitcast(F16).rearrange("p b (s c r) -> p b s c r", s=2, c=DC)
        ctxT = sb("ctxT", [P, 2, 2, DC, T], F16)
        nat = sb("nat", [TP, 2, 2, NT, D], F16)
        stage = sb("stage", [P, PIECES, JP * D])
        stageN = stage[0:TP, :, :].rearrange("p k (j d) -> p k j d", j=JP)
        stageT = stage[:, :, 0:T * DC // PIECES]
        probT_bytes = NT * R * 2 * 2
        arena = sb("arena", [P, probT_bytes // 4])
        probT = arena[0:TP + 1, :].bitcast(F16).rearrange("p (s j r) -> p s j r", s=2, j=NT)
        prob = sb("prob", [P, 2, T + 4])
        WSL = DC * HPC * P
        at = 4 * WSL
        wring = arena[:, 0:at].rearrange("p (k n) -> p k n", k=4)
        w16 = arena[:, at:2 * at].bitcast(F16).rearrange("p (k s n) -> p k s n", k=4, s=2)
        bvm = arena[0:H, 2 * at:2 * at + H * P].bitcast(F16).rearrange("p (s h k) -> p s h k", s=2, h=H)
        hT = arena[:, 2 * at:2 * at + DC * NQ].bitcast(F16).rearrange("p (s c n) -> p s c n", s=2, c=DC)
        hring = prob[:, :, :].rearrange("p i t -> p (i t)")[:, 0:4 * NQ].bitcast(F16)\
            .rearrange("p (k s n) -> p k s n", k=4, s=2)
        hid = prob[:, :, :].rearrange("p i t -> p (i t)")[:, 4 * NQ:6 * NQ].rearrange("p (k n) -> p k n", k=2)
        xc = prob[:, 0, 0:DC * NQ].rearrange("p (c n) -> p c n", c=DC)
        sq = prob[:, 1, 0:DC * NQ].rearrange("p (c n) -> p c n", c=DC)
        std = sb("std", [P, NQ])
        xT = sb("xT", [P, DC, NQ])
        pk = sb("pk", [P, NPACK])
        bkd = sb("bkd", [P, 2, H])
        bkd16 = sb("bkd16", [P, 2, 2, H], F16)
        bkm = sb("bkm", [P, 2, 2, H, H], F16)
        vr = sb("vr", [H, 2, 2, P])
        bvd = sb("bvd", [H, 2, P])
        bvd16 = vr[:, 0, :, :].rearrange("p i k -> p (i k)").bitcast(F16).rearrange("p (l s k) -> p l s k", l=2, s=2)
        small = sb("small", [P, 4 * NQ])
        tok_hl = small[0:H, 0:NQ].bitcast(F16).rearrange("p (s n) -> p s n", s=2)
        rowbuf = sb("rowbuf", [P, 2 * R])
        tokrow = rowbuf[0:2, 0:R].bitcast(F16).rearrange("p (i r) -> p i r", i=2)
        maskb = rowbuf[:, 0:T].bitcast(BF16).rearrange("p (i t) -> p i t", i=2)
        ptok_raw = small[0:H, NQ:2 * NQ].bitcast(F16).rearrange("p (s n) -> p s n", s=2)
        ptok_hl = tok_hl
        ident = sb("ident", [P, P])
        dmean = sb("dmean", [P, P])
        one = sb("one", [2, 1], F16)
        epsc = sb("epsc", [P, 1])
        warm = sb("warm", [P, 1])
        mx3 = sb("mx3", [P, 2, 4])
        nmax = sb("nmax", [P, 2, 1])
        sum3 = sb("sum3", [P, 2, 4])
        rsum = sb("rsum", [P, 2, 2])
        stats = sb("stats", [TP, B, NT, 6])
        mu = sb("mu", [TP, B * NT])
        rstd = sb("rstd", [TP, B * NT])
        stt = sb("stt", [TP, 2, B * NT])
        mrb = sb("mrb", [TP, 2, NT])
        a_sc = sb("a_sc", [TP, D])
        a_of = sb("a_of", [TP, D])
        mask8 = sb("mask8", [P, T], U8)
        anym = sb("anym", [P, 4])
        tg = sb("tg", [P, 2])

        flat = qc[:, :, :].rearrange("p b n -> p (b n)")
        n0 = B * 2 * DC * APAD // 2
        qbd = flat[:, 0:n0].bitcast(F16).rearrange("p (b s c r) -> p b s c r", b=B, s=2, c=DC)
        keyT = flat[:, n0:n0 + 2 * DC * T].bitcast(F16).rearrange("p (i s c t) -> p i s c t", i=2, s=2, c=DC)
        aT = ctxT[:, 0, :, :, :]
        spare = ctxT[:, 1, :, :, :].rearrange("p s c t -> p (s c t)")
        wkv = spare[:, 0:4 * DC * D].rearrange("p (w s c e) -> p w s c e", w=2, s=2, c=DC)
        wqo = spare[:, 4 * DC * D:8 * DC * D].bitcast(F32).rearrange("p (w c e) -> p w c e", w=2, c=DC)
        attnT = small[:, 0:DC * NQ].rearrange("p (c n) -> p c n", c=DC)
        picked = small[:, DC * NQ:DC * NQ + AR]
        qhl = small[:, 2 * NQ:4 * NQ].bitcast(F16).rearrange("p (m s n) -> p m s n", m=2, s=2)
        hm = sb("hm", [P, HA])
        hms = sb("hms", [P, HA])

        S = [es.enter_context(nc.psum_tensor(f"S{i}", [P, 512], F32)) for i in range(NB)]
        TB = [es.enter_context(nc.psum_tensor(f"TB{i}", [P, 512], F32)) for i in range(2)]
        PV = [es.enter_context(nc.psum_tensor(f"PV{i}", [P, 512], F32)) for i in range(2)]
        M = es.enter_context(nc.psum_tensor("M", [P, 512], F32))
        QB = [S[0], S[1], PV[0], PV[1]]
        rs = S[0][:, 8:8 + NQ]

        in_x = sem("in_x")
        in_aud = sem("in_aud")
        in_pack = sem("in_pack")
        passed = sem("passed")
        w_full = [sem(f"w_full{k}") for k in range(4)]
        stage_full = [sem(f"stage_full{k}") for k in range(4)]
        stage_free = sem("stage_free")
        mask_full = sem("mask_full")
        mask_ready = sem("mask_ready")
        const_ready = sem("const_ready")
        bkd_ready = sem("bkd_ready")
        bvd_ready = sem("bvd_ready")
        bvm_ready = sem("bvm_ready")
        mean_ready = sem("mean_ready")
        xc_ready = sem("xc_ready")
        sq_ready = sem("sq_ready")
        var_ready = sem("var_ready")
        std_ready = sem("std_ready")
        rs_ready = sem("rs_ready")
        xn_ready = sem("xn_ready")
        h_ready = sem("h_ready")
        x_ready = sem("x_ready")
        q_mm = sem("q_mm")
        qp_mm = sem("qp_mm")
        qp_hi = sem("qp_hi")
        qp_lo = sem("qp_lo")
        tok_scores = sem("tok_scores")
        tok_ready = sem("tok_ready")
        tokrow_full = [sem(f"tokrow_full{k}") for k in range(2)]
        split_hi = sem("split_hi")
        norm_step = sem("norm_step")
        a_ready = sem("a_ready")
        m_mm = sem("m_mm")
        m_hi = sem("m_hi")
        m_lo = sem("m_lo")
        w_hi = sem("w_hi")
        w_lo = sem("w_lo")
        in_qo = sem("in_qo")
        aq_mm = sem("aq_mm")
        aq_hi = sem("aq_hi")
        aq_lo = sem("aq_lo")
        qbd_ready = sem("qbd_ready")
        picked_ready = sem("picked_ready")
        mask_sum = sem("mask_sum")
        mask_term = sem("mask_term")
        score_ready = sem("score_ready")
        max_part = sem("max_part")
        negmax_ready = sem("negmax_ready")
        exp_done = sem("exp_done")
        sum_ready = sem("sum_ready")
        rsum_ready = sem("rsum_ready")
        probs_ready = sem("probs_ready")
        turned = sem("turned")
        pt_hi = sem("pt_hi")
        pt_lo = sem("pt_lo")
        pv_done = sem("pv_done")
        avg_ready = sem("avg_ready")
        ptok_moved = [sem(f"ptok_moved{k}") for k in range(2)]
        ptok_ready = sem("ptok_ready")
        tok_hi = sem("tok_hi")
        stats_done = sem("stats_done")
        ln_step = sem("ln_step")
        ln_step2 = sem("ln_step2")
        rstd_ready = sem("rstd_ready")
        sd_ready = sem("sd_ready")
        pool_step = sem("pool_step")
        ah_mm = sem("ah_mm")
        wo_mm = sem("wo_mm")
        f1_mm = sem("f1_mm")
        f2_mm = sem("f2_mm")
        tg_ready = sem("tg_ready")
        out_done = sem("out_done")
        avg_moved = sem("avg_moved")
        rs_row = sem("rs_row")
        sq_part = sem("sq_part")
        ring_free = sem("ring_free")
        q_hi = sem("q_hi")
        q_lo = sem("q_lo")
        ah_hi = sem("ah_hi")
        ah_lo = sem("ah_lo")
        avg_hi = sem("avg_hi")
        f1_act = sem("f1_act")
        f1_hi = sem("f1_hi")
        f1_lo = sem("f1_lo")
        h_hi = sem("h_hi")
        x_biased = sem("x_biased")
        bd_step = sem("bd_step")
        bq_scaled = sem("bq_scaled")

        def slot_uses(l, b, natural):
            return 2 * B * l + 2 * b + (2 if natural else 1) if l < 2 else 4 * B + b + 1

        chunks = []
        W_Q, W_O = [], []
        for l in range(2):
            W_Q.append(len(chunks))
            for n in range(2 * WCH):
                chunks.append(((wq, wk)[n % 2][l][n // 2], (qp_mm, DC * (H * l + HPC * (n // 2 + 1)))))
            W_O.append(len(chunks))
            for n in range(2 * WCH):
                chunks.append(((wv, wo)[n % 2][l][n // 2], (wo_mm, H * l + HPC * (n // 2 + 1))))
        W_KV = len(chunks)
        chunks += [(wk[2], None), (wv[2], None)]
        W_M = len(chunks)
        chunks += [((w1, w2)[n % 2][n // 2], ((f1_mm, f2_mm)[n % 2], 4 * (n // 2 + 1))) for n in range(4)]

        RING_FREE = [3 * (((k + 1) * WSL - 1) // (R // 2)) + 2 for k in range(4)]

        def split_of(i):
            n = i // 2
            w = chunks[n][0].shape[1] // 2
            part = slice(i % 2 * w, (i % 2 + 1) * w)
            if W_KV <= n < W_M:
                to = [wkv[:, n - W_KV, s, :, :].rearrange("p c e -> p (c e)")[:, part] for s in range(2)]
            else:
                to = [w16[:, n % 4, s, part] for s in range(2)]
            return [wring[:, n % 4, part]] + to

        UB = [M, PV[1]]
        NFILL = PIECES * DC
        NKU = DC * NB
        NVU = NT // 2
        MU = NFILL + NKU + NVU
        UNITS = [[0, 1], [2, 3, 4], [8, 9, 5], [6, 10, 7], [11, 12, 14], [13, 15, 16], [17, 18, 19]]
        SEQ = [u for units in UNITS for u in units]
        UNITS_AT = [[SEQ.index(u) for u in units] for units in UNITS]
        EARLY_STEPS = 3
        EARLY = sum(len(units) for units in UNITS[:EARLY_STEPS])
        HEAD_UNITS = {6: 0, 7: 1, 8: 2, 9: 3, 11: 4, 12: 5, 13: 6, 14: 7}
        LN_UNITS = [[8, 9], [10, 11], [12], list(range(13, MU))]
        MLP_UNITS = list(range(EARLY))

        def unit_of(b, at):
            early = isinstance(b, int) and (b == 0 or (b == 1 and at < EARLY))
            banks = [M, S[1]] if early else UB
            return (at if isinstance(b, int) and b == 0 else SEQ[at]), banks[at % 2]

        def units_at(l, s, first, last):
            return [] if l < 2 or last or (first and s < EARLY_STEPS) else UNITS_AT[s]

        def unit_out(b, par, at, half):
            u, bank = unit_of(b, at)
            if u < NFILL + NKU:
                n, m = divmod(u - NFILL, DC)
                return keyT[:, par, half, m, n * CW:(n + 1) * CW], bank[:, 0:CW]
            c = 2 * (u - NFILL - NKU)
            return nat[:, par, half, c:c + 2, :].rearrange("p j d -> p (j d)"), bank[0:TP, :]

        def turn_bank(tpar, f, spare):
            return (TB + PV)[f] if spare else TB[(3 * tpar + f) % 2]

        def has_spare(s, first):
            return int(first and 1 <= s < GROUP_A)

        def col(name, c):
            a = PACK[name] + c
            return pk[:, a:a + 1]

        def apart(eng):
            eng.sem_inc(passed, 1)

        def batches(eng, body, tail=None):
            body(0, 0, True, False)
            with eng.Fori(1, B - 2, 2) as b:
                body(b, 1, False, False)
                body(b + 1, 0, False, False)
            body(B - 1, (B - 1) % 2, False, True)

        def pv_part(l, s):
            if s == 0:
                return (0, 2, 3, 1)
            if s <= 3 or (s == 4 and l < 2):
                return (1, s - 1, 4 if l < 2 else 3, 1)
            return (0, s - 5, 3, 0) if s > 4 else None

        def group(l, grp):
            if l < 2:
                return (slice(0, GROUP_A * P) if grp == 0 else slice(GROUP_A * P, R)), DC * NT * 3
            return slice(grp * AR, (grp + 1) * AR), NT * 3

        def pv_before(l, b):
            return 4 * (B * l + b) if l < 2 else 8 * B + 2 * b

        block = es.enter_context(nc.Block())

        @block.sync
        def _(sp):
            def weights(lo, hi):
                for n in range(lo, hi):
                    if n >= 4:
                        sp.wait_ge(w_lo, 2 * (n - 3))
                    src = chunks[n][0]
                    sp.dma_start(wring[:, n % 4, 0:src.shape[1]], src).then_inc(w_full[n % 4], 16)

            def piece(l, b, k, natural):
                if l < 2:
                    n = 8 * (B * l + b) + (4 if natural else 0) + k
                    if l > 0 or natural or not isinstance(b, int) or b > 0:
                        sp.wait_ge(stage_free, n - 3)
                        apart(sp)
                    if l == 1 and not natural and (not isinstance(b, int) or b > 0):
                        sp.wait_ge(stats_done, 4 * b - 4 + k + 1)
                        apart(sp)
                else:
                    if isinstance(b, int) and b == 0:
                        sp.wait_ge(stage_free, 16 * B + k - 3)
                        sp.wait_ge(stats_done, 4 * (B - 1) + k + 1)
                    else:
                        sp.wait_ge(m_mm, MU * (b - 1) + SEQ.index(DC * k + DC - 1) + 1)
                        apart(sp)
                bb = bass.ds(b, 1)
                if natural:
                    src = ctx_nat[bb, :, k * JP * D:(k + 1) * JP * D].rearrange("b p n -> (b p) n")
                    dst = stage[0:TP, k, :]
                else:
                    w = T * DC // PIECES
                    src = ctx_t[bb, :, k * w:(k + 1) * w].rearrange("b p n -> (b p) n")
                    dst = stageT[:, k, :]
                sp.dma_start(dst, src).then_inc(stage_full[k], 16)

            def pieces(l, b):
                for natural in ((False, True) if l < 2 else (True,)):
                    for k in range(PIECES):
                        piece(l, b, k, natural)

            def token_row(l, b, par):
                g = B * l + b
                if l > 0 or not isinstance(b, int) or b > 1:
                    sp.wait_ge(score_ready, 3 * RT * (g - 1))
                    apart(sp)
                if isinstance(b, int) and b == 0:
                    sp.wait_ge(tok_ready, l + 1)
                    apart(sp)
                for i in range(2):
                    sp.dma_start(tokrow[i:i + 1, par, :].rearrange("p (h q) -> p h q", h=H),
                                 tok_hl[:, i, bass.ds(b * Q, Q)]).then_inc(tokrow_full[par], 16)

            def batch_loads(l, b, par):
                pieces(l, b)
                if l < 2:
                    token_row(l, b, par)
                else:
                    mask_load(b)

            def mask_load(b):
                if not isinstance(b, int) or b > 0:
                    sp.wait_ge(mask_ready, b)
                    apart(sp)
                sp.dma_start(mask8[:, :], mask[bass.ds(b, 1), :].broadcast_to([P, T])).then_inc(mask_full, 16)

            sp.dma_start(xT[:, :, :], x_t).then_inc(in_x, 16)
            sp.dma_start(pk[:, :], pack).then_inc(in_pack, 16)
            sp.dma_start(vr[:, :, :, :], vrows).then_inc(in_pack, 16)
            weights(0, 4)
            for k in range(PIECES):
                piece(0, 0, k, False)
            sp.dma_start(a_sc[:, :], a_scale.broadcast_to([TP, D])).then_inc(in_aud, 16)
            sp.dma_start(a_of[:, :], a_offset.broadcast_to([TP, D])).then_inc(in_aud, 16)
            sp.dma_start(tg[:, 0:1], gate.broadcast_to([P, 1])).then_inc(in_aud, 16)
            weights(4, 8)
            for k in range(PIECES):
                piece(0, 0, k, True)
            for l in range(L):
                if l < 2:
                    token_row(l, 0, 0)
                batch_loads(l, 1, 1)
                with sp.Fori(2, B - 1, 2) as b:
                    batch_loads(l, b, 0)
                    batch_loads(l, b + 1, 1)
                if l == 2:
                    break
                for k in range(4):
                    sp.wait_ge(ring_free, 4 * l + k + 1)
                    weights(W_O[l] + k, W_O[l] + k + 1)
                for k in range(PIECES):
                    piece(l + 1, 0, k, l + 1 == 2)
                if l == 0:
                    weights(W_O[0] + 4, W_O[0] + 8)
                    for k in range(PIECES):
                        piece(1, 0, k, True)
                    weights(W_Q[1], W_Q[1] + 8)
                else:
                    mask_load(0)
                    for w in range(2):
                        sp.dma_start(wqo[:, w, :, :], (wq, wo)[w][2].rearrange("p (c e) -> p c e", c=DC))\
                            .then_inc(in_qo, 16)
                    weights(W_O[1] + 4, len(chunks))
            for c in range(DC):
                sp.wait_ge(x_ready, 3 * DC + c + 1)
                sp.dma_start(out[:, c, :], xT[:, c, :]).then_inc(out_done, 16)
            sp.wait_ge(out_done, 16 * DC)

        @block.gpsimd
        def _(pool):
            steps = [0]

            def link(ins):
                steps[0] += 1
                ins.then_inc(pool_step, 1)
                pool.wait_ge(pool_step, steps[0])

            nc.gpsimd.memset(one[:, :], 1.0)
            nc.gpsimd.memset(epsc[:, :], EPS)
            nc.gpsimd.memset(dmean[:, :], 1.0 / D)
            link(nc.gpsimd.memset(ident[:, :], 0.0))
            nc.gpsimd.affine_select(out=ident[:, :], in_=ident[:, :], compare_op=ALU.not_equal, fill=1.0, base=0,
                                    pattern=[[-1, P]], channel_multiplier=1).then_inc(const_ready, 1)
            pool.wait_ge(bkd_ready, 1)
            for l in range(2):
                for i in range(2):
                    src = bkd16[:, l, i, :].unsqueeze(2).broadcast_to([P, H, H])
                    ins = nc.gpsimd.affine_select(out=bkm[:, l, i, :, :], in_=src, compare_op=ALU.is_equal, fill=0.0,
                                                  base=0, pattern=[[1, H], [-1, H]], channel_multiplier=0)
                ins.then_inc(const_ready, 1)

            def split(l, b, par, natural):
                g = B * l + b
                if l > 0 or not isinstance(b, int) or b >= 2:
                    if natural:
                        pool.wait_ge(pv_done, 4 * g - 4)
                    else:
                        pool.wait_ge(score_ready, 3 * RT * (g - 1))
                for k in range(PIECES):
                    pool.wait_ge(stage_full[k], 16 * slot_uses(l, b, natural))
                    apart(pool)
                    if natural:
                        src = stageN[:, k, :, :]
                        hi, lo = (nat[:, par, i, k * JP:(k + 1) * JP, :] for i in range(2))
                    else:
                        w = T * DC // PIECES
                        src = stageT[:, k, :]
                        hi, lo = (ctxT[:, par, i, k * w // T, (k * w) % T:(k * w) % T + w] for i in range(2))
                    nc.gpsimd.tensor_copy(hi, src).then_inc(split_hi, 1)
                    n = (8 * g + (4 if natural else 0) if l < 2 else 16 * B + 4 * b) + k + 1
                    pool.wait_ge(split_hi, n)
                    ins = nc.gpsimd.tensor_tensor(lo, src, hi, ALU.subtract)
                    ins.then_inc(stage_free, 1)

            link(nc.gpsimd.memset(hm[:, :], 1.0))
            link(nc.gpsimd.affine_select(out=hm[:, :], in_=hm[:, :], compare_op=ALU.is_ge, fill=0.0, base=0,
                                         pattern=[[-KA, HA]], channel_multiplier=1))
            link(nc.gpsimd.affine_select(out=hm[:, :], in_=hm[:, :], compare_op=ALU.is_ge, fill=0.0, base=KA - 1,
                                         pattern=[[KA, HA]], channel_multiplier=-1))
            nc.gpsimd.tensor_scalar(hms[:, :], hm[:, :], 1.0 / PROB_SCALE, None, ALU.mult).then_inc(const_ready, 1)

            def normalise(b):
                if isinstance(b, int) and b == 0:
                    pool.wait_ge(in_aud, 48)
                    pool.wait_ge(rstd_ready, 1)
                base = 9 * b
                for i, src in enumerate((mu, rstd)):
                    ins = nc.gpsimd.tensor_copy(mrb[:, i, :], src[:, bass.ds(b * NT, NT)])
                ins.then_inc(norm_step, 1)
                pool.wait_ge(norm_step, base + 1)
                for k in range(PIECES):
                    pool.wait_ge(stage_full[k], 16 * slot_uses(2, b, True))
                    apart(pool)
                    for j in range(JP):
                        c = k * JP + j
                        ins = nc.gpsimd.tensor_scalar(stageN[:, k, j, :], stageN[:, k, j, :], mrb[:, 0, c:c + 1],
                                                      mrb[:, 1, c:c + 1], ALU.subtract, ALU.mult)
                    ins.then_inc(norm_step, 1)
                    pool.wait_ge(norm_step, base + 2 + 2 * k)
                    bc = [v[:, :].unsqueeze(1).broadcast_to([TP, JP, D]) for v in (a_sc, a_of)]
                    nc.gpsimd.tensor_tensor(stageN[:, k, :, :], stageN[:, k, :, :], bc[0], ALU.mult)\
                        .then_inc(norm_step, 1)
                    pool.wait_ge(norm_step, base + 3 + 2 * k)
                    nc.gpsimd.tensor_tensor(stageN[:, k, :, :], stageN[:, k, :, :], bc[1], ALU.add)\
                        .then_inc(a_ready, 1)

            def prepare(l, b, par):
                if l < 2:
                    split(l, b, par, False)
                else:
                    normalise(b)
                    return
                split(l, b, par, True)

            for l in range(L):
                first = 0
                if l == 0:
                    prepare(0, 0, 0)
                    prepare(0, 1, 1)
                    first = 2
                if l == 2:
                    prepare(2, 0, 0)
                    prepare(2, 1, 1)
                    first = 2
                with pool.Fori(first, B - 1, 2) as b:
                    prepare(l, b, 0)
                    prepare(l, b + 1, 1)
                if l < 2:
                    pool.wait_ge(pv_done, 4 * B * (l + 1))
                    pool.wait_ge(bvd_ready, 1)
                    for i in range(2):
                        src = bvd16[:, l, i, :].unsqueeze(1).broadcast_to([H, H, P])
                        ins = nc.gpsimd.affine_select(out=bvm[:, i, :, :], in_=src, compare_op=ALU.is_equal, fill=0.0,
                                                      base=0, pattern=[[-1, H], [0, P]], channel_multiplier=1)
                    ins.then_inc(bvm_ready, 1)

        @block.tensor
        def _(pe):
            def mm(o, a, c, start, stop, skip=False):
                return nc.tensor.matmul(o, a, c, start=start, stop=stop, skip_group_check=skip)

            def layer_norm(n, x_count, fill=lambda at: None):
                if n == 0:
                    pe.wait_ge(const_ready, 1)
                    pe.wait_ge(in_x, 16)
                else:
                    pe.wait_ge(x_ready, x_count)
                for c in range(DC):
                    ins = mm(S[2][:, 0:NQ], dmean[:, :], xT[:, c, :], c == 0, c == DC - 1)
                ins.then_inc(mean_ready, 1)
                fill(0)
                pe.wait_ge(sq_ready, n + 1)
                for j in range(NQ // QP):
                    ins = mm(S[0][0:QP, j:j + 1], sq[:, 0, j * QP:(j + 1) * QP], dmean[:, 0:1], True, True)
                ins.then_inc(var_ready, 1)
                fill(1)
                pe.wait_ge(rs_ready, n + 1)
                for j in range(NQ // QP):
                    ins = mm(rs[:, j * QP:(j + 1) * QP], std[0:QP, 4 + j:5 + j].broadcast_to([QP, P]),
                             ident[0:QP, 0:QP], True, True)
                ins.then_inc(rs_row, 1)
                fill(2)

            PASSES = ((0, 0), (0, 1), (1, 0))

            def weights_in(n, half=1):
                pe.wait_ge(w_lo, 2 * n + half + 1)
                return w16[:, n % 4, :, :]

            def mm3(o, a, c, start, stop):
                for n, (i, j) in enumerate(PASSES):
                    ins = mm(o, a(i), c(j), start and n == 0, stop and n == 2)
                return ins

            def query_projection(l):
                def query(h):
                    if l > 0 or h >= 2:
                        pe.wait_ge(q_lo, H * l + h - 1)
                    j = h % HPC
                    for c in range(DC):
                        w = weights_in(W_Q[l] + h // HPC * 2, c).rearrange("p s (c n) -> p s c n", c=DC)
                        if h == 0:
                            pe.wait_ge(h_ready, DC * l + c + 1)
                        ins = mm3(TB[h % 2][:, 0:NQ], lambda i: w[:, i, c, j * KD:(j + 1) * KD],
                                  lambda i: hT[:, i, c, :], c == 0, c == DC - 1)
                    ins.then_inc(q_mm, 1)

                def through_keys(h):
                    w = weights_in(W_Q[l] + h // HPC * 2 + 1).rearrange("p s (j n) -> p s j n", j=HPC)
                    pe.wait_ge(q_lo, H * l + h + 1)
                    q = lambda i: hring[:, h % 4, i, :]
                    if l == 0 and h == 0:
                        pe.wait_ge(const_ready, 4)
                    ins = mm3(M[0:H, 0:NQ], lambda i: bkm[:, l, i, h, :], q, h == 0, h == H - 1)
                    if h == H - 1:
                        ins.then_inc(tok_scores, 1)
                    for c in range(DC):
                        n = DC * (H * l + h) + c
                        if n >= 4:
                            pe.wait_ge(qp_lo, n - 3)
                        ins = mm3(QB[n % 4][:, 0:NQ], lambda i: w[:, i, h % HPC, c * P:(c + 1) * P], q, True, True)
                        ins.then_inc(qp_mm, 1)

                query(0)
                query(1)
                for h in range(H):
                    if h + 2 < H:
                        query(h + 2)
                    through_keys(h)

            def scores(l, b, s, par, first):
                g = B * l + b
                t = RT * g + s
                if first and s == 0:
                    if l < 2:
                        pe.wait_ge(qp_lo, DC * H * (l + 1))
                    else:
                        pe.wait_ge(qbd_ready, 2 * DC)
                if s == 0:
                    if l < 2:
                        pe.wait_ge(stage_free, 8 * g + 4)
                    else:
                        pe.wait_ge(m_lo, MU * b + SEQ.index(NFILL + NKU - 1) + 1)
                bb = bass.ds(b, 1)
                for c in range(NB):
                    if l == 2 and first and s == 0 and c == 1:
                        pe.wait_ge(m_lo, MU + EARLY)
                    if l < 2 and not (first and s == 0):
                        pe.wait_ge(exp_done, 3 * t + c - 2)
                    if l == 2 and not (first and s == 0):
                        pe.wait_ge(max_part, 3 * t + c - 2)
                    o = S[c][:, 0:CW]
                    ds = range(DC) if l < 2 or s == RT // 2 else (int(s > RT // 2),)
                    n = 0
                    for d in ds:
                        for qi, ci in ((0, 0), (0, 1), (1, 0)):
                            if l < 2:
                                q = qs16[:, bb, qi, d, s * P:(s + 1) * P]
                                k = ctxT[:, par, ci, d, c * CW:(c + 1) * CW]
                            else:
                                r0 = s * P - d * (R - APAD)
                                q = qbd[:, bb, qi, d, r0:r0 + P]
                                k = keyT[:, par, ci, d, c * CW:(c + 1) * CW]
                            ins = mm(o, q.rearrange("p b r -> p (b r)"), k, n == 0, n == 3 * len(ds) - 1)
                            n += 1
                    if l < 2 and c == NB - 1:
                        if s == 0:
                            pe.wait_ge(tokrow_full[par], 128 * l + 16 * (b - par) + 32)
                        ins = mm(S[c][:, CW:CW + 1], tokrow[:, par, s * P:(s + 1) * P], one[:, :],
                                 False, True, skip=True)
                    ins.then_inc(score_ready, 1)

            def turn(l, t, tpar, f, W, spare):
                if f == 0:
                    pe.wait_ge(probs_ready, t + 1)
                n = 3 * t + f - 1 - spare
                if not (isinstance(t, int) and n < 1):
                    pe.wait_ge(pt_lo, n)
                bank = turn_bank(tpar, f, spare)
                for j in range(TPB):
                    c = f * TPB + j
                    ins = nc.tensor.transpose(bank[0:W, j * P:(j + 1) * P],
                                              prob[:, tpar % 2, c * TP:c * TP + W], ident[:, :])
                ins.then_inc(turned, 1)

            def average(l, b, par, grp, lo, hi):
                g = B * l + b
                rows, _ = group(l, grp)
                nrow = rows.stop - rows.start
                if lo == 0:
                    if grp == 0:
                        if l < 2:
                            pe.wait_ge(stage_free, 8 * g + 8)
                        else:
                            pe.wait_ge(m_lo, MU * b + MU)
                for m in range(lo, hi):
                    d, r = divmod(m, 3 * NT)
                    j, i = divmod(r, 3)
                    if d == 0 and i == 0 and j % TPB == 0:
                        pe.wait_ge(pt_lo, 3 * (RT * g + (GROUP_A if grp == 0 else RT)) - 2 + j // TPB)
                    pi, ci = ((0, 0), (1, 0), (0, 1))[i]
                    k = 2 * grp + d if l < 2 else grp
                    if r == 0:
                        if l == 2:
                            if not (isinstance(b, int) and b == 0 and k == 0):
                                pe.wait_ge(avg_moved, 2 * b + k)
                        elif not (isinstance(g, int) and g == 0 and k < 2):
                            pe.wait_ge(avg_ready, pv_before(l, b) + k - 1)
                    e = d if l < 2 else grp
                    ins = mm(PV[k % 2 if l < 2 else 0][:, 0:nrow], nat[:, par, ci, j, e * P:(e + 1) * P],
                             probT[0:TP, pi, j, rows], r == 0, r == 3 * NT - 1)
                    if r == 3 * NT - 1:
                        ins.then_inc(pv_done, 1)
                    if l < 2 and k == 3 and isinstance(b, int) and b == B - 1 and r in RING_FREE:
                        ins.then_inc(ring_free, 1)

            def unit(b, par, at):
                if not (isinstance(b, int) and b == 0 and at < 2):
                    pe.wait_ge(m_lo, MU * b + at - 1)
                u, o = unit_of(b, at)
                if u < NFILL:
                    k, c = divmod(u, DC)
                    if c == 0:
                        pe.wait_ge(a_ready, 4 * b + k + 1)
                    for j in range(JP):
                        ins = nc.tensor.transpose(o[:, j * TP:(j + 1) * TP], stageN[:, k, j, c * P:(c + 1) * P],
                                                  ident[0:TP, 0:TP])
                elif u < NFILL + NKU:
                    n, m = divmod(u - NFILL, DC)
                    i = 0
                    for d in range(DC):
                        for wi, ai in ((0, 0), (0, 1), (1, 0)):
                            ins = mm(o[:, 0:CW], wkv[:, 0, wi, d, m * P:(m + 1) * P],
                                     aT[:, ai, d, n * CW:(n + 1) * CW], i == 0, i == 3 * DC - 1)
                            i += 1
                else:
                    for j in range(2):
                        c = 2 * (u - NFILL - NKU) + j
                        i = 0
                        for d in range(DC):
                            for wi, ai in ((0, 0), (1, 0), (0, 1)):
                                ins = mm(o[0:TP, j * D:(j + 1) * D], aT[:, ai, d, c * TP:(c + 1) * TP],
                                         wkv[:, 1, wi, d, :], i == 0, i == 3 * DC - 1)
                                i += 1
                ins.then_inc(m_mm, 1)

            def attention(l):
                W = TP + 1 if l < 2 else TP

                def body(b, par, first, last):
                    t0 = RT * (B * l + b)
                    for s in range(RT):
                        scores(l, b, s, par, first)
                        prev = s > 0 or not first
                        if prev:
                            tp = RT * par + s - 1 if s > 0 else RT * (1 - par) + RT - 1
                            turn(l, t0 + s - 1, tp, 0, W, has_spare(s, first))
                            turn(l, t0 + s - 1, tp, 1, W, has_spare(s, first))
                        units = units_at(l, s, first, last)
                        for u in units[0:2]:
                            unit(b + 1, 1 - par, u)
                        work = pv_part(l, s)
                        if work is not None:
                            grp, part, parts, back = work
                            n = group(l, grp)[1]
                            lo, hi = part * n // parts, (part + 1) * n // parts
                            mid = lo + (hi - lo) * 2 // 3
                        if work is None or (first and back):
                            lo = mid = hi = 0
                        if hi:
                            average(l, b - back, (par + back) % 2, grp, lo, mid)
                        if prev:
                            turn(l, t0 + s - 1, tp, 2, W, has_spare(s, first))
                        if hi:
                            average(l, b - back, (par + back) % 2, grp, mid, hi)
                        for u in units[2:3]:
                            unit(b + 1, 1 - par, u)
                    if last:
                        t = t0 + RT - 1
                        n = group(l, 0)[1]
                        average(l, b, par, 0, 2 * n // 3, 11 * n // 12)
                        for f in range(2):
                            turn(l, t, RT * par + RT - 1, f, W, 0)
                        average(l, b, par, 0, 11 * n // 12, n)
                        turn(l, t, RT * par + RT - 1, 2, W, 0)
                        average(l, b, par, 1, 0, group(l, 1)[1])

                batches(pe, body)

            def output_projection(l):
                pe.wait_ge(avg_ready, 4 * B * (l + 1))

                def head(h):
                    n = H * l + h
                    if n >= 2:
                        pe.wait_ge(ah_lo, n - 1)
                    j = h % HPC
                    o = TB[h % 2][:, 0:NQ]
                    for c in range(DC):
                        w = weights_in(W_O[l] + h // HPC * 2, c).rearrange("p s (c n) -> p s c n", c=DC)
                        mm3(o, lambda i: w[:, i, c, j * KD:(j + 1) * KD], lambda i: qs16[:, :, i, c, h * Q:(h + 1) * Q],
                            c == 0, False)
                    if h == 0:
                        pe.wait_ge(bvm_ready, l + 1)
                        pe.wait_ge(ptok_ready, l + 1)
                    mm3(o, lambda i: bvm[:, i, h, :], lambda i: ptok_hl[:, i, :], False, True).then_inc(ah_mm, 1)

                def out(h):
                    w = weights_in(W_O[l] + h // HPC * 2 + 1).rearrange("p s (j n) -> p s j n", j=HPC)
                    pe.wait_ge(ah_lo, H * l + h + 1)
                    for c in range(DC):
                        ins = mm3(PV[c][:, 0:NQ], lambda i: w[:, i, h % HPC, c * P:(c + 1) * P],
                                  lambda i: hring[:, h % 4, i, :], h == 0, h == H - 1)
                    ins.then_inc(wo_mm, 1)

                head(0)
                head(1)
                for h in range(H):
                    if h + 2 < H:
                        head(h + 2)
                    out(h)
                    if l == 1 and h in HEAD_UNITS:
                        unit(0, 0, HEAD_UNITS[h])

            def ln_units(at):
                for u in LN_UNITS[at + 1]:
                    unit(0, 0, u)

            def mlp():

                def hidden(f):
                    w = weights_in(W_M + f // 4 * 2).rearrange("p s (c n) -> p s c n", c=DC)
                    if f >= 2:
                        pe.wait_ge(f1_act, f - 1)
                    j = f % 4
                    for c in range(DC):
                        if f == 0:
                            pe.wait_ge(h_ready, 2 * DC + c + 1)
                        ins = mm3(TB[f % 2][:, 0:NQ], lambda i: w[:, i, c, j * P:(j + 1) * P],
                                  lambda i: hT[:, i, c, :], c == 0, c == DC - 1)
                    ins.then_inc(f1_mm, 1)

                def out(f):
                    w = weights_in(W_M + f // 4 * 2 + 1).rearrange("p s (j n) -> p s j n", j=4)
                    pe.wait_ge(f1_lo, f + 1)
                    for c in range(DC):
                        ins = mm3(PV[c][:, 0:NQ], lambda i: w[:, i, f % 4, c * P:(c + 1) * P],
                                  lambda i: hring[:, f % 4, i, :], f == 0, f == FC - 1)
                    ins.then_inc(f2_mm, 1)

                hidden(0)
                hidden(1)
                for f in range(FC):
                    if f + 2 < FC:
                        hidden(f + 2)
                    out(f)
                    unit(1, 1, MLP_UNITS[f])

            layer_norm(0, 0)
            query_projection(0)
            attention(0)
            output_projection(0)
            layer_norm(1, DC)
            query_projection(1)
            attention(1)
            output_projection(1)
            pe.wait_ge(w_lo, 2 * W_M)
            for u in LN_UNITS[0]:
                unit(0, 0, u)
            layer_norm(2, 2 * DC, ln_units)
            mlp()
            pe.wait_ge(x_ready, 3 * DC)
            pe.wait_ge(in_qo, 32)
            for m in range(DC):
                for c in range(DC):
                    ins = mm(TB[m][:, 0:NQ], wqo[:, 0, c, m * P:(m + 1) * P], xT[:, c, :], c == 0, c == DC - 1)
                ins.then_inc(aq_mm, 1)
            attention(2)
            pe.wait_ge(avg_ready, 8 * B + 2 * B)
            for m in range(DC):
                for c in range(DC):
                    ins = mm(PV[m][:, 0:NQ], wqo[:, 1, c, m * P:(m + 1) * P], attnT[:, c, :], c == 0, c == DC - 1)
                ins.then_inc(wo_mm, 1)

        @block.scalar
        def _(act):
            def table(f):
                nc.scalar.activation(warm[:, :], epsc[:, :], f)

            def layer_norm(n, fill=lambda at: None):
                if n == 0:
                    act.wait_ge(const_ready, 1)
                table(ACT.Sqrt)
                for c in range(DC):
                    act.wait_ge(xc_ready, DC * n + c + 1)
                    ins = nc.scalar.activation(sq[:, c, :], xc[:, c, :], ACT.Square)
                ins.then_inc(sq_part, 1)
                fill(0)
                act.wait_ge(var_ready, n + 1)
                nc.scalar.activation(std[0:QP, 0:4], S[0][0:QP, 0:4], ACT.Sqrt, bias=epsc[0:QP, :])\
                    .then_inc(std_ready, 1)
                fill(1)
                for c in range(DC):
                    act.wait_ge(xn_ready, DC * n + c + 1)
                    nc.scalar.activation(hT[:, 0, c, :], xc[:, c, :], ACT.Identity,
                                         bias=col(f"ln_offset{n}", c)).then_inc(h_hi, 1)
                fill(2)

            def weights_high(i):
                n = i // 2
                act.wait_ge(w_full[n % 4], 16 * (n // 4 + 1))
                if n >= 4 and not W_KV <= n < W_M and chunks[n - 4][1]:
                    act.wait_ge(*chunks[n - 4][1])
                raw, hi, _ = split_of(i)
                nc.scalar.activation(hi, raw, ACT.Copy, scale=W_SCALE).then_inc(w_hi, 1)

            def query_projection(l):
                for h in range(H + 1):
                    if h < H:
                        act.wait_ge(q_mm, H * l + h + 1)
                        if h >= 4:
                            act.wait_ge(qp_mm, DC * (H * l + h - 3))
                        nc.scalar.activation(hring[:, h % 4, 0, :], TB[h % 2][:, 0:NQ], ACT.Identity,
                                             bias=col(("bq", l), h)).then_inc(q_hi, 1)
                    if h + 4 < 4 * WCH:
                        weights_high(2 * W_Q[l] + h + 4)
                    if h > 0:
                        for c in range(DC):
                            n = DC * (H * l + h - 1) + c
                            act.wait_ge(qp_mm, n + 1)
                            o = qs16[:, :, 0, c, (h - 1) * Q:h * Q]
                            nc.scalar.activation(o, QB[n % 4][:, 0:NQ].rearrange("p (b q) -> p b q", b=B),
                                                 ACT.Copy, scale=QK_SCALE).then_inc(qp_hi, 1)
                table(ACT.Exp)
                act.wait_ge(tok_scores, l + 1)
                nc.scalar.activation(tok_hl[:, 0, :], M[0:H, 0:NQ], ACT.Copy, scale=QK_SCALE).then_inc(tok_hi, 1)

            def exponentiate(l, t, tp, c, first):
                i = tp % 2
                w = CW + 1 if l < 2 and c == NB - 1 else CW
                if c == 0:
                    act.wait_ge(negmax_ready, t + 1)
                    if l < 2 and not first:
                        act.wait_ge(turned, 3 * t - 3)
                o = prob[:, i, c * CW:c * CW + w]
                src = S[c][:, 0:w] if l < 2 else o
                nc.scalar.activation(o, src, ACT.Exp, bias=nmax[:, i, :],
                                     accum_out=sum3[:, i, c:c + 1]).then_inc(exp_done, 1)

            def high_half(l, g, t, tp, s, f, W, fresh, spare=0):
                act.wait_ge(turned, 3 * t + f + 1)
                if l < 2 and f == 0 and not fresh and s in (0, GROUP_A):
                    act.wait_ge(pv_done, 4 * g - 4 + (2 if s < GROUP_A else 4))
                if l < 2 and f == 0 and not fresh and s in (0, GROUP_A - 1):
                    act.wait_ge(ptok_moved[int(s > 0)], 32 * g)
                if l == 2 and f == 0 and not fresh and s in (0, RT // 2):
                    act.wait_ge(pv_done, 2 * g + 4 * B - 2 + (1 if s == 0 else 2))
                o = probT[0:W, 0, f * TPB:(f + 1) * TPB, s * P:(s + 1) * P]
                src = turn_bank(tp, f, spare)[0:W, :].rearrange("p (j r) -> p j r", j=TPB)
                nc.scalar.activation(o, src, ACT.Copy).then_inc(pt_hi, 1)

            def store_average(l, b, k):
                g = B * l + b
                grp, d = divmod(k, 2)
                act.wait_ge(pv_done, 4 * g + k + 1)
                r0, r1 = (0, GROUP_A * P) if grp == 0 else (GROUP_A * P, R)
                o = qs16[:, bass.ds(b, 1), 0, d, r0:r1].rearrange("p b r -> p (b r)")
                nc.scalar.activation(o, PV[k % 2][:, 0:r1 - r0], ACT.Copy, scale=1.0 / PROB_SCALE)\
                    .then_inc(avg_hi, 1)

            def move_average(b, grp):
                n = 2 * b + grp + 1
                act.wait_ge(pv_done, 8 * B + n)
                if not isinstance(b, int) or n > 1:
                    act.wait_ge(avg_ready, 8 * B + n - 1)
                nc.scalar.activation(picked, PV[0][:, 0:AR], ACT.Copy).then_inc(avg_moved, 1)

            def move_token(l, b, grp):
                act.wait_ge(pt_lo, 3 * (RT * (B * l + b) + (GROUP_A if grp == 0 else RT)))
                h0, h1 = (0, HEADS_A) if grp == 0 else (HEADS_A, H)
                for i in range(2):
                    act.dma_start(ptok_raw[h0:h1, i, bass.ds(b * Q, Q)],
                                  probT[TP:TP + 1, i, NT - 1, h0 * Q:h1 * Q].rearrange("p (h q) -> p h q", h=h1 - h0))\
                        .then_inc(ptok_moved[grp], 16)

            def unit_high(b, par, at):
                u, bank = unit_of(b, at)
                act.wait_ge(m_mm, MU * b + at + 1)
                if u < NFILL:
                    k, c = divmod(u, DC)
                    o, src, scale = aT[:, 0, c, k * JP * TP:(k + 1) * JP * TP], bank[:, 0:JP * TP], 1.0
                else:
                    o, src = unit_out(b, par, at, 0)
                    scale = 1.0 / W_SCALE
                nc.scalar.activation(o, src, ACT.Copy, scale=scale).then_inc(m_hi, 1)

            def mask_row(b, par):
                act.wait_ge(mask_full, 16 * b + 16)
                nc.scalar.activation(maskb[:, par, :], mask8[:, :], ACT.Copy, accum_out=anym[:, 0:1])\
                    .then_inc(mask_sum, 1)

            def mask_addend(b, par):
                act.wait_ge(mask_term, 4 * b + 4)
                nc.scalar.activation(maskb[:, par, :], mask8[:, :], ACT.Identity, scale=MASKED,
                                     bias=anym[:, 3:4]).then_inc(mask_ready, 1)

            def attention(l):
                W = TP + 1 if l < 2 else TP

                def body(b, par, first, last):
                    t0 = RT * (B * l + b)
                    for s in range(RT):
                        prev = s > 0 or not first
                        tp = RT * par + s - 1 if s > 0 else RT * (1 - par) + RT - 1
                        ps = (s - 1) % RT
                        units = units_at(l, s, first, last)
                        start = first and l == 0
                        for f in range(NB):
                            if prev and f < 2:
                                high_half(l, B * l + b - (s == 0), t0 + s - 1, tp, ps, f, W, start or
                                          (l == 2 and first), has_spare(s, first))
                            for u in units[f - 1:f] if f else []:
                                unit_high(b + 1, 1 - par, u)
                            exponentiate(l, t0 + s, RT * par + s, f, start and s < 2)
                        if prev:
                            high_half(l, B * l + b - (s == 0), t0 + s - 1, tp, ps, 2, W, start or
                                      (l == 2 and first), has_spare(s, first))
                        if l == 2:
                            if s == 5 and not last:
                                mask_row(b + 1, 1 - par)
                                mask_addend(b + 1, 1 - par)
                            for u in units[2:3]:
                                unit_high(b + 1, 1 - par, u)
                            if s in (0, 3) and not first:
                                move_average(b - 1, s // 3)
                            continue
                        if s == 0 and not first:
                            store_average(l, b - 1, 1)
                        if s == 1 and not first:
                            move_token(l, b - 1, 1)
                        if s == 2 and not first:
                            store_average(l, b - 1, 2)
                        if s == GROUP_A + 1:
                            move_token(l, b, 0)
                        if s == 4 and not first:
                            store_average(l, b - 1, 3)
                        if s == 6:
                            store_average(l, b, 0)
                    if last:
                        for f in range(NB):
                            high_half(l, B * l + b, t0 + RT - 1, RT * par + RT - 1, RT - 1, f, W, False)
                            if f == 1 and l < 2:
                                store_average(l, b, 1)
                            if f == 1 and l == 2:
                                move_average(b, 0)
                        if l < 2:
                            move_token(l, b, 1)
                            store_average(l, b, 2)
                            store_average(l, b, 3)
                        else:
                            move_average(b, 1)

                batches(act, body)

            def output_projection(l):
                act.wait_ge(pv_done, 4 * B * (l + 1))
                for k in range(2):
                    act.wait_ge(ptok_moved[k], 32 * B * (l + 1))
                for i in range(2):
                    weights_high(2 * W_O[l] + i)
                nc.scalar.activation(ptok_hl, ptok_raw, ACT.Copy, scale=TOK_SCALE / PROB_SCALE).then_inc(ptok_ready, 1)
                for i in range(2, 4):
                    weights_high(2 * W_O[l] + i)
                for h in range(H):
                    act.wait_ge(ah_mm, H * l + h + 1)
                    if h >= 4:
                        act.wait_ge(wo_mm, H * l + h - 3)
                    nc.scalar.activation(hring[:, h % 4, 0, :], TB[h % 2][:, 0:NQ], ACT.Identity,
                                         bias=col(("bv", l), h)).then_inc(ah_hi, 1)
                    if l == 1 and h == 2:
                        act.wait_ge(ln_step, 5)
                        nc.scalar.activation(rstd[:, :], stt[:, 0, :], ACT.Sqrt, bias=epsc[0:TP, :])\
                            .then_inc(sd_ready, 1)
                    if l == 1 and h - 1 in HEAD_UNITS:
                        unit_high(0, 0, HEAD_UNITS[h - 1])
                    weights_high(2 * W_O[l] + h + 4)

            act.wait_ge(in_pack, 32)
            layer_norm(0, lambda at: [weights_high(2 * W_Q[0] + i) for i in range(4) if at == 0])
            act.wait_ge(bq_scaled, 1)
            query_projection(0)
            attention(0)
            output_projection(0)
            layer_norm(1)
            query_projection(1)
            attention(1)
            output_projection(1)
            for u in LN_UNITS[0]:
                unit_high(0, 0, u)

            def ln_units(at):
                if at == 2:
                    table(ACT.Gelu)
                for n, u in enumerate(LN_UNITS[at + 1]):
                    unit_high(0, 0, u)
                    if at == 2:
                        weights_high(2 * W_M + n)
            layer_norm(2, ln_units)
            weights_high(2 * W_M + 7)
            for f in range(FC):
                act.wait_ge(f1_mm, f + 1)
                if f >= 2:
                    act.wait_ge(f1_lo, f - 1)
                nc.scalar.activation(hid[:, f % 2, :], TB[f % 2][:, 0:NQ], ACT.Gelu, scale=1.0 / W_SCALE,
                                     bias=col("b_fc1", f)).then_inc(f1_act, 1)
                if f > 0:
                    unit_high(1, 1, MLP_UNITS[f - 1])
                if f == 2:
                    mask_row(0, 0)
                if f == 4:
                    mask_addend(0, 0)
            unit_high(1, 1, MLP_UNITS[FC - 1])
            act.wait_ge(in_aud, 48)
            nc.scalar.activation(tg[:, 1:2], tg[:, 0:1], ACT.Tanh).then_inc(tg_ready, 1)
            table(ACT.Exp)
            for m in range(DC):
                act.wait_ge(aq_mm, m + 1)
                nc.scalar.activation(qhl[:, m, 0, :], TB[m][:, 0:NQ], ACT.Copy, scale=KA ** -0.5).then_inc(aq_hi, 1)
            for m in range(DC):
                act.wait_ge(aq_hi, m + 1)
                for j in range(HA_ACT):
                    r0 = j * Q + m * (APAD - AR)
                    ins = nc.scalar.activation(qbd[:, :, 0, m, r0:r0 + Q],
                                               qhl[:, m, 0, :].rearrange("p (b q) -> p b q", b=B), ACT.Copy,
                                               scale=hm[:, j:j + 1])
                ins.then_inc(qbd_ready, 1)
            attention(2)

        @block.vector
        def _(dve):
            def layer_norm(n, fill=lambda at: None):
                dve.wait_ge(mean_ready, n + 1)
                for c in range(DC):
                    ins = nc.vector.tensor_tensor(xc[:, c, :], xT[:, c, :], S[2][:, 0:NQ], ALU.subtract)
                    ins.then_inc(xc_ready, 1)
                dve.wait_ge(sq_part, n + 1)
                nc.vector.tensor_tensor(sq[:, 0, :], sq[:, 0, :], sq[:, 1, :], ALU.add).then_inc(sq_ready, 1)
                fill(0)
                dve.wait_ge(std_ready, n + 1)
                nc.vector.reciprocal(std[0:QP, 4:8], std[0:QP, 0:4]).then_inc(rs_ready, 1)
                fill(1)
                dve.wait_ge(rs_row, n + 1)
                for c in range(DC):
                    nc.vector.scalar_tensor_tensor(xc[:, c, :], xc[:, c, :], col(f"ln_scale{n}", c), rs,
                                                   ALU.mult, ALU.mult).then_inc(xn_ready, 1)
                for c in range(DC):
                    dve.wait_ge(h_hi, DC * n + c + 1)
                    nc.vector.scalar_tensor_tensor(hT[:, 1, c, :], xc[:, c, :], col(f"ln_offset{n}", c),
                                                   hT[:, 0, c, :], ALU.add, ALU.subtract).then_inc(h_ready, 1)
                fill(2)

            def weights_low(i):
                dve.wait_ge(w_hi, i + 1)
                raw, hi, lo = split_of(i)
                nc.vector.scalar_tensor_tensor(lo, raw, W_SCALE, hi, ALU.mult, ALU.subtract).then_inc(w_lo, 1)

            def head_low(h, ready, n, bias, done):
                dve.wait_ge(ready, n)
                nc.vector.scalar_tensor_tensor(hring[:, h % 4, 1, :], TB[h % 2][:, 0:NQ], bias, hring[:, h % 4, 0, :],
                                               ALU.add, ALU.subtract).then_inc(done, 1)

            def query_projection(l):
                for h in range(H + 1):
                    if h < H:
                        head_low(h, q_hi, H * l + h + 1, col(("bq", l), h), q_lo)
                    if h + 4 < 4 * WCH:
                        weights_low(2 * W_Q[l] + h + 4)
                    if h > 0:
                        for c in range(DC):
                            n = DC * (H * l + h - 1) + c
                            dve.wait_ge(qp_hi, n + 1)
                            hi, lo = (qs16[:, :, i, c, (h - 1) * Q:h * Q] for i in range(2))
                            nc.vector.scalar_tensor_tensor(
                                lo, QB[n % 4][:, 0:NQ].rearrange("p (b q) -> p b q", b=B), QK_SCALE, hi,
                                ALU.mult, ALU.subtract).then_inc(qp_lo, 1)
                dve.wait_ge(tok_hi, l + 1)
                nc.vector.scalar_tensor_tensor(tok_hl[:, 1, :], M[0:H, 0:NQ], QK_SCALE, tok_hl[:, 0, :],
                                               ALU.mult, ALU.subtract).then_inc(tok_ready, 1)
                for c in range(DC):
                    ins = nc.vector.tensor_scalar(xT[:, c, :], xT[:, c, :], col(f"bo{l}", c), None, ALU.add)
                ins.then_inc(x_biased, 1)

            def average_low(l, b, k):
                dve.wait_ge(avg_hi, 4 * (B * l + b) + k + 1)
                apart(dve)
                grp, d = divmod(k, 2)
                r0, r1 = (0, GROUP_A * P) if grp == 0 else (GROUP_A * P, R)
                hi, lo = (qs16[:, bass.ds(b, 1), i, d, r0:r1].rearrange("p b r -> p (b r)") for i in range(2))
                nc.vector.scalar_tensor_tensor(lo, PV[k % 2][:, 0:r1 - r0], 1.0 / PROB_SCALE, hi,
                                               ALU.mult, ALU.subtract).then_inc(avg_ready, 1)

            def ln_link(ins, n):
                ins.then_inc(ln_step, 1)
                dve.wait_ge(ln_step, n)

            def context_variance():
                dve.wait_ge(stats_done, 4 * B)
                st = stats[:, :, :, :].rearrange("p b j n -> p (b j) n")
                ln_link(nc.vector.tensor_tensor(mu[:, :], st[:, :, 1], st[:, :, 4], ALU.add), 1)
                ln_link(nc.vector.tensor_tensor(stt[:, 1, :], st[:, :, 1], st[:, :, 4], ALU.subtract), 2)
                ln_link(nc.vector.tensor_tensor(stt[:, 0, :], st[:, :, 2], st[:, :, 5], ALU.add), 3)
                ln_link(nc.vector.scalar_tensor_tensor(stt[:, 1, :], stt[:, 1, :], D / 4.0, stt[:, 1, :],
                                                       ALU.mult, ALU.mult), 4)
                nc.vector.tensor_scalar(mu[:, :], mu[:, :], 0.5, None, ALU.mult)
                nc.vector.tensor_tensor(stt[:, 0, :], stt[:, 0, :], stt[:, 1, :], ALU.add).then_inc(ln_step2, 1)
                dve.wait_ge(ln_step2, 1)
                ln_link(nc.vector.tensor_scalar(stt[:, 0, :], stt[:, 0, :], 1.0 / D, None, ALU.mult), 5)

            def output_projection(l):
                for i in range(2):
                    weights_low(2 * W_O[l] + i)
                for i in range(2, 4):
                    weights_low(2 * W_O[l] + i)
                for h in range(H):
                    head_low(h, ah_hi, H * l + h + 1, col(("bv", l), h), ah_lo)
                    if l == 1 and h == 1:
                        context_variance()
                    if l == 1 and h == 3:
                        dve.wait_ge(sd_ready, 1)
                        nc.vector.reciprocal(rstd[:, :], rstd[:, :]).then_inc(rstd_ready, 1)
                    if l == 1 and h - 1 in HEAD_UNITS:
                        unit_low(0, 0, HEAD_UNITS[h - 1])
                    weights_low(2 * W_O[l] + h + 4)

            def maxima(l, t, tp, c, par):
                i = tp % 2
                w = CW + 1 if l < 2 and c == NB - 1 else CW
                dve.wait_ge(score_ready, 3 * t + c + 1)
                if l < 2:
                    nc.vector.tensor_reduce(mx3[:, i, c:c + 1], S[c][:, 0:w], AX_X, ALU.max).then_inc(max_part, 1)
                else:
                    if c == 0:
                        dve.wait_ge(turned, 3 * t - 3)
                    apart(dve)
                    nc.vector.tensor_tensor_reduce(
                        out=prob[:, i, c * CW:(c + 1) * CW], in0=S[c][:, 0:CW],
                        in1=maskb[:, par, c * CW:(c + 1) * CW], scale=1.0, scalar=-3.0e38,
                        op0=ALU.add, op1=ALU.max, accum_out=mx3[:, i, c:c + 1]).then_inc(max_part, 1)

            def row_maximum(l, t, tp):
                i = tp % 2
                dve.wait_ge(max_part, 3 * t + 3)
                nc.vector.tensor_reduce(nmax[:, i, :], mx3[:, i, 0:NB], AX_X, ALU.max, negate=True)\
                    .then_inc(negmax_ready, 1)

            def normalise(l, t, tp):
                i = tp % 2
                w = T + 1 if l < 2 else T
                dve.wait_ge(exp_done, 3 * t + 3)
                nc.vector.tensor_reduce(rsum[:, i, 0:1], sum3[:, i, 0:NB], AX_X, ALU.add).then_inc(sum_ready, 1)
                dve.wait_ge(sum_ready, t + 1)
                nc.vector.reciprocal(rsum[:, i, 1:2], rsum[:, i, 0:1]).then_inc(rsum_ready, 1)
                dve.wait_ge(rsum_ready, t + 1)
                nc.vector.tensor_scalar(prob[:, i, 0:w], prob[:, i, 0:w], rsum[:, i, 1:2], PROB_SCALE,
                                        ALU.mult, ALU.mult).then_inc(probs_ready, 1)

            def low_half(t, tp, s, f, W, spare=0):
                dve.wait_ge(pt_hi, 3 * t + f + 1)
                hi, lo = (probT[0:W, i, f * TPB:(f + 1) * TPB, s * P:(s + 1) * P] for i in range(2))
                src = turn_bank(tp, f, spare)[0:W, :].rearrange("p (j r) -> p j r", j=TPB)
                nc.vector.tensor_tensor(lo, src, hi, ALU.subtract).then_inc(pt_lo, 1)

            def unit_low(b, par, at):
                u, bank = unit_of(b, at)
                dve.wait_ge(m_hi, MU * b + at + 1)
                if u < NFILL:
                    k, c = divmod(u, DC)
                    hi, lo = (aT[:, i, c, k * JP * TP:(k + 1) * JP * TP] for i in range(2))
                    nc.vector.tensor_tensor(lo, bank[:, 0:JP * TP], hi, ALU.subtract).then_inc(m_lo, 1)
                else:
                    hi, src = unit_out(b, par, at, 0)
                    lo, _ = unit_out(b, par, at, 1)
                    nc.vector.scalar_tensor_tensor(lo, src, 1.0 / W_SCALE, hi, ALU.mult, ALU.subtract)\
                        .then_inc(m_lo, 1)

            def pick_average(b, grp):
                n = 2 * b + grp + 1
                heads = picked.rearrange("p (h q) -> p h q", h=HA)
                dve.wait_ge(avg_moved, n)
                nc.vector.tensor_tensor(heads, heads, hms[:, :].unsqueeze(2).broadcast_to([P, HA, Q]), ALU.mult)\
                    .then_inc(picked_ready, 1)
                dve.wait_ge(picked_ready, n)
                nc.vector.tensor_reduce(attnT[:, grp, bass.ds(b * Q, Q)], heads.rearrange("p h q -> p q h"),
                                        AX_X, ALU.add).then_inc(avg_ready, 1)

            def context_stats(b, k):
                dve.wait_ge(stage_full[k], 16 * slot_uses(1, b, True))
                for j in range(JP):
                    o = stats[:, bass.ds(b, 1), k * JP + j, :].rearrange("p b n -> p (b n)")
                    ins = nc.vector.bn_stats(o, stageN[:, k, j, :])
                ins.then_inc(stats_done, 1)

            def mask_term_of(b):
                dve.wait_ge(mask_sum, b + 1)
                base = 4 * b
                nc.vector.tensor_scalar(anym[:, 1:2], anym[:, 0:1], 1.0, 1.0, ALU.min, ALU.subtract)\
                    .then_inc(mask_term, 1)
                dve.wait_ge(mask_term, base + 1)
                nc.vector.tensor_scalar(anym[:, 2:3], anym[:, 1:2], 3.0e38, 4.0, ALU.mult, ALU.mult)\
                    .then_inc(mask_term, 1)
                dve.wait_ge(mask_term, base + 2)
                nc.vector.tensor_scalar(anym[:, 1:2], anym[:, 2:3], 0.0, -MASKED, ALU.mult, ALU.add)\
                    .then_inc(mask_term, 1)
                dve.wait_ge(mask_term, base + 3)
                nc.vector.tensor_copy(anym[:, 3:4], anym[:, 1:2]).then_inc(mask_term, 1)

            def attention(l):
                W = TP + 1 if l < 2 else TP

                def body(b, par, first, last):
                    t0 = RT * (B * l + b)
                    for s in range(RT):
                        prev = s > 0 or not first
                        tp = RT * par + s - 1 if s > 0 else RT * (1 - par) + RT - 1
                        units = units_at(l, s, first, last)
                        if l == 2 and s == 0:
                            dve.wait_ge(mask_ready, b + 1)
                        for c in range(NB):
                            maxima(l, t0 + s, RT * par + s, c, par)
                        row_maximum(l, t0 + s, RT * par + s)
                        if prev:
                            low_half(t0 + s - 1, tp, (s - 1) % RT, 0, W, has_spare(s, first))
                            low_half(t0 + s - 1, tp, (s - 1) % RT, 1, W, has_spare(s, first))
                        for u in units[0:2]:
                            unit_low(b + 1, 1 - par, u)
                        normalise(l, t0 + s, RT * par + s)
                        if prev:
                            low_half(t0 + s - 1, tp, (s - 1) % RT, 2, W, has_spare(s, first))
                        if l == 2 and not last and s == 5:
                            mask_term_of(b + 1)
                        for u in units[2:3]:
                            unit_low(b + 1, 1 - par, u)
                        if l == 2 and not first and s in (1, 4):
                            pick_average(b - 1, s // 4)
                        if l < 2 and s % 2 == 0 and not (first and s < 6):
                            average_low(l, b if s == 6 else b - 1, (s // 2 + 1) % 4)
                        if l == 1 and not last and 2 <= s < 6:
                            context_stats(b + 1, s - 2)
                    if last:
                        for f in range(NB):
                            low_half(t0 + RT - 1, RT * par + RT - 1, RT - 1, f, W)
                            if f == 1 and l < 2:
                                average_low(l, b, 1)
                        if l < 2:
                            average_low(l, b, 2)
                            average_low(l, b, 3)
                        if l == 2:
                            pick_average(b, 0)
                            pick_average(b, 1)

                batches(dve, body)

            def add_output(l):
                if l < 2:
                    dve.wait_ge(wo_mm, H * (l + 1))
                    dve.wait_ge(x_biased, l + 1)
                else:
                    dve.wait_ge(tg_ready, 1)
                for c in range(DC):
                    sc = W_SCALE ** -2 if l < 2 else tg[:, 1:2]
                    if l == 2:
                        dve.wait_ge(wo_mm, 2 * H + c + 1)
                    nc.vector.scalar_tensor_tensor(xT[:, c, :], PV[c][:, 0:NQ], sc, xT[:, c, :],
                                                   ALU.mult, ALU.add).then_inc(x_ready, 1)

            dve.wait_ge(in_pack, 32)
            for l in range(2):
                a, c = PACK["bias_k", l], PACK["bk", l]
                ins = nc.vector.tensor_tensor(bkd[:, l, :], pk[:, a:a + H], pk[:, c:c + H], ALU.subtract)
            nc.vector.tensor_tensor(bvd[:, :, :], vr[:, :, 0, :], vr[:, :, 1, :], ALU.subtract).then_inc(bd_step, 1)
            dve.wait_ge(bd_step, 1)
            nc.vector.tensor_scalar(bkd16[:, :, 0, :], bkd[:, :, :], W_SCALE, None, ALU.mult)
            nc.vector.tensor_scalar(bvd16[:, :, 0, :], bvd[:, :, :], W_SCALE / TOK_SCALE, None, ALU.mult)\
                .then_inc(bd_step, 1)
            dve.wait_ge(bd_step, 2)
            nc.vector.scalar_tensor_tensor(bkd16[:, :, 1, :], bkd[:, :, :], W_SCALE, bkd16[:, :, 0, :],
                                           ALU.mult, ALU.subtract).then_inc(bkd_ready, 1)
            nc.vector.scalar_tensor_tensor(bvd16[:, :, 1, :], bvd[:, :, :], W_SCALE / TOK_SCALE, bvd16[:, :, 0, :],
                                           ALU.mult, ALU.subtract).then_inc(bvd_ready, 1)
            layer_norm(0, lambda at: [weights_low(2 * W_Q[0] + i) for i in range(4) if at == 0])
            for l in range(2):
                for n in ("bq", "bv"):
                    v = pk[:, PACK[n, l]:PACK[n, l] + H]
                    ins = nc.vector.tensor_scalar(v, v, W_SCALE, None, ALU.mult)
            ins.then_inc(bq_scaled, 1)
            query_projection(0)
            attention(0)
            output_projection(0)
            add_output(0)
            layer_norm(1)
            query_projection(1)
            for k in range(PIECES):
                context_stats(0, k)
            attention(1)

            output_projection(1)
            add_output(1)
            for u in LN_UNITS[0]:
                unit_low(0, 0, u)

            def ln_units(at):
                for n, u in enumerate(LN_UNITS[at + 1]):
                    unit_low(0, 0, u)
                    if at == 2:
                        weights_low(2 * W_M + n)
            layer_norm(2, ln_units)
            weights_low(2 * W_M + 7)
            for c in range(DC):
                ins = nc.vector.tensor_scalar(xT[:, c, :], xT[:, c, :], col("b_fc2", c), None, ALU.add)
            ins.then_inc(x_biased, 1)
            for f in range(FC):
                dve.wait_ge(f1_act, f + 1)
                if f >= 4:
                    dve.wait_ge(f2_mm, f - 3)
                nc.vector.tensor_copy(hring[:, f % 4, 0, :], hid[:, f % 2, :]).then_inc(f1_hi, 1)
                dve.wait_ge(f1_hi, f + 1)
                nc.vector.tensor_tensor(hring[:, f % 4, 1, :], hid[:, f % 2, :], hring[:, f % 4, 0, :],
                                        ALU.subtract).then_inc(f1_lo, 1)
                if f > 0:
                    unit_low(1, 1, MLP_UNITS[f - 1])
                if f == 3:
                    mask_term_of(0)
                if f in (4, 5):
                    nc.vector.memset(qbd[:, :, :, f - 4, (AR, 0)[f - 4]:(APAD, APAD - AR)[f - 4]], 0.0)
            unit_low(1, 1, MLP_UNITS[FC - 1])
            dve.wait_ge(f2_mm, FC)
            dve.wait_ge(x_biased, 3)
            for c in range(DC):
                nc.vector.scalar_tensor_tensor(xT[:, c, :], PV[c][:, 0:NQ], 1.0 / W_SCALE, xT[:, c, :],
                                               ALU.mult, ALU.add).then_inc(x_ready, 1)
            for m in range(DC):
                dve.wait_ge(aq_hi, m + 1)
                nc.vector.scalar_tensor_tensor(qhl[:, m, 1, :], TB[m][:, 0:NQ], KA ** -0.5, qhl[:, m, 0, :],
                                               ALU.mult, ALU.subtract).then_inc(aq_lo, 1)
            for m in range(DC):
                dve.wait_ge(aq_lo, m + 1)
                for j in range(HA):
                    r0 = j * Q + m * (APAD - AR)
                    for i in range(2 if j >= HA_ACT else 1):
                        ins = nc.vector.tensor_scalar(qbd[:, :, 1 - i, m, r0:r0 + Q],
                                                      qhl[:, m, 1 - i, :].rearrange("p (b q) -> p b q", b=B),
                                                      hm[:, j:j + 1], None, ALU.mult)
                ins.then_inc(qbd_ready, 1)
            attention(2)
            add_output(2)


_L0 = "L0_xattn_"
_L1 = "L1_xattn_"


def kernel(**inputs):
    import numpy as np
    import concourse.bacc as bacc
    from concourse.bass_utils import run_bass_kernel_spmd

    a = {k: np.asarray(v) for k, v in inputs.items()}
    by_partition = lambda v: v.reshape(-1, P).T

    cols = []
    for l in ("1", "2"):
        cols += [by_partition(a[_L0 + n + l].reshape(-1)) for n in ("bq", "bk", "bv", "bias_k")]
    for n in ("ln1_scale", "ln1_offset", "ln2_scale", "ln2_offset", "ln_mlp_scale", "ln_mlp_offset", "bo1", "bo2",
              "b_fc2", "b_fc1"):
        cols.append(by_partition(a[_L0 + n]))

    def by_model_rows(w):
        return w.reshape(DC, P, WCH, -1).transpose(2, 1, 0, 3).reshape(WCH, P, -1)

    def by_head_rows(w):
        return w.reshape(WCH, HPC, -1, D).transpose(0, 2, 1, 3).reshape(WCH, w.shape[0] // H, -1)

    def audio(w):
        return w.T.reshape(DC, P, D).transpose(1, 0, 2).reshape(P, DC * D)

    ctx = a["ctx_2048"]
    arrays = {
        "x_t": a["x"].reshape(NQ, DC, P).transpose(2, 1, 0),
        "ctx_nat": ctx.reshape(B, TP, NT * D),
        "ctx_t": ctx.reshape(B, TP, NT, DC, P).transpose(0, 4, 3, 2, 1).reshape(B, P, DC * T),
        "mask": a["mask_BxS2_bf1"].reshape(B, TP, NT).transpose(0, 2, 1).reshape(B, T).view(np.uint8),
        "pack": np.concatenate(cols, axis=1),
        "vrows": np.stack([np.stack([a[_L0 + n + l].reshape(H, P) for n in ("bias_v", "bv")], axis=1)
                           for l in ("1", "2")], axis=1),
        "a_scale": a[_L1 + "ln_gamma"].reshape(1, D),
        "a_offset": a[_L1 + "ln_beta"].reshape(1, D),
        "gate": a[_L1 + "gate"].reshape(1, 1),
        "wq0": by_model_rows(a[_L0 + "wq1"]), "wq1": by_model_rows(a[_L0 + "wq2"]),
        "wq2": audio(a[_L1 + "Wq"]), "wk2": audio(a[_L1 + "Wk"]), "wv2": audio(a[_L1 + "Wv"]),
        "wo2": audio(a[_L1 + "Wo"]),
        "wk0": by_head_rows(a[_L0 + "wk1"].T), "wk1": by_head_rows(a[_L0 + "wk2"].T),
        "wv0": by_model_rows(a[_L0 + "wv1"]), "wv1": by_model_rows(a[_L0 + "wv2"]),
        "wo0": by_head_rows(a[_L0 + "wo1"]), "wo1": by_head_rows(a[_L0 + "wo2"]),
        "w1": a[_L0 + "w_fc1"].reshape(DC, P, 2, F // 2).transpose(2, 1, 0, 3).reshape(2, P, -1),
        "w2": a[_L0 + "w_fc2"].reshape(2, FC // 2, P, D).transpose(0, 2, 1, 3).reshape(2, P, -1),
    }
    nc = bacc.Bacc("TRN2", target_bir_lowering=False, num_devices=1)
    args, feed = {}, {}
    for name, v in arrays.items():
        v = np.ascontiguousarray(v)
        feed[f"in_{name}_dram"] = v
        args[name] = nc.dram_tensor(f"in_{name}_dram", v.shape, mybir.dt.from_np(v.dtype), kind="ExternalInput").ap()
    out = nc.dram_tensor("out_0_dram", (P, DC, NQ), F32, kind="ExternalOutput").ap()
    by_layer = {n: [args.pop(f"{n}{l}") for l in range(L)] for n in ("wq", "wk", "wv", "wo")}
    build(nc, **args, **by_layer, out=out)
    r = run_bass_kernel_spmd(nc, [feed], core_ids=[0])
    got = r.results[0]["out_0_dram"]
    return np.ascontiguousarray(got.transpose(2, 1, 0).reshape(B, Q, D))
```
